# Optimizing a Trainium2 kernel written in Bass

```python
import numpy as np
import jax
import jax.numpy as jnp

def _softmax(x, axis=-1):
    return jax.nn.softmax(x, axis=axis)

def _gelu(x):
    return jax.nn.gelu(x, approximate=True)

def _silu(x):
    return jax.nn.silu(x)

def _sigmoid(x):
    return jax.nn.sigmoid(x)

def _layernorm(x, axis=-1, eps=1e-05):
    m = jnp.mean(x, axis=axis, keepdims=True)
    v = jnp.var(x, axis=axis, keepdims=True)
    return (x - m) / jnp.sqrt(v + eps)

def _scatter_add(tgt, idx, src, axis=0):
    return tgt.at[idx].add(src)

def _segment_sum(src, seg, n):
    return jax.ops.segment_sum(src, seg, n)
kernel_name = 'mk_gnn_ffn_d2_gnn_r8_45d8c4'

def setup_inputs(seed: int=0):
    np.random.seed(seed)
    _w = jnp.asarray

    def _rec_inputs():
        import jax
        import jax.numpy as jnp
        _gk = jax.random.key(seed)
        x = -0.0001126 + 1 * jax.random.normal(jax.random.fold_in(_gk, 1), (6250, 256), jnp.float32)
        src = jax.random.randint(jax.random.fold_in(_gk, 2), (100000,), 0, 6250, jnp.int32)
        dst = jnp.minimum((6250 * jax.random.uniform(jax.random.fold_in(_gk, 3), (100000,)) ** 2.0).astype(jnp.int32), 49999)
        _o = jnp.argsort(dst, stable=True)
        src = src[_o]
        dst = dst[_o]
        edge_type_8 = jax.random.randint(jax.random.fold_in(_gk, 12), (100000,), 0, 8, jnp.int32)
        return (x, src, dst, edge_type_8)
    x, src, dst, edge_type_8 = _rec_inputs()

    def _L0_gnn_setup():
        import jax, jax.numpy as jnp
        import numpy as np
        N, E, R, H, D = (3750, 37500, 8, 8, 32)
        IN_F = 256
        NEG_SLOPE = 0.2
        key = jax.random.key(seed)
        k = jax.random.split(key, 6)
        x = jax.random.normal(k[0], (N, IN_F), dtype=jnp.float32)
        W = jax.random.normal(k[1], (R, H * D, IN_F), dtype=jnp.float32) * 0.05
        attn_src = jax.random.normal(k[2], (H, D), dtype=jnp.float32) * 0.1
        attn_dst = jax.random.normal(k[3], (H, D), dtype=jnp.float32) * 0.1
        edge_index = jax.random.randint(k[4], (2, E), 0, N, dtype=jnp.int64) if jax.config.read('jax_enable_x64') else jax.random.randint(k[4], (2, E), 0, N, dtype=jnp.int32)
        edge_type = jax.random.randint(k[5], (E,), 0, R, dtype=edge_index.dtype)
        return dict(x=x, W=W, attn_src=attn_src, attn_dst=attn_dst, edge_index=edge_index, edge_type=edge_type)
    _L0_gnn_all = _L0_gnn_setup()
    _L0_gnn_in = {k: v for k, v in _L0_gnn_all.items() if k in ('W', 'attn_src', 'attn_dst')}
    del _L0_gnn_all

    def _L0_ffn_setup():
        import jax, jax.numpy as jnp
        import numpy as np
        B, K, D = (512, 16, 256)
        E = 32
        H = int(D * 0.25)
        key = jax.random.key(seed)
        ks = jax.random.split(key, 7)
        d_rs = D ** (-0.5)
        h_rs = H ** (-0.5)
        x = jax.random.normal(ks[0], (B, K, D), dtype=jnp.float32)
        router_w = jax.random.uniform(ks[1], (E, D), jnp.float32, -d_rs, d_rs)
        router_b = jax.random.uniform(ks[2], (E,), jnp.float32, -d_rs, d_rs)
        W1 = jax.random.uniform(ks[3], (E, D, H), jnp.float32, -h_rs, h_rs)
        b1 = jax.random.uniform(ks[4], (E, H), jnp.float32, -h_rs, h_rs)
        W2 = jax.random.uniform(ks[5], (E, H, D), jnp.float32, -d_rs, d_rs)
        b2 = jax.random.uniform(ks[6], (E, D), jnp.float32, -d_rs, d_rs)
        return {'x': x, 'router_w': router_w, 'router_b': router_b, 'W1': W1, 'b1': b1, 'W2': W2, 'b2': b2}
    _L0_ffn_all = _L0_ffn_setup()
    _L0_ffn_in = {k: v for k, v in _L0_ffn_all.items() if k in ('router_w', 'router_b', 'W1', 'b1', 'W2', 'b2')}
    del _L0_ffn_all

    def _L1_gnn_setup():
        import jax, jax.numpy as jnp
        import numpy as np
        N, IN_CH, HEADS, OUT_CH, E = (6250, 256, 4, 64, 100000)
        key = jax.random.key(seed)
        k1, k2, k3, k4, k5 = jax.random.split(key, 5)
        x = jax.random.normal(k1, (N, IN_CH), dtype=jnp.float32)
        edge_index = jax.random.randint(k2, (2, E), 0, N, dtype=jnp.int64)
        bw = float(np.sqrt(6.0 / (IN_CH + HEADS * OUT_CH)))
        ba = float(np.sqrt(6.0 / (HEADS + OUT_CH)))
        weight = jax.random.uniform(k3, (IN_CH, HEADS * OUT_CH), jnp.float32, -bw, bw)
        attn_l = jax.random.uniform(k4, (HEADS, OUT_CH), jnp.float32, -ba, ba)
        attn_r = jax.random.uniform(k5, (HEADS, OUT_CH), jnp.float32, -ba, ba)
        return {'x': x, 'edge_index': edge_index, 'weight': weight, 'attn_l': attn_l, 'attn_r': attn_r}
    _L1_gnn_all = _L1_gnn_setup()
    _L1_gnn_in = {k: v for k, v in _L1_gnn_all.items() if k in ('weight', 'attn_l', 'attn_r')}
    del _L1_gnn_all

    def _L1_ffn_setup():
        import jax, jax.numpy as jnp
        import numpy as np
        TOP_K = 2
        LN_EPS = 1e-05
        key = jax.random.key(seed)
        ks = jax.random.split(key, 8)
        B, S, D, E, H = (16, 1024, 256, 8, 1024)
        x = jax.random.normal(ks[0], (B, S, D), dtype=jnp.float32)
        Wr = jax.random.normal(ks[1], (D, E), dtype=jnp.float32) * 0.1
        br = jnp.zeros((E,), dtype=jnp.float32)
        ln_g = jnp.ones((E, D), dtype=jnp.float32)
        ln_b = jnp.zeros((E, D), dtype=jnp.float32)
        W1 = jax.random.normal(ks[2], (E, D, H), dtype=jnp.float32) * (1.0 / np.sqrt(D))
        b1 = jnp.zeros((E, H), dtype=jnp.float32)
        W2 = jax.random.normal(ks[3], (E, H, D), dtype=jnp.float32) * (1.0 / np.sqrt(H))
        b2 = jnp.zeros((E, D), dtype=jnp.float32)
        return {'x': x, 'Wr': Wr, 'br': br, 'ln_g': ln_g, 'ln_b': ln_b, 'W1': W1, 'b1': b1, 'W2': W2, 'b2': b2}
    _L1_ffn_all = _L1_ffn_setup()
    _L1_ffn_in = {k: v for k, v in _L1_ffn_all.items() if k in ('Wr', 'br', 'ln_g', 'ln_b', 'W1', 'b1', 'W2', 'b2')}
    del _L1_ffn_all
    return {'x': x, 'src': src, 'dst': dst, 'edge_type_8': edge_type_8, 'L0_gnn_W': _L0_gnn_in['W'], 'L0_gnn_attn_src': _L0_gnn_in['attn_src'], 'L0_gnn_attn_dst': _L0_gnn_in['attn_dst'], 'L0_ffn_router_w': _L0_ffn_in['router_w'], 'L0_ffn_router_b': _L0_ffn_in['router_b'], 'L0_ffn_W1': _L0_ffn_in['W1'], 'L0_ffn_b1': _L0_ffn_in['b1'], 'L0_ffn_W2': _L0_ffn_in['W2'], 'L0_ffn_b2': _L0_ffn_in['b2'], 'L1_gnn_weight': _L1_gnn_in['weight'], 'L1_gnn_attn_l': _L1_gnn_in['attn_l'], 'L1_gnn_attn_r': _L1_gnn_in['attn_r'], 'L1_ffn_Wr': _L1_ffn_in['Wr'], 'L1_ffn_br': _L1_ffn_in['br'], 'L1_ffn_ln_g': _L1_ffn_in['ln_g'], 'L1_ffn_ln_b': _L1_ffn_in['ln_b'], 'L1_ffn_W1': _L1_ffn_in['W1'], 'L1_ffn_b1': _L1_ffn_in['b1'], 'L1_ffn_W2': _L1_ffn_in['W2'], 'L1_ffn_b2': _L1_ffn_in['b2']}

def reference(x, src, dst, edge_type_8, L0_gnn_W, L0_gnn_attn_src, L0_gnn_attn_dst, L0_ffn_router_w, L0_ffn_router_b, L0_ffn_W1, L0_ffn_b1, L0_ffn_W2, L0_ffn_b2, L1_gnn_weight, L1_gnn_attn_l, L1_gnn_attn_r, L1_ffn_Wr, L1_ffn_br, L1_ffn_ln_g, L1_ffn_ln_b, L1_ffn_W1, L1_ffn_b1, L1_ffn_W2, L1_ffn_b2):
    import jax
    import jax.numpy as jnp

    def _L0_gnn_ref(x, W, attn_src, attn_dst, edge_index, edge_type):
        import jax, jax.numpy as jnp
        import numpy as np
        N, E, R, H, D = (3750, 37500, 8, 8, 32)
        IN_F = 256
        NEG_SLOPE = 0.2
        n = x.shape[0]
        r = W.shape[0]
        h, d = attn_src.shape
        h_all = jnp.einsum('nf,rof->rno', x, W).reshape(r, n, h, d)
        src, dst = (edge_index[0], edge_index[1])
        h_src = h_all[edge_type, src]
        h_dst = h_all[edge_type, dst]
        scores = jnp.einsum('ehd,hd->eh', h_src, attn_src) + jnp.einsum('ehd,hd->eh', h_dst, attn_dst)
        scores = jnp.where(scores > 0, scores, NEG_SLOPE * scores)
        amax = jnp.maximum(jax.ops.segment_max(scores, dst, num_segments=n), 0.0)
        w = jnp.exp(scores - amax[dst])
        denom = jax.ops.segment_sum(w, dst, num_segments=n) + 1e-12
        w = w / denom[dst]
        msg = h_src * w[..., None]
        out = jax.ops.segment_sum(msg, dst, num_segments=n)
        return out.reshape(n, h * d)

    def _L0_ffn_ref(x, router_w, router_b, W1, b1, W2, b2):
        import jax, jax.numpy as jnp
        import numpy as np
        B, K, D = (512, 16, 256)
        E = 32
        H = int(D * 0.25)
        xf = x.reshape(-1, D)
        logits = xf @ router_w.T + router_b
        idx = jnp.argmax(logits, axis=-1)
        w1t = jnp.take(W1, idx, axis=0)
        h = jnp.einsum('nd,ndh->nh', xf, w1t) + jnp.take(b1, idx, axis=0)
        h = jax.nn.relu(h)
        w2t = jnp.take(W2, idx, axis=0)
        out = jnp.einsum('nh,nhd->nd', h, w2t) + jnp.take(b2, idx, axis=0)
        out = jax.nn.relu(out)
        return out.reshape(x.shape)

    def _L1_gnn_ref(x, edge_index, weight, attn_l, attn_r):
        import jax, jax.numpy as jnp
        import numpy as np
        N, IN_CH, HEADS, OUT_CH, E = (6250, 256, 4, 64, 100000)
        heads, out_ch = attn_l.shape
        n = x.shape[0]
        xt = jnp.matmul(x, weight).reshape(-1, heads, out_ch)
        row, col = (edge_index[0], edge_index[1])
        alpha_l = jnp.einsum('ehd,hd->eh', xt[row], attn_l)
        alpha_r = jnp.einsum('ehd,hd->eh', xt[col], attn_r)
        alpha = jax.nn.softmax(jax.nn.leaky_relu(alpha_l + alpha_r, 0.01), axis=1)
        tmp = jnp.einsum('nh,nhd->nd', alpha[:n], xt[col[:n]])
        out = jnp.broadcast_to(tmp[:, None, :], (n, heads, out_ch))
        return out.reshape(n, heads * out_ch)

    def _L1_ffn_ref(x, Wr, br, ln_g, ln_b, W1, b1, W2, b2):
        import jax, jax.numpy as jnp
        import numpy as np
        TOP_K = 2
        LN_EPS = 1e-05
        B, S, D = x.shape
        N = B * S
        xt = x.reshape(N, D)
        logits = xt @ Wr + br
        probs = jax.nn.softmax(logits, axis=-1)
        top_p, top_idx = jax.lax.top_k(probs, TOP_K)
        weights = top_p / top_p.sum(axis=-1, keepdims=True)
        mu = xt.mean(axis=-1, keepdims=True)
        var = ((xt - mu) ** 2).mean(axis=-1, keepdims=True)
        xn = (xt - mu) * jax.lax.rsqrt(var + LN_EPS)
        xe = xn[None, :, :] * ln_g[:, None, :] + ln_b[:, None, :]
        h = jax.nn.gelu(jnp.einsum('end,edh->enh', xe, W1) + b1[:, None, :], approximate=False)
        y = jnp.einsum('enh,ehd->end', h, W2) + b2[:, None, :]
        y_tok = jnp.transpose(y, (1, 0, 2))
        sel = jnp.take_along_axis(y_tok, top_idx[:, :, None], axis=1)
        out = (weights[:, :, None] * sel).sum(axis=1)
        return out.reshape(B, S, D)
    edge_index = jnp.stack([src, dst])
    x = x + _L0_gnn_ref(_layernorm(x, axis=-1), L0_gnn_W, L0_gnn_attn_src, L0_gnn_attn_dst, edge_index, edge_type_8)
    x = x + _L0_ffn_ref(_layernorm(x, axis=-1)[None], L0_ffn_router_w, L0_ffn_router_b, L0_ffn_W1, L0_ffn_b1, L0_ffn_W2, L0_ffn_b2)[0]
    x = x + _L1_gnn_ref(_layernorm(x, axis=-1), edge_index, L1_gnn_weight, L1_gnn_attn_l, L1_gnn_attn_r)
    x = x + _L1_ffn_ref(_layernorm(x, axis=-1)[None], L1_ffn_Wr, L1_ffn_br, L1_ffn_ln_g, L1_ffn_ln_b, L1_ffn_W1, L1_ffn_b1, L1_ffn_W2, L1_ffn_b2)[0]
    return x

_drawn_inputs = setup_inputs


def setup_inputs(seed=0):
    import zlib

    import numpy as np

    out = dict(_drawn_inputs(seed))
    spreads = {'L1_ffn_br': (0.0, 0.1),
     'L1_ffn_ln_g': (1.0, 0.2),
     'L1_ffn_ln_b': (0.0, 0.1),
     'L1_ffn_b1': (0.0, 0.1),
     'L1_ffn_b2': (0.0, 0.1)}
    factors = {}
    for name, (base, spread) in spreads.items():
        noise = np.random.default_rng([zlib.crc32(name.encode()), seed]).standard_normal(out[name].shape)
        drawn = base * np.exp(spread * noise) if base else spread * noise
        out[name] = jnp.asarray(drawn.astype(out[name].dtype))
    for name, factor in factors.items():
        out[name] = (out[name] * factor).astype(out[name].dtype)
    return out
```

```python
import concourse.bass as bass
from concourse import mybir
from contextlib import ExitStack

F32 = mybir.dt.float32
I32 = mybir.dt.int32
F16 = mybir.dt.float16
ALU = mybir.AluOpType
ACT = mybir.ActivationFunctionType
AX = mybir.AxisListType

P = 128
N = 6250
D = 256
DC = D // P
NT = -(-N // P)
TAIL = N - (NT - 1) * P
NPAD = NT * P
E = 100000
C = 16
CE = E // C
R, H0, HD0 = 8, 8, 32
H1, HD1 = 4, 64
E0, F0 = 32, 64
E1, F1 = 8, 1024
EPS = 1e-5
ITEMS = 832
U = 8
assert CE == N and ITEMS >= C * NT + NT - 1 and ITEMS % U == 0


class Chain:

    def __init__(self, eng, sem):
        self.eng, self.sem, self.n = eng, sem, 0

    def link(self, ins):
        ins.then_inc(self.sem, 1)
        self.n = self.n + 1
        self.eng.wait_ge(self.sem, self.n)


class Count:

    def __init__(self, stage, name, ahead):
        self.sem, self.ahead = stage.sem(name), ahead

    def start(self, eng):
        eng.sem_inc(self.sem, self.ahead)

    def done(self, eng, t):
        eng.wait_ge(self.sem, t + 1 + self.ahead)

    def slot(self, eng, t):
        eng.wait_ge(self.sem, t + 1)


class Stage:

    def __init__(self, nc, name):
        self.nc, self.name, self.ctx, self.sems = nc, name, ExitStack(), []

    def __enter__(self):
        return self

    def __exit__(self, *a):
        self.ctx.close()
        if self.sems:
            self.nc.clear_and_free_semaphores(self.sems)
            self.nc.all_engine_barrier()

    def sb(self, name, shape, dt=F32):
        return self.ctx.enter_context(self.nc.sbuf_tensor(f"{self.name}_{name}", shape, dt))

    def banks(self, n=8):
        return [self.ctx.enter_context(self.nc.psum_tensor(f"{self.name}_bank{i}", [P, 512], F32)) for i in range(n)]

    def sem(self, name):
        self.sems.append(self.nc.alloc_semaphore(f"{self.name}_{name}"))
        return self.sems[-1]

    def block(self):
        return self.ctx.enter_context(self.nc.Block())


def col(ap, start, size=1):
    out = ap[:, start:start + size] if isinstance(start, int) else ap[:, bass.ds(start, size)]
    if size == 1 and len(ap.shape) > 2:
        names = " ".join("abcd"[: len(ap.shape) - 2])
        out = out.rearrange(f"p o {names} -> p (o {names})")
    return out


def flat(ap):
    names = " ".join("abcd"[: len(ap.shape) - 1])
    return ap.rearrange(f"p {names} -> p ({names})")


def rows(ap, start, size):
    return ap[start:start + size, :] if isinstance(start, int) else ap[bass.ds(start, size), :]


def tiles(eng, n, unroll, body, base=0):
    with eng.Fori(0, n // unroll) as i:
        for u in range(unroll):
            body(i * unroll + u, u)
    for t in range(n - n % unroll, n):
        body(t, t % unroll)


def rounds(eng, n, unroll, body):
    for u in range(unroll):
        body(0, u)
    with eng.Fori(1, n // unroll) as i:
        for u in range(unroll):
            body(i, u)
    for u in range(n % unroll):
        body(n // unroll, u)


class Norm:

    def __init__(self, nc, s, k, banks):
        self.nc, self.k, self.banks = nc, k, banks
        self.st6 = s.sb("stats", [P, NT, 6])
        self.mean, self.rstd = s.sb("mean", [P, NT]), s.sb("rstd", [P, NT])
        self.tmp, self.var, self.sd = (s.sb(n, [P, NT]) for n in ("tmp", "var", "sd"))
        self.xn = s.sb("xn", [P, 2, D])
        self.xT = s.sb("xnT", [P, 2, D])
        self.dve = s.sem("dve")
        self.var_ok, self.sd_ok = s.sem("var_ready"), s.sem("sd_ready")
        self.xn_ok = Count(s, "xn_ready", 2)
        self.t_ps = Count(s, "xnT_in_psum", 2)
        self.t_ok = Count(s, "xnT_ready", 2)

    def statistics(self, v, ch):
        nc, c0 = self.nc, ch.n

        def one(t, u):
            nc.vector.bn_stats(col(self.st6, t), col(self.k.x, t)).then_inc(self.dve, 1)
        tiles(v, NT, 7, one)
        ch.n = c0 + NT
        v.wait_ge(self.dve, ch.n)
        me, ve, mo, vo = (self.st6[:, :, i] for i in (1, 2, 4, 5))
        tmp, var, mean = self.tmp[:, :], self.var[:, :], self.mean[:, :]
        moments(nc, ch, me, ve, mo, vo, mean, var, tmp)
        v.sem_inc(self.var_ok, 1)
        v.wait_ge(self.sd_ok, 1)
        rsqrt_newton(nc, ch, self.rstd[:, :], tmp, var, self.sd[:, :])
        self.xn_ok.start(v)

    def root(self, act):
        act.wait_ge(self.var_ok, 1)
        self.nc.scalar.activation(self.sd[:, :], self.var[:, :], ACT.Sqrt).then_inc(self.sd_ok, 1)
        self.t_ok.start(act)

    def normalise(self, v, t, u):
        self.t_ps.slot(v, t)
        self.nc.vector.tensor_scalar(self.xn[:, u, :], col(self.k.x, t), col(self.mean, t), col(self.rstd, t),
                                     ALU.subtract, ALU.mult).then_inc(self.xn_ok.sem, 1)

    def transpose(self, pe, t, u):
        self.xn_ok.done(pe, t)
        self.t_ok.slot(pe, t)
        for c in range(DC):
            last = self.nc.tensor.transpose(self.banks[u][:, c * P:(c + 1) * P], self.xn[:, u, c * P:(c + 1) * P], self.k.ident[:, :])
        last.then_inc(self.t_ps.sem, 1)

    def keep(self, act, t, u, used):
        self.t_ps.done(act, t)
        used.slot(act, t)
        self.nc.scalar.activation(self.xT[:, u, :], self.banks[u][:, 0:D], ACT.Copy).then_inc(self.t_ok.sem, 1)


def moments(nc, ch, me, ve, mo, vo, mean, var, tmp):
    ch.link(nc.vector.tensor_tensor(tmp, me, mo, ALU.add))
    ch.link(nc.vector.tensor_scalar(mean, tmp, 0.5, None, ALU.mult))
    ch.link(nc.vector.tensor_tensor(tmp, me, mo, ALU.subtract))
    ch.link(nc.vector.tensor_tensor(tmp, tmp, tmp, ALU.mult))
    ch.link(nc.vector.tensor_scalar(tmp, tmp, 0.25, EPS, ALU.mult, ALU.add))
    ch.link(nc.vector.tensor_tensor(var, ve, vo, ALU.add))
    ch.link(nc.vector.scalar_tensor_tensor(var, var, 1.0 / D, tmp, ALU.mult, ALU.add))


def rsqrt_newton(nc, ch, out, tmp, var, sd):
    ch.link(nc.vector.reciprocal(out, sd))
    ch.link(nc.vector.tensor_tensor(tmp, out, out, ALU.mult))
    ch.link(nc.vector.tensor_tensor(tmp, tmp, var, ALU.mult))
    ch.link(nc.vector.tensor_scalar(tmp, tmp, -0.5, 1.5, ALU.mult, ALU.add))
    ch.link(nc.vector.tensor_tensor(out, out, tmp, ALU.mult))


def prepare(nc, a, k):
    with Stage(nc, "prep") as s:
        names = ("src", "dst", "edge_type_8")
        ints = [s.sb(f"{n}_i", [NT, C, P], I32) for n in names]
        floats = [k.score[0:NT, j * C * P:(j + 1) * C * P].rearrange("g (c p) -> g c p", c=C) for j in range(3)]
        idx = k.w[:, 0:3 * NT * C].rearrange("p (j q) -> p j q", j=3)
        iota_i, col_i = s.sb("iota_i", [P, P], I32), s.sb("col_i", [P, 1], I32)
        wn = s.sb("w_natural", [P, R, DC, D])
        ablk = s.sb("attn_blocks", [P, DC, 2 * H0])
        vst = s.sb("score_weights", [P, DC, 2 * R * H0])
        scores = s.sb("scores", [P, 2, 2 * R * H0])
        first = s.sb("first_last", [NT, 2, C])
        first_i = s.sb("first_last_i", [NT, 2, C], I32)
        bank = s.banks()
        norm = Norm(nc, s, k, bank[0:2])
        cleared, loaded, edges, weights = (s.sem(n) for n in ("cleared", "x_loaded", "edges_loaded", "weights_loaded"))
        iotas, consts, edges_f = s.sem("iotas"), s.sem("consts"), s.sem("edges_as_floats")
        wt_ps, wt_free, v_ps, v_ok = (s.sem(n) for n in ("wT_in_psum", "wT_bank_free", "v_in_psum", "v_ready"))
        e_ps, e_free = s.sem("edges_in_psum"), s.sem("edges_bank_free")
        sc_ps, sc_ok, stored = Count(s, "scores_in_psum", 2), Count(s, "scores_ready", 2), Count(s, "scores_stored", 2)
        st_dma, spans, spans_st = s.sem("scores_written"), s.sem("spans_ready"), s.sem("spans_written")
        block = s.block()

        @block.gpsimd
        def _(pool):
            nc.gpsimd.memset(k.x[:, NT - 1, :], 0.0).then_inc(cleared, 1)
            nc.gpsimd.memset(ablk[:, :, :], 0.0).then_inc(cleared, 1)
            for t in ints:
                nc.gpsimd.memset(t[:, :, :], 0).then_inc(cleared, 1)
            nc.gpsimd.iota(iota_i[:, :], [[1, P]], base=0, channel_multiplier=0).then_inc(iotas, 1)
            nc.gpsimd.iota(col_i[:, :], [[0, 1]], base=0, channel_multiplier=1).then_inc(iotas, 1)

        @block.sync
        def _(sp):
            sp.wait_ge(cleared, 5)
            for t, name in zip(ints, names):
                e = a[name].rearrange("(c e) -> c e", c=C)
                sp.dma_start(t[0:NT - 1, :, :], e[:, 0:(NT - 1) * P].rearrange("c (g p) -> g c p", p=P)).then_inc(edges, 16)
                sp.dma_start(t[NT - 1:NT, :, 0:TAIL], e[:, (NT - 1) * P:].rearrange("c (o p) -> o c p", o=1)).then_inc(edges, 16)
            sp.dma_start(wn[:, :, :, :], a["L0_gnn_W"].rearrange("r (c p) f -> p r c f", p=P)).then_inc(weights, 16)
            with nc.allow_non_contiguous_dma(reason="short vectors onto partitions"):
                for j, name in enumerate(("L0_gnn_attn_src", "L0_gnn_attn_dst")):
                    for h in range(H0):
                        p0 = h * HD0 % P
                        sp.dma_start(ablk[p0:p0 + HD0, h * HD0 // P, j * H0 + h:j * H0 + h + 1],
                                     a[name][h:h + 1, :].rearrange("a b -> b a")).then_inc(weights, 16)
                sp.wait_ge(spans, 1)
                for j in range(2):
                    sp.dma_start(k.span_tab[j:j + 1, :].rearrange("o (c g) -> (o g) c", c=C), first[:, j, :]).then_inc(spans_st, 16)
            stored.start(sp)

            def store(t, u):
                sc_ok.done(sp, t)
                for j, tab in enumerate((k.src_tab, k.dst_tab)):
                    sp.dma_start(rows(tab.rearrange("(n r) h -> n (r h)", r=R), t * P, P),
                                 scores[:, u, j * R * H0:(j + 1) * R * H0]).then_inc(st_dma, 16)
                sp.wait_ge(st_dma, (t + 1) * 32)
                sp.sem_inc(stored.sem, 1)
            tiles(sp, NT, 2, store)
            sp.wait_ge(spans_st, 32)

        @block.scalar
        def _(act):
            act.wait_ge(cleared, 1)
            act.dma_start(k.x[:, 0:NT - 1, :], a["x"][0:(NT - 1) * P, :].rearrange("(t p) f -> p t f", p=P)).then_inc(loaded, 16)
            act.dma_start(k.x[0:TAIL, NT - 1, :], a["x"][(NT - 1) * P:N, :]).then_inc(loaded, 16)
            norm.root(act)
            tiles(act, NT, 2, lambda t, u: norm.keep(act, t, u, sc_ps))

        @block.vector
        def _(v):
            ch = Chain(v, norm.dve)
            v.wait_ge(iotas, 2)
            ch.link(nc.vector.tensor_copy(k.iota[:, :], iota_i[:, :]))
            ch.link(nc.vector.tensor_copy(k.col[:, :], col_i[:, :]))
            ch.link(nc.vector.memset(k.ones[:, :], 1.0))
            ch.link(nc.vector.tensor_scalar(k.ident[:, :], k.iota[:, :], k.col[:, 0:1], None, ALU.is_equal))
            ch.link(nc.vector.tensor_scalar(k.before[:, :], k.iota[:, :], k.col[:, 0:1], None, ALU.is_gt))
            v.sem_inc(consts, 1)
            v.wait_ge(edges, 96)
            for t, f in zip(ints, floats):
                ch.link(nc.vector.tensor_copy(f[:, :, :], t[:, :, :]))
            v.sem_inc(edges_f, 1)
            ch.link(nc.vector.tensor_copy(first[:, 0, :], floats[1][:, :, 0]))
            ch.link(nc.vector.reduce_max(first[:, 1, :], floats[1][:, :, :], AX.X))
            ch.link(nc.vector.tensor_copy(first_i[:, :, :], first[:, :, :]))
            ch.link(nc.vector.tensor_scalar(first_i[:, :, :], first_i[:, :, :], 7, None, ALU.arith_shift_right))
            nc.vector.tensor_copy(first[:, :, :], first_i[:, :, :]).then_inc(spans, 1)
            for n in range(6):
                j, half = divmod(n, 2)
                v.wait_ge(e_ps, n + 1)
                nc.vector.tensor_copy(idx[:, j, :].rearrange("p (g c) -> p g c", c=C)[:, :, half * 8:half * 8 + 8],
                                      bank[n % 4][:, 0:8 * NT].rearrange("p (c g) -> p g c", c=8)).then_inc(e_free, 1)
            v.wait_ge(e_free, 6)
            nc.vector.scalar_tensor_tensor(k.edge_row[:, :], idx[:, 0, :], float(R), idx[:, 2, :], ALU.mult, ALU.add)
            nc.vector.scalar_tensor_tensor(k.dst_row[:, :], idx[:, 1, :], float(R), idx[:, 2, :], ALU.mult, ALU.add)
            nc.vector.tensor_copy(k.dst_f[:, :], idx[:, 1, :])
            nc.vector.tensor_copy(k.dst_i[:, :], idx[:, 1, :].rearrange("p (g c) -> p g c", c=C)[:, :, 0])
            nc.vector.tensor_copy(k.src_i[:, :], idx[:, 0, :].rearrange("p (g c) -> p g c", c=C)[:, :, 0])
            for r in range(R):
                v.wait_ge(wt_ps, r + 1)
                nc.vector.tensor_copy(k.wT[:, :, r * D:(r + 1) * D], bank[r % 4][:, :].rearrange("p (c o) -> p c o", c=DC)).then_inc(wt_free, 1)
            v.wait_ge(v_ps, 1)
            got = bank[4][:, 0:DC * R * 2 * H0].rearrange("p (c r j h) -> p c r j h", c=DC, r=R, j=2)
            for c in range(DC):
                for j in range(2):
                    nc.vector.tensor_copy(vst[:, c, j * R * H0:(j + 1) * R * H0].rearrange("p (r h) -> p r h", r=R), got[:, c, :, j, :]).then_inc(v_ok, 1)
            v.wait_ge(loaded, 32)
            norm.statistics(v, ch)
            sc_ok.start(v)

            def evacuate(t, u):
                sc_ps.done(v, t)
                stored.slot(v, t)
                nc.vector.tensor_copy(scores[:, u, :], bank[2 + u][:, 0:P]).then_inc(sc_ok.sem, 1)

            norm.normalise(v, 0, 0)
            with v.Fori(0, (NT - 1) // 2) as i:
                for u in range(2):
                    norm.normalise(v, i * 2 + u + 1, 1 - u)
                    evacuate(i * 2 + u, u)
            evacuate(NT - 1, 0)

        @block.tensor
        def _(pe):
            pe.wait_ge(consts, 1)
            pe.wait_ge(edges_f, 1)
            for n in range(6):
                j, half = divmod(n, 2)
                if n >= 4:
                    pe.wait_ge(e_free, n - 3)
                for c in range(8):
                    last = nc.tensor.transpose(bank[n % 4][:, c * NT:(c + 1) * NT], floats[j][:, half * 8 + c, :], k.ident[0:NT, 0:NT])
                last.then_inc(e_ps, 1)
            pe.wait_ge(weights, 16 * 17)
            pe.wait_ge(e_free, 6)
            for r in range(R):
                if r >= 4:
                    pe.wait_ge(wt_free, r - 3)
                for fc in range(DC):
                    for oc in range(DC):
                        last = nc.tensor.transpose(bank[r % 4][:, fc * D + oc * P:fc * D + (oc + 1) * P],
                                                   wn[:, r, oc, fc * P:(fc + 1) * P], k.ident[:, :])
                last.then_inc(wt_ps, 1)
            for fc in range(DC):
                for r in range(R):
                    o = (fc * R + r) * 2 * H0
                    for oc in range(DC):
                        last = nc.tensor.matmul(bank[4][:, o:o + 2 * H0], wn[:, r, oc, fc * P:(fc + 1) * P], ablk[:, oc, :],
                                                start=(oc == 0), stop=(oc == DC - 1))
            last.then_inc(v_ps, 1)
            pe.wait_ge(v_ok, 4)
            pe.wait_ge(wt_free, R)
            norm.t_ps.start(pe)
            sc_ps.start(pe)

            def body(t, u):
                norm.transpose(pe, t, u)
                norm.t_ok.done(pe, t)
                sc_ok.slot(pe, t)
                for c in range(DC):
                    last = nc.tensor.matmul(bank[2 + u][:, 0:P], norm.xT[:, u, c * P:(c + 1) * P], vst[:, c, :],
                                            start=(c == 0), stop=(c == DC - 1))
                last.then_inc(sc_ps.sem, 1)
            tiles(pe, NT, 2, body)
        k.norm0 = None


def edge_scores(nc, a, k):
    with Stage(nc, "score") as s:
        bank = s.banks()
        norm = Norm(nc, s, k, bank[0:2])
        hb = s.sb("h_rows", [P, 2, R * D])
        ids = s.sb("rows", [P, 2, 2, C], I32)
        half = s.sb("halves", [P, 2, 2, C * H0])
        both = s.sb("sum", [P, 2, C * H0])
        leaky = s.sb("leaky", [P, 2, C * H0])
        products = Count(s, "h_tile_in_psum", 2)
        h_ps, h_ok, stored = s.sem("h_bank_full"), s.sem("h_bank_empty"), Count(s, "h_rows_stored", 2)
        st_dma = s.sem("h_rows_written")
        ids_ok, begun = s.sem("rows_ready"), s.sem("gathers_begun")
        gathered = [s.sem(f"halves_gathered{u}") for u in range(2)]
        sum_ok, leaky_ok = Count(s, "sum_ready", 2), Count(s, "leaky_ready", 2)
        turned, kept = Count(s, "scores_turned", 2), Count(s, "scores_kept", 2)
        block = s.block()

        @block.gpsimd
        def _(pool):
            def body(t, u):
                sum_ok.slot(pool, t)
                nc.gpsimd.tensor_copy(ids[:, u, 0, :], col(k.edge_row, t * C, C)).then_inc(ids_ok, 1)
                nc.gpsimd.tensor_copy(ids[:, u, 1, :], col(k.dst_row, t * C, C)).then_inc(ids_ok, 1)
                pool.wait_ge(ids_ok, 2 * t + 2)
                pool.sem_inc(begun, 1)
                for j, tab in enumerate((k.src_tab, k.dst_tab)):
                    for c in range(C):
                        nc.gpsimd.indirect_dma_start(half[:, u, j, c * H0:(c + 1) * H0], None, tab,
                                                     bass.IndirectOffsetOnAxis(ids[:, u, j, c:c + 1], 0)).then_inc(gathered[u], 16)
            tiles(pool, NT, 2, body)

        @block.vector
        def _(v):
            ch = Chain(v, norm.dve)
            sum_ok.start(v)
            leaky_ok.start(v)
            norm.statistics(v, ch)

            def scores(i, u):
                t = i * 2 + u
                v.wait_ge(gathered[u], (i + 1) * 2 * C * 16)
                nc.vector.tensor_tensor(both[:, u, :], half[:, u, 0, :], half[:, u, 1, :], ALU.add).then_inc(sum_ok.sem, 1)
                sum_ok.done(v, t)
                turned.slot(v, t)
                nc.vector.scalar_tensor_tensor(leaky[:, u, :], both[:, u, :], 0.2, both[:, u, :], ALU.mult, ALU.max).then_inc(leaky_ok.sem, 1)
            norm.normalise(v, 0, 0)
            with v.Fori(0, (NT - 1) // 2) as i:
                for u in range(2):
                    norm.normalise(v, i * 2 + u + 1, 1 - u)
                    scores(i, u)
            scores((NT - 1) // 2, 0)

        @block.tensor
        def _(pe):
            for n in (norm.t_ps, products, turned):
                n.start(pe)
            pe.sem_inc(h_ps, 4)

            def body(t, u):
                norm.transpose(pe, t, u)
                norm.t_ok.done(pe, t)
                for j in range(4):
                    pe.wait_ge(h_ok, 4 * t + j + 1)
                    for c in range(DC):
                        last = nc.tensor.matmul(bank[2 + j][:, :], norm.xT[:, u, c * P:(c + 1) * P], k.wT[:, c, j * 512:(j + 1) * 512],
                                                start=(c == 0), stop=(c == DC - 1))
                    last.then_inc(h_ps, 1)
                pe.sem_inc(products.sem, 1)
                leaky_ok.done(pe, t)
                kept.slot(pe, t)
                nc.tensor.transpose(bank[6 + u][:, 0:P], leaky[:, u, :], k.ident[:, :]).then_inc(turned.sem, 1)
            tiles(pe, NT, 2, body)

        @block.scalar
        def _(act):
            norm.root(act)
            act.sem_inc(h_ok, 4)
            kept.start(act)

            def body(t, u):
                norm.keep(act, t, u, products)
                stored.slot(act, t)
                for j in range(4):
                    act.wait_ge(h_ps, 4 + 4 * t + j + 1)
                    nc.scalar.activation(hb[:, u, j * 512:(j + 1) * 512], bank[2 + j][:, :], ACT.Copy).then_inc(h_ok, 1)
                turned.done(act, t)
                nc.scalar.activation(col(k.score, t * P, P), bank[6 + u][:, 0:P], ACT.Copy).then_inc(kept.sem, 1)
            tiles(act, NT, 2, body)

        @block.sync
        def _(sp):
            stored.start(sp)

            def body(t, u):
                sp.wait_ge(h_ok, 4 + 4 * t + 4)
                sp.dma_start(rows(k.h_tab.rearrange("(n r) o -> n (r o)", r=R), t * P, P), hb[:, u, :]).then_inc(st_dma, 16)
                sp.wait_ge(st_dma, (t + 1) * 16)
                sp.sem_inc(stored.sem, 1)
            tiles(sp, NT, 2, body)


def edge_weights(nc, a, k):
    with Stage(nc, "weight") as s:
        bank = s.banks()
        d = s.sb("dst", [P, CE], I32)
        same = s.sb("same", [P, CE + 1])
        seg = s.sb("segment_max", [P, CE])
        ends = s.sb("ends", [P, 4])
        row = s.sb("rows", [1, 4, H0 * C])
        link, one, nxt, g, fc, bc = (s.sb(n, [1, H0, C]) for n in ("link", "one", "next", "gate", "forward", "backward"))
        carry = s.sb("carry", [1, 2, C * H0])
        carry_c = s.sb("carry_col", [P, 2])
        loaded, dve, ends_ps, ends_ok, carry_ok, carry_ps = (s.sem(n) for n in ("dst_loaded", "dve", "ends_in_psum", "ends_ready", "carry_ready", "carry_in_psum"))
        diff_ok, exp_ok, w_ps, w_ok, cleared = (s.sem(n) for n in ("diff_ready", "exp_ready", "w_in_psum", "w_ready", "cleared"))
        block = s.block()

        @block.sync
        def _(sp):
            for c in range(C):
                sp.dma_start(d[c * H0:(c + 1) * H0, :], a["dst"][c * CE:(c + 1) * CE].rearrange("(o e) -> o e", o=1).broadcast_to([H0, CE])).then_inc(loaded, 16)

        @block.gpsimd
        def _(pool):
            nc.gpsimd.memset(k.w[:, (NT - 1) * P:], 0.0).then_inc(cleared, 1)
            nc.gpsimd.memset(same[:, 0:1], 0.0).then_inc(cleared, 1)
            nc.gpsimd.memset(same[:, CE:CE + 1], 0.0).then_inc(cleared, 1)
            for t in (link, nxt, carry):
                nc.gpsimd.memset(t[:, :, :], 0.0).then_inc(cleared, 1)

        @block.vector
        def _(v):
            ch = Chain(v, dve)
            v.wait_ge(loaded, 16 * C)
            v.wait_ge(cleared, 6)
            ch.link(nc.vector.tensor_tensor(same[:, 1:CE], d[:, 1:CE], d[:, 0:CE - 1], ALU.is_equal))
            ch.link(nc.vector.tensor_tensor_scan(seg[:, :], same[:, 0:CE], k.score[:, 0:CE], 0.0, ALU.mult, ALU.max))
            ch.link(nc.vector.tensor_tensor_scan(seg[:, ::-1], same[:, CE:0:-1], seg[:, ::-1], 0.0, ALU.mult, ALU.max))
            ch.link(nc.vector.tensor_copy(ends[:, 0:1], seg[:, 0:1]))
            ch.link(nc.vector.tensor_copy(ends[:, 1:2], seg[:, CE - 1:CE]))
            ch.link(nc.vector.tensor_copy(ends[:, 2:3], d[:, 0:1]))
            ch.link(nc.vector.tensor_copy(ends[:, 3:4], d[:, CE - 1:CE]))
            v.sem_inc(ends_ok, 1)
            v.wait_ge(ends_ps, 1)
            ch.link(nc.vector.tensor_copy(row[:, :, :].rearrange("o j (h c) -> o j h c", c=C), bank[0][0:1, :].rearrange("o (j c h) -> o j h c", j=4, h=H0)))
            r4 = row[:, :, :].rearrange("o j (h c) -> o j h c", c=C)
            ch.link(nc.vector.tensor_tensor(link[:, :, 1:C], r4[:, 2, :, 1:C], r4[:, 3, :, 0:C - 1], ALU.is_equal))
            ch.link(nc.vector.tensor_copy(nxt[:, :, 0:C - 1], link[:, :, 1:C]))
            ch.link(nc.vector.tensor_tensor(one[:, :, :], r4[:, 2], r4[:, 3], ALU.is_equal))
            ch.link(nc.vector.tensor_tensor(g[:, :, :], one[:, :, :], link[:, :, :], ALU.mult))
            ch.link(nc.vector.tensor_tensor_scan(flat(fc[:, :, :]), flat(g[:, :, :]), row[:, 1, :], 0.0, ALU.mult, ALU.max))
            ch.link(nc.vector.tensor_tensor(g[:, :, :], one[:, :, :], nxt[:, :, :], ALU.mult))
            ch.link(nc.vector.tensor_tensor_scan(flat(bc[:, :, :])[:, ::-1], flat(g[:, :, :])[:, ::-1], row[:, 0, ::-1], 0.0, ALU.mult, ALU.max))
            cr = carry[:, :, :].rearrange("o j (c h) -> o j h c", h=H0)
            ch.link(nc.vector.tensor_tensor(cr[:, 0, :, 1:C], fc[:, :, 0:C - 1], link[:, :, 1:C], ALU.mult))
            ch.link(nc.vector.tensor_tensor(cr[:, 1, :, 0:C - 1], bc[:, :, 1:C], nxt[:, :, 0:C - 1], ALU.mult))
            v.sem_inc(carry_ok, 1)
            v.wait_ge(carry_ps, 1)
            ch.link(nc.vector.tensor_copy(carry_c[:, :], bank[1][:, 0:2]))
            for j in range(2):
                ch.link(nc.vector.tensor_scalar(same[:, 0:CE], d[:, :], ends[:, 2 + j:3 + j], carry_c[:, j:j + 1], ALU.is_equal, ALU.mult))
                ch.link(nc.vector.tensor_tensor(seg[:, :], seg[:, :], same[:, 0:CE], ALU.max))
            nc.vector.tensor_tensor(seg[:, :], k.score[:, 0:CE], seg[:, :], ALU.subtract).then_inc(diff_ok, 1)
            for n in range(-(-NT // 4)):
                v.wait_ge(w_ps, n + 1)
                if 4 * n + 4 <= NT:
                    nc.vector.tensor_copy(k.w[:, 4 * n * P:(4 * n + 4) * P], bank[2 + n % 4][:, :]).then_inc(w_ok, 1)
                else:
                    nc.vector.tensor_copy(k.w[0:TAIL, 4 * n * P:], bank[2 + n % 4][0:TAIL, 0:P]).then_inc(w_ok, 1)

        @block.scalar
        def _(act):
            act.wait_ge(diff_ok, 1)
            nc.scalar.activation(k.score[:, 0:CE], seg[:, :], ACT.Exp).then_inc(exp_ok, 1)

        @block.tensor
        def _(pe):
            pe.wait_ge(ends_ok, 1)
            for j in range(4):
                last = nc.tensor.transpose(bank[0][0:1, j * P:(j + 1) * P], ends[:, j:j + 1], k.ident[:, :])
            last.then_inc(ends_ps, 1)
            pe.wait_ge(carry_ok, 1)
            for j in range(2):
                last = nc.tensor.transpose(bank[1][:, j:j + 1], carry[0:1, j, :], k.ident[0:1, 0:1])
            last.then_inc(carry_ps, 1)
            pe.wait_ge(exp_ok, 1)
            for n in range(-(-NT // 4)):
                if n >= 4:
                    pe.wait_ge(w_ok, n - 3)
                for t in range(4 * n, min(4 * n + 4, NT)):
                    m = P if t < NT - 1 else TAIL
                    last = nc.tensor.transpose(bank[2 + n % 4][0:m, t % 4 * P:(t % 4 + 1) * P], k.score[:, t * P:t * P + m], k.ident[:, :])
                last.then_inc(w_ps, 1)

    with Stage(nc, "items") as s:
        Q = C * NT
        IC = -(-ITEMS // P)
        span = s.sb("span", [P, 2, Q])
        n_of, before, junk = s.sb("blocks_of_tile", [P, Q]), s.sb("items_before", [P, Q]), s.sb("junk", [P, Q])
        place_i, q_i, item_i = s.sb("place_i", [P, Q], I32), s.sb("tile_i", [P, Q], I32), s.sb("item_i", [P, IC], I32)
        place, q_f, item = s.sb("place", [P, Q]), s.sb("tile_f", [P, Q]), s.sb("item", [P, IC])
        zero, zero_ok, zeroed = s.sb("zero", [P, D]), s.sem("zero_ready"), s.sem("zeroed")
        got = s.sb("got", [P, 4, IC])
        res = s.sb("result", [P, 3, IC])
        loaded, iotas, dve, done, st = (s.sem(n) for n in ("span_loaded", "iotas", "dve", "result_ready", "tables_moved"))
        block = s.block()

        @block.gpsimd
        def _(pool):
            nc.gpsimd.memset(zero[:, :], 0.0).then_inc(zero_ok, 1)
            nc.gpsimd.iota(place_i[:, :], [[1, C], [C, NT]], base=0, channel_multiplier=0).then_inc(iotas, 1)
            nc.gpsimd.iota(q_i[:, :], [[1, Q]], base=0, channel_multiplier=0).then_inc(iotas, 1)
            nc.gpsimd.iota(item_i[:, :], [[P, IC]], base=0, channel_multiplier=1).then_inc(iotas, 1)

        @block.sync
        def _(sp):
            sp.wait_ge(zero_ok, 1)
            for tab in k.sorted:
                sp.dma_start(tab.rearrange("(t p) f -> p t f", p=P), zero[:, :].rearrange("p (o f) -> p o f", o=1).broadcast_to([P, tab.shape[0] // P, D])).then_inc(zeroed, 16)
            sp.dma_start(span[:, :, :], k.span_tab.rearrange("(o j) q -> o j q", o=1).broadcast_to([P, 2, Q])).then_inc(loaded, 16)
            with nc.allow_non_contiguous_dma(reason="item tables, a few words of each partition"):
                sp.wait_ge(done, 1)
                sp.dma_start(k.item_tab.rearrange("j (c p) -> p j c", p=P), res[:, :, :]).then_inc(st, 16)
            sp.wait_ge(st, 16)
            sp.dma_start(k.item_f[:, :, :], k.item_tab.rearrange("(o j) c -> o j c", o=1)[:, 0:2, 0:ITEMS]).then_inc(st, 16)
            sp.dma_start(k.item_base[:, :], k.item_tab[2:3, 0:ITEMS].broadcast_to([P, ITEMS])).then_inc(st, 16)
            sp.wait_ge(st, 48)
            sp.wait_ge(zeroed, 16 * len(k.sorted))

        @block.vector
        def _(v):
            ch = Chain(v, dve)
            v.wait_ge(loaded, 16)
            v.wait_ge(iotas, 3)
            for o, i in ((place, place_i), (q_f, q_i), (item, item_i)):
                ch.link(nc.vector.tensor_copy(o[:, :], i[:, :]))
            ch.link(nc.vector.tensor_tensor(n_of[:, :], span[:, 1, :], span[:, 0, :], ALU.subtract))
            ch.link(nc.vector.tensor_scalar(n_of[:, :], n_of[:, :], 1.0, None, ALU.add))
            ch.link(nc.vector.tensor_tensor_scan(before[:, :], n_of[:, :], n_of[:, :], 0.0, ALU.add, ALU.bypass))
            ch.link(nc.vector.tensor_tensor(before[:, :], before[:, :], n_of[:, :], ALU.subtract))
            for c in range(IC):
                ch.link(nc.vector.tensor_scalar(junk[:, :], before[:, :], item[:, c:c + 1], -1.0, ALU.is_le, ALU.add, accum_out=got[:, 0, c:c + 1]))
                for j, t in ((1, before), (2, span[:, 0, :]), (3, place)):
                    ch.link(nc.vector.scalar_tensor_tensor(junk[:, :], q_f[:, :], got[:, 0, c:c + 1], t[:, :] if j != 2 else t, ALU.is_equal, ALU.mult,
                                                           accum_out=got[:, j, c:c + 1]))
            ch.link(nc.vector.tensor_tensor(got[:, 0, :], item[:, :], got[:, 1, :], ALU.subtract))
            ch.link(nc.vector.tensor_tensor(got[:, 0, :], got[:, 0, :], got[:, 2, :], ALU.add))
            ch.link(nc.vector.tensor_copy(res[:, 0, :], got[:, 3, :]))
            ch.link(nc.vector.tensor_scalar(res[:, 1, :], got[:, 0, :], float(NT - 1), None, ALU.min))
            ch.link(nc.vector.tensor_scalar(res[:, 2, :], got[:, 0, :], float(P), None, ALU.mult))
            v.sem_inc(done, 1)


def registers(nc, eng, ap, top):
    return nc.values_load_multi_w_load_instructions(ap, engines=(eng,), min_val=0, max_val=top,
                                                    skip_runtime_bounds_check_because="the tables are built on the chip, within the bound")[1]


def aggregate(nc, a, k):
    with Stage(nc, "sum") as s:
        bank = s.banks()
        acc = s.sb("acc", [P, NT, D + H0])
        got = s.sb("gathered", [P, U, D])
        ids = s.sb("rows", [P, U], I32)
        msg, hot = s.sb("messages", [P, U, D + H0]), s.sb("one_hot", [P, U, P])
        den = s.sb("denominator", [P, NT, H0])
        item_i = s.sb("item_i", [1, 2, ITEMS], I32)
        tables, ids_ok, used = s.sem("tables"), s.sem("rows_ready"), Count(s, "rows_used", U)
        arrived = [s.sem(f"gathered{u}") for u in range(U)]
        msg_ok, summed, added = Count(s, "messages_ready", U), Count(s, "summed", U), Count(s, "added", 1)
        begun, cleared, dve = s.sem("gathers_begun"), s.sem("cleared"), s.sem("dve")
        block = s.block()

        @block.gpsimd
        def _(pool):
            nc.gpsimd.memset(acc[:, :, :], 0.0).then_inc(cleared, 1)
            with pool.Fori(0, ITEMS // U) as i:
                for u in range(U):
                    pool.wait_ge(ids_ok, i * U + u + 1)
                    pool.sem_inc(begun, 1)
                    nc.gpsimd.indirect_dma_start(got[:, u, :], None, k.h_tab, bass.IndirectOffsetOnAxis(ids[:, u:u + 1], 0)).then_inc(arrived[u], 16)

        @block.scalar
        def _(act):
            act.wait_ge(tables, 1)
            with act.Fori(0, ITEMS // U) as i:
                z = registers(nc, mybir.EngineType.Activation, item_i[0:1, 0, bass.ds(i * U, U)], NT * C - 1)
                for u in range(U):
                    used.slot(act, i * U + u)
                    nc.scalar.activation(ids[:, u:u + 1], col(k.edge_row, z[u]), ACT.Copy).then_inc(ids_ok, 1)

        @block.vector
        def _(v):
            nc.vector.tensor_copy(item_i[:, :, :], k.item_f[:, :, :]).then_inc(tables, 1)
            used.start(v)
            msg_ok.start(v)
            added.start(v)
            v.wait_ge(tables, 1)
            v.wait_ge(cleared, 1)
            LAG = 3

            def add(i, u, b):
                summed.done(v, i * U + u)
                added.slot(v, i * U + u)
                nc.vector.tensor_tensor(col(acc, b), bank[u][:, 0:D + H0], col(acc, b), ALU.add).then_inc(added.sem, 1)

            with v.Fori(0, ITEMS // U) as i:
                z = registers(nc, mybir.EngineType.DVE, item_i[0:1, 0, bass.ds(i * U, U)], NT * C - 1)
                b = registers(nc, mybir.EngineType.DVE, item_i[0:1, 1, bass.ds(i * U, U)], NT - 1)
                for u in range(U):
                    w = k.w[:, bass.ds(z[u] * H0, H0)]
                    v.wait_ge(arrived[u], (i + 1) * 16)
                    nc.vector.tensor_tensor(msg[:, u, 0:D].rearrange("p (h d) -> p h d", h=H0), got[:, u, :].rearrange("p (h d) -> p h d", h=H0),
                                            w.rearrange("p (h o) -> p h o", o=1).broadcast_to([P, H0, HD0]), ALU.mult).then_inc(used.sem, 1)
                    nc.vector.tensor_copy(msg[:, u, D:D + H0], w)
                    nc.vector.tensor_scalar(hot[:, u, :], k.iota[:, :], col(k.item_base, i * U + u), col(k.dst_f, z[u]),
                                            ALU.add, ALU.is_equal).then_inc(msg_ok.sem, 1)
                    if u >= LAG:
                        add(i, u - LAG, b[u - LAG])
                for u in range(U - LAG, U):
                    add(i, u, b[u])
            ch = Chain(v, dve)
            added.done(v, ITEMS - 1)
            ch.link(nc.vector.tensor_scalar(den[:, :, :], acc[:, :, D:D + H0], 1e-12, None, ALU.add))
            ch.link(nc.vector.reciprocal(den[:, :, :], den[:, :, :]))

            def finish(t, u):
                m = col(acc, t)[:, 0:D].rearrange("p (h d) -> p h d", h=H0)
                nc.vector.tensor_tensor(m, m, col(den, t).rearrange("p (h o) -> p h o", o=1).broadcast_to([P, H0, HD0]), ALU.mult).then_inc(dve, 1)
            c0 = ch.n
            tiles(v, NT, 7, finish)
            ch.n = c0 + NT
            v.wait_ge(dve, ch.n)
            ch.link(nc.vector.tensor_tensor(k.x[:, :, :], k.x[:, :, :], acc[:, :, 0:D], ALU.add))

        @block.tensor
        def _(pe):
            summed.start(pe)
            with pe.Fori(0, ITEMS // U) as i:
                for u in range(U):
                    msg_ok.done(pe, i * U + u)
                    nc.tensor.matmul(bank[u][:, 0:D + H0], hot[:, u, :], msg[:, u, :], start=True, stop=True).then_inc(summed.sem, 1)


def route_tiles(experts, top):
    return (N * top + experts * (P - 1)) // P


class Route:

    def __init__(self, nc, s, k, experts, top, spare=0):
        self.nc, self.k, self.K, self.top = nc, k, experts, top
        self.tiles = route_tiles(experts, top) + spare
        self.place = [s.sb(f"place{j}", [P, NT]) for j in range(top)]
        self.expert = s.sb("expert", [1, self.tiles], I32)

    def work_in(self, s, bank):
        experts, top, self.bank = self.K, self.top, bank
        K, T = experts, self.tiles
        self.logits = s.sb("logits", [P, NT, K])
        self.pick = [s.sb(f"pick{j}", [P, NT, K]) for j in range(top)]
        self.best = [s.sb(f"best{j}", [P, NT]) for j in range(top)]
        self.at = s.sb("at", [P, NT])
        self.work = s.sb("work", [P, NT, K])
        self.mask = self.logits
        self.reset = self.work[:, :, :].rearrange("p t e -> p (t e)").rearrange("p (e t) -> p e t", e=K)
        self.number, self.total = s.sb("number", [P, K]), s.sb("total", [P, K, NT])
        self.running = s.sb("running", [P, K, NT])
        self.count, self.start_row, self.count_i = s.sb("count", [P, K]), s.sb("start_row", [P, K]), s.sb("count_i", [P, K], I32)
        self.valid = s.sb("valid", [P, 1])
        self.tile_row_i, self.tile_row = s.sb("tile_row_i", [1, T], I32), s.sb("tile_row", [1, T])
        self.tile_cmp, self.expert_f = s.sb("tile_cmp", [1, T, K]), s.sb("expert_f", [1, T])
        self.iotas, self.picked, self.counted = s.sem("route_iotas"), s.sem("picked"), s.sem("counted")
        self.per = NT * K // 4 if NT * K > 512 else NT * K
        self.chunks = NT * K // self.per
        assert self.per <= 512 and self.chunks * self.per == NT * K

    def pool(self):
        nc = self.nc
        nc.gpsimd.iota(self.tile_row_i[:, :], [[P, self.tiles]], base=0, channel_multiplier=0).then_inc(self.iotas, 1)

    def choose(self, v, ch):
        nc, K = self.nc, self.K
        b3 = lambda x: x.rearrange("p (t o) -> p t o", o=1).broadcast_to([P, NT, K])
        bk = lambda x: x.rearrange("p (o e) -> p o e", o=1).broadcast_to([P, NT, K])
        ch.link(nc.vector.tensor_copy(self.number[:, :], self.k.iota[:, 0:K]))
        for j in range(self.top):
            ch.link(nc.vector.reduce_max(self.best[j][:, :], self.logits[:, :, :], AX.X))
            ch.link(nc.vector.tensor_tensor(self.work[:, :, :], self.logits[:, :, :], b3(self.best[j][:, :]), ALU.is_equal))
            ch.link(nc.vector.scalar_tensor_tensor(self.work[:, :, :], self.work[:, :, :], -1000.0, bk(self.number[:, :]), ALU.mult, ALU.add))
            ch.link(nc.vector.tensor_reduce(self.at[:, :], self.work[:, :, :], AX.X, ALU.min))
            ch.link(nc.vector.scalar_tensor_tensor(self.pick[j][:, :, :], bk(self.number[:, :]), -1000.0, b3(self.at[:, :]), ALU.add, ALU.is_equal))
            if j + 1 < self.top:
                ch.link(nc.vector.scalar_tensor_tensor(self.logits[:, :, :], self.pick[j][:, :, :], -3e38, self.logits[:, :, :], ALU.mult, ALU.add))

    def vector(self, v, ch):
        nc, K = self.nc, self.K
        v.wait_ge(self.iotas, 1)
        self.choose(v, ch)
        ch.link(nc.vector.tensor_scalar(self.valid[:, :], self.k.col[:, :], float(TAIL), None, ALU.is_lt))
        ch.link(nc.vector.tensor_copy(self.mask[:, :, :], self.pick[0][:, :, :]))
        for j in range(1, self.top):
            ch.link(nc.vector.tensor_tensor(self.mask[:, :, :], self.mask[:, :, :], self.pick[j][:, :, :], ALU.add))
        ch.link(nc.vector.tensor_scalar(self.mask[:, NT - 1, :], self.mask[:, NT - 1, :], self.valid[:, 0:1], None, ALU.mult))
        v.sem_inc(self.picked, 1)
        ch.link(nc.vector.tensor_copy(self.tile_row[:, :], self.tile_row_i[:, :]))
        v.wait_ge(self.counted, 1)
        w = flat(self.work[:, :, :])
        for n in range(self.chunks):
            ch.link(nc.vector.tensor_copy(w[:, n * self.per:(n + 1) * self.per], self.bank[4 + n][:, 0:self.per]))
        ch.link(nc.vector.tensor_copy(self.total[:, :, :], self.work[:, :, :].rearrange("p t e -> p e t")))
        ch.link(nc.vector.memset(self.reset, 1.0))
        ch.link(nc.vector.memset(self.reset[:, :, 0:1], 0.0))
        ch.link(nc.vector.tensor_tensor_scan(flat(self.running[:, :, :]), flat(self.reset), flat(self.total[:, :, :]), 0.0, ALU.mult, ALU.add))
        ch.link(nc.vector.tensor_scalar(self.count[:, :], self.running[:, :, NT - 1], float(P - 1), None, ALU.add))
        ch.link(nc.vector.tensor_copy(self.count_i[:, :], self.count[:, :]))
        ch.link(nc.vector.tensor_scalar(self.count_i[:, :], self.count_i[:, :], 7, 7, ALU.arith_shift_right, ALU.logical_shift_left))
        ch.link(nc.vector.tensor_copy(self.count[:, :], self.count_i[:, :]))
        ch.link(nc.vector.tensor_tensor_scan(self.start_row[:, :], self.count[:, :], self.count[:, :], 0.0, ALU.add, ALU.bypass))
        ch.link(nc.vector.tensor_tensor(self.start_row[:, :], self.start_row[:, :], self.count[:, :], ALU.subtract))
        ch.link(nc.vector.tensor_tensor(self.running[:, :, :], self.running[:, :, :], self.total[:, :, :], ALU.subtract))
        sr = self.start_row[:, :].rearrange("p (e o) -> p e o", o=1).broadcast_to([P, K, NT])
        ch.link(nc.vector.tensor_tensor(self.running[:, :, :], self.running[:, :, :], sr, ALU.add))
        ch.link(nc.vector.tensor_copy(self.work[:, :, :], self.running[:, :, :].rearrange("p e t -> p t e")))
        for n in range(self.chunks):
            c = w[:, n * self.per:(n + 1) * self.per]
            ch.link(nc.vector.tensor_tensor(c, self.bank[n][:, 0:self.per], c, ALU.add))
        for j in range(self.top):
            ch.link(nc.vector.tensor_tensor(self.mask[:, :, :], self.pick[j][:, :, :], self.work[:, :, :], ALU.mult))
            ch.link(nc.vector.reduce_sum(self.place[j][:, :], self.mask[:, :, :], AX.X))
        T = self.tiles
        ch.link(nc.vector.tensor_tensor(self.tile_cmp[:, :, :], self.tile_row[:, :].rearrange("p (t o) -> p t o", o=1).broadcast_to([1, T, K]),
                                        self.start_row[0:1, :].rearrange("p (o e) -> p o e", o=1).broadcast_to([1, T, K]), ALU.is_ge))
        ch.link(nc.vector.reduce_sum(self.expert_f[:, :], self.tile_cmp[:, :, :], AX.X))
        ch.link(nc.vector.tensor_scalar(self.expert_f[:, :], self.expert_f[:, :], -1.0, None, ALU.add))
        ch.link(nc.vector.tensor_copy(self.expert[:, :], self.expert_f[:, :]))

    def tensor(self, pe):
        nc = self.nc
        pe.wait_ge(self.picked, 1)
        m = flat(self.mask[:, :, :])
        for n in range(self.chunks):
            c = m[:, n * self.per:(n + 1) * self.per]
            nc.tensor.matmul(self.bank[n][:, 0:self.per], self.k.before[:, :], c, start=True, stop=True)
            last = nc.tensor.matmul(self.bank[4 + n][:, 0:self.per], self.k.ones[:, :], c, start=True, stop=True)
        last.then_inc(self.counted, 1)


def moe0(nc, a, k):
    with Stage(nc, "moe0") as s:
        bank = s.banks()
        norm = Norm(nc, s, k, bank[0:2])
        route = Route(nc, s, k, E0, 1)
        route.work_in(s, bank)
        T = route.tiles
        rw_n, rw = s.sb("router_natural", [E0, D]), s.sb("router", [P, DC, E0])
        rb = s.sb("router_bias", [P, E0])
        w1, w2 = s.sb("w1", [P, DC, E0, F0]), s.sb("w2", [F0, E0, D])
        b1, b2 = s.sb("b1", [P, E0, F0]), s.sb("b2", [P, E0, D])
        ids = s.sb("rows", [P, 4], I32)
        xi, xT = s.sb("tile", [P, 4, D]), s.sb("tile_T", [P, 4, D])
        hid, hT = s.sb("hidden", [P, 4, P]), s.sb("hidden_T", [F0, 4, P])
        y = s.sb("y", [P, 4, D])
        loaded, rw_ps, rw_ok = s.sem("weights_loaded"), s.sem("router_in_psum"), s.sem("router_ready")
        lg_ps, lg_ok = Count(s, "logits_in_psum", 2), Count(s, "logits_ready", 2)
        route_ok, row_ok = s.sem("route_ready"), s.sem("row_ready")
        scattered, gathered = [s.sem(f"scattered{u}") for u in range(4)], [s.sem(f"gathered{u}") for u in range(4)]
        begun, sent, added = s.sem("dma_begun"), s.sem("all_scattered"), Count(s, "added", 4)
        tile_in = [s.sem(f"tile_loaded{u}") for u in range(4)]
        tile_out = s.sem("tile_written")
        x_ps, x_ok, h_ps, h_ok, ht_ps, ht_ok, y_ps, y_add, y_ok, out_ok = (Count(s, n, 4) for n in (
            "x_in_psum", "xT_ready", "hidden_in_psum", "hidden_ready", "hidden_T_in_psum", "hidden_T_ready", "y_in_psum", "y_biased", "y_ready", "y_written"))
        block = s.block()

        @block.gpsimd
        def _(pool):
            route.pool()

            def scatter(i, u):
                t = i * 4 + u
                m = P if not isinstance(t, int) or t < NT - 1 else TAIL
                pool.wait_ge(row_ok, t + 1)
                pool.sem_inc(begun, 1)
                nc.gpsimd.indirect_dma_start(k.xs0, bass.IndirectOffsetOnAxis(ids[0:m, u:u + 1], 0), xi[0:m, u, :], None).then_inc(scattered[u], 16)
            rounds(pool, NT, 4, scatter)
            for u in range(4):
                pool.wait_ge(scattered[u], 16 * ((NT - u + 3) // 4))
            pool.sem_inc(sent, 1)
            pool.wait_ge(out_ok.sem, 4 + T)

            def gather(i, u):
                t = i * 4 + u
                m = P if not isinstance(t, int) or t < NT - 1 else TAIL
                pool.wait_ge(row_ok, NT + t + 1)
                pool.sem_inc(begun, 1)
                nc.gpsimd.indirect_dma_start(y[0:m, u, :], None, k.ys0, bass.IndirectOffsetOnAxis(ids[0:m, u:u + 1], 0)).then_inc(gathered[u], 16)
            rounds(pool, NT, 4, gather)

        @block.sync
        def _(sp):
            sp.dma_start(rw_n[:, :], a["L0_ffn_router_w"]).then_inc(loaded, 16)
            sp.dma_start(rb[:, :], a["L0_ffn_router_b"].rearrange("(o e) -> o e", o=1).broadcast_to([P, E0])).then_inc(loaded, 16)
            for c in range(DC):
                sp.dma_start(w1[:, c, :, :], a["L0_ffn_W1"][:, c * P:(c + 1) * P, :].rearrange("e p h -> p e h")).then_inc(loaded, 16)
            sp.dma_start(w2[:, :, :], a["L0_ffn_W2"].rearrange("e h d -> h e d")).then_inc(loaded, 16)
            for t, name in ((b1, "L0_ffn_b1"), (b2, "L0_ffn_b2")):
                v = a[name].rearrange("e h -> (e h)").rearrange("(o n) -> o n", o=1)
                sp.dma_start(flat(t[:, :, :]), v.broadcast_to([P, v.shape[1]])).then_inc(loaded, 16)
            sp.wait_ge(sent, 1)
            out_ok.start(sp)

            def load(i, u):
                x_ps.slot(sp, i * 4 + u)
                sp.dma_start(xi[:, u, :], rows(k.xs0, (i * 4 + u) * P, P)).then_inc(tile_in[u], 16)

            def save(i, u):
                y_ok.done(sp, i * 4 + u)
                sp.dma_start(rows(k.ys0, (i * 4 + u) * P, P), y[:, u, :]).then_inc(tile_out, 16)
            for u in range(4):
                load(0, u)
            with sp.Fori(0, T // 4 - 1) as i:
                for u in range(4):
                    load(i + 1, u)
                for u in range(4):
                    save(i, u)
                sp.wait_ge(tile_out, (i + 1) * 64)
                sp.sem_inc(out_ok.sem, 4)
            for u in range(4):
                save(T // 4 - 1, u)
            sp.wait_ge(tile_out, T * 16)
            sp.sem_inc(out_ok.sem, 4)

        @block.scalar
        def _(act):
            norm.root(act)
            tiles(act, NT, 2, lambda t, u: norm.keep(act, t, u, lg_ps))
            act.wait_ge(route_ok, 1)
            for n in (x_ok, ht_ok, y_ok):
                n.start(act)
            with act.Fori(0, T // 4) as i:
                for u in range(4):
                    x_ps.done(act, i * 4 + u)
                    nc.scalar.activation(xT[:, u, :], bank[2 * u][:, 0:D], ACT.Copy).then_inc(x_ok.sem, 1)
                for u in range(4):
                    ht_ps.done(act, i * 4 + u)
                    nc.scalar.activation(hT[:, u, :], bank[2 * u][0:F0, 3 * P:4 * P], ACT.Relu).then_inc(ht_ok.sem, 1)
                for u in range(4):
                    y_add.done(act, i * 4 + u)
                    nc.scalar.activation(y[:, u, :], y[:, u, :], ACT.Relu).then_inc(y_ok.sem, 1)

        @block.vector
        def _(v):
            ch = Chain(v, norm.dve)
            ch.link(nc.vector.memset(hid[:, :, :], 0.0))
            norm.statistics(v, ch)
            v.wait_ge(loaded, 7 * 16)
            v.wait_ge(rw_ps, 1)
            nc.vector.tensor_copy(rw[:, :, :], bank[4][:, 0:DC * E0].rearrange("p (c e) -> p c e", c=DC)).then_inc(rw_ok, 1)
            lg_ok.start(v)

            def logits(t, u):
                lg_ps.done(v, t)
                nc.vector.tensor_tensor(col(route.logits, t), bank[2 + u][:, 0:E0], rb[:, :], ALU.add).then_inc(lg_ok.sem, 1)
            norm.normalise(v, 0, 0)
            with v.Fori(0, (NT - 1) // 2) as i:
                for u in range(2):
                    norm.normalise(v, i * 2 + u + 1, 1 - u)
                    logits(i * 2 + u, u)
            logits(NT - 1, 0)
            lg_ok.done(v, NT - 1)
            route.vector(v, ch)
            v.sem_inc(route_ok, 1)

            def send(i, u):
                t = i * 4 + u
                if not isinstance(i, int) or i:
                    v.wait_ge(scattered[u], i * 16)
                nc.vector.tensor_scalar(xi[:, u, :], col(k.x, t), col(norm.mean, t), col(norm.rstd, t), ALU.subtract, ALU.mult)
                nc.vector.tensor_copy(ids[:, u:u + 1], col(route.place[0], t)).then_inc(row_ok, 1)
            rounds(v, NT, 4, send)
            for n in (h_ok, y_add):
                n.start(v)
            with v.Fori(0, T // 4) as i:
                e = registers(nc, mybir.EngineType.DVE, route.expert[0:1, bass.ds(i * 4, 4)], E0 - 1)
                for u in range(4):
                    h_ps.done(v, i * 4 + u)
                    nc.vector.tensor_tensor(hid[:, u, 0:F0], bank[2 * u][:, D:D + F0], col(b1, e[u]), ALU.add).then_inc(h_ok.sem, 1)
                for u in range(4):
                    y_ps.done(v, i * 4 + u)
                    out_ok.slot(v, i * 4 + u)
                    nc.vector.tensor_tensor(y[:, u, :], bank[2 * u + 1][:, 0:D], col(b2, e[u]), ALU.add).then_inc(y_add.sem, 1)
            for u in range(4):
                v.wait_ge(scattered[u], 16 * ((NT - u + 3) // 4))

            def address(i, u):
                nc.vector.tensor_copy(ids[:, u:u + 1], col(route.place[0], i * 4 + u)).then_inc(row_ok, 1)

            def add(i, u):
                v.wait_ge(gathered[u], i * 16 + 16)
                m = P if not isinstance(i, int) or i * 4 + u < NT - 1 else TAIL
                x = col(k.x, i * 4 + u)[0:m]
                nc.vector.tensor_tensor(x, x, y[0:m, u, :], ALU.add).then_inc(norm.dve, 1)
            for u in range(4):
                address(0, u)
            with v.Fori(0, NT // 4 - 1) as i:
                for u in range(4):
                    add(i, u)
                    address(i + 1, u)
            for u in range(4):
                add(NT // 4 - 1, u)
            address(NT // 4, 0)
            add(NT // 4, 0)

        @block.tensor
        def _(pe):
            pe.wait_ge(loaded, 7 * 16)
            for c in range(DC):
                last = nc.tensor.transpose(bank[4][:, c * E0:(c + 1) * E0], rw_n[:, c * P:(c + 1) * P], k.ident[0:E0, 0:E0])
            last.then_inc(rw_ps, 1)
            pe.wait_ge(rw_ok, 1)
            norm.t_ps.start(pe)
            lg_ps.start(pe)

            def body(t, u):
                norm.transpose(pe, t, u)
                norm.t_ok.done(pe, t)
                lg_ok.slot(pe, t)
                for c in range(DC):
                    last = nc.tensor.matmul(bank[2 + u][:, 0:E0], norm.xT[:, u, c * P:(c + 1) * P], rw[:, c, :], start=(c == 0), stop=(c == DC - 1))
                last.then_inc(lg_ps.sem, 1)
            tiles(pe, NT, 2, body)
            route.tensor(pe)
            pe.wait_ge(route_ok, 1)
            for n in (x_ps, h_ps, ht_ps, y_ps):
                n.start(pe)
            with pe.Fori(0, T // 4) as i:
                e = registers(nc, mybir.EngineType.PE, route.expert[0:1, bass.ds(i * 4, 4)], E0 - 1)
                for u in range(4):
                    pe.wait_ge(tile_in[u], (i + 1) * 16)
                    for c in range(DC):
                        last = nc.tensor.transpose(bank[2 * u][:, c * P:(c + 1) * P], xi[:, u, c * P:(c + 1) * P], k.ident[:, :])
                    last.then_inc(x_ps.sem, 1)
                for u in range(4):
                    x_ok.done(pe, i * 4 + u)
                    for c in range(DC):
                        last = nc.tensor.matmul(bank[2 * u][:, D:D + F0], xT[:, u, c * P:(c + 1) * P], col(w1[:, c], e[u]),
                                                start=(c == 0), stop=(c == DC - 1))
                    last.then_inc(h_ps.sem, 1)
                for u in range(4):
                    h_ok.done(pe, i * 4 + u)
                    nc.tensor.transpose(bank[2 * u][:, 3 * P:4 * P], hid[:, u, :], k.ident[:, :]).then_inc(ht_ps.sem, 1)
                for u in range(4):
                    ht_ok.done(pe, i * 4 + u)
                    y_add.slot(pe, i * 4 + u)
                    nc.tensor.matmul(bank[2 * u + 1][:, 0:D], hT[:, u, :], col(w2, e[u]), start=True, stop=True).then_inc(y_ps.sem, 1)


def attend1(nc, a, k):
    with Stage(nc, "gnn1") as s:
        bank = s.banks()
        norm = Norm(nc, s, k, bank[0:2])
        W = D + 2 * H1
        w, wT = s.sb("w", [P, DC, W]), s.sb("wT", [P, DC, D])
        ablk = s.sb("attn_blocks", [P, DC, 2 * H1])
        g = s.sb("rows_out", [P, 2, W])
        ids = s.sb("rows", [P, 4, 2], I32)
        got, left = s.sb("gathered", [P, 4, W]), s.sb("row_half", [P, 4, H1])
        al, mx, ex, sm, prod, red = (s.sb(n, [P, 4, m]) for n, m in (("alpha", H1), ("max", 1), ("exp", H1), ("sum", 1), ("products", D), ("reduced", HD1)))
        loaded, cleared, wt_ps, wt_ok, v_ps, v_ok = (s.sem(n) for n in ("weights_loaded", "cleared", "wT_in_psum", "wT_ready", "v_in_psum", "v_ready"))
        xt_ps, g_ok, stored, written = Count(s, "products_in_psum", 2), Count(s, "rows_ready", 2), Count(s, "rows_stored", 2), s.sem("rows_written")
        tables, begun, ids_ok = s.sem("tables_written"), s.sem("gathers_begun"), s.sem("ids_ready")
        arrived = [s.sem(f"arrived{u}") for u in range(4)]
        used, al_ok, ex_ok = Count(s, "used", 4), Count(s, "alpha_ready", 4), Count(s, "exp_ready", 4)
        block = s.block()

        @block.gpsimd
        def _(pool):
            nc.gpsimd.memset(ablk[:, :, :], 0.0).then_inc(cleared, 1)
            pool.wait_ge(tables, 1)

            def gather(t, u):
                pool.wait_ge(ids_ok, t + 1)
                pool.sem_inc(begun, 1)
                nc.gpsimd.indirect_dma_start(got[:, u, :], None, k.g_tab, bass.IndirectOffsetOnAxis(ids[:, u, 0:1], 0)).then_inc(arrived[u], 16)
                nc.gpsimd.indirect_dma_start(left[:, u, :], None, k.l_tab, bass.IndirectOffsetOnAxis(ids[:, u, 1:2], 0)).then_inc(arrived[u], 16)
            tiles(pool, NT, 4, gather)

        @block.sync
        def _(sp):
            sp.dma_start(w[:, :, 0:D], a["L1_gnn_weight"].rearrange("(c p) o -> p c o", p=P)).then_inc(loaded, 16)
            sp.wait_ge(cleared, 1)
            with nc.allow_non_contiguous_dma(reason="short vectors onto partitions"):
                for j, name in enumerate(("L1_gnn_attn_r", "L1_gnn_attn_l")):
                    for h in range(H1):
                        p0 = h * HD1 % P
                        sp.dma_start(ablk[p0:p0 + HD1, h * HD1 // P, j * H1 + h:j * H1 + h + 1],
                                     a[name][h:h + 1, :].rearrange("a b -> b a")).then_inc(loaded, 16)
            stored.start(sp)

            def save(t, u):
                g_ok.done(sp, t)
                sp.dma_start(rows(k.g_tab, t * P, P), g[:, u, :]).then_inc(written, 16)
                sp.dma_start(rows(k.l_tab, t * P, P), g[:, u, D + H1:W]).then_inc(written, 16)
                sp.wait_ge(written, (t + 1) * 32)
                sp.sem_inc(stored.sem, 1)
            tiles(sp, NT, 2, save)
            sp.sem_inc(tables, 1)

        @block.scalar
        def _(act):
            norm.root(act)
            g_ok.start(act)

            def body(t, u):
                norm.keep(act, t, u, xt_ps)
                xt_ps.done(act, t)
                stored.slot(act, t)
                nc.scalar.activation(g[:, u, :], bank[2 + u][:, 0:W], ACT.Copy).then_inc(g_ok.sem, 1)
            tiles(act, NT, 2, body)
            ex_ok.start(act)

            def exps(t, u):
                al_ok.done(act, t)
                nc.scalar.activation(ex[:, u, :], al[:, u, :], ACT.Exp, accum_out=sm[:, u, :]).then_inc(ex_ok.sem, 1)
            tiles(act, NT, 4, exps)

        @block.vector
        def _(v):
            ch = Chain(v, norm.dve)
            norm.statistics(v, ch)
            v.wait_ge(wt_ps, 1)
            nc.vector.tensor_copy(wT[:, :, :], bank[4][:, :].rearrange("p (c f) -> p c f", c=DC)).then_inc(wt_ok, 1)
            v.wait_ge(v_ps, 1)
            nc.vector.tensor_copy(w[:, :, D:W], bank[5][:, 0:DC * 2 * H1].rearrange("p (c j) -> p c j", c=DC)).then_inc(v_ok, 1)
            tiles(v, NT, 2, lambda t, u: norm.normalise(v, t, u))
            used.start(v)
            al_ok.start(v)
            c0 = ch.n

            def one(t, u, m):
                used.slot(v, t)
                nc.vector.tensor_copy(ids[:, u, 0:1], col(k.dst_i, t))
                nc.vector.tensor_copy(ids[:, u, 1:2], col(k.src_i, t)).then_inc(ids_ok, 1)

            def first(n, i, u):
                t = i * 4 + u
                v.wait_ge(arrived[u], (i + 1) * 32)
                ch.link(nc.vector.tensor_tensor(al[:, u, :], left[:, u, :], got[:, u, D:D + H1], ALU.add))
                ch.link(nc.vector.scalar_tensor_tensor(al[:, u, :], al[:, u, :], 0.01, al[:, u, :], ALU.mult, ALU.max))
                ch.link(nc.vector.reduce_max(mx[:, u, :], al[:, u, :], AX.X))
                nc.vector.tensor_scalar(al[:, u, :], al[:, u, :], mx[:, u, :], None, ALU.subtract).then_inc(al_ok.sem, 1)

            def second(n, i, u):
                t = i * 4 + u
                ex_ok.done(v, t)
                ch.link(nc.vector.reciprocal(mx[:, u, :], sm[:, u, :]))
                p4 = prod[:, u, :].rearrange("p (h d) -> p h d", h=H1)
                ch.link(nc.vector.tensor_tensor(p4, got[:, u, 0:D].rearrange("p (h d) -> p h d", h=H1),
                                                ex[:, u, :].rearrange("p (h o) -> p h o", o=1).broadcast_to([P, H1, HD1]), ALU.mult))
                ch.link(nc.vector.reduce_sum(red[:, u, :], p4.rearrange("p h d -> p d h"), AX.X))
                x4 = col(k.x, t).rearrange("p (h d) -> p h d", h=H1)
                nc.vector.scalar_tensor_tensor(x4, red[:, u, :].rearrange("p (o d) -> p o d", o=1).broadcast_to([P, H1, HD1]),
                                               mx[:, u, :], x4, ALU.mult, ALU.add).then_inc(used.sem, 1)
            for u in range(4):
                one(u, u, 0)
            with v.Fori(0, NT // 4 - 1) as i:
                ch.n = c0 + i * 24
                for u in range(4):
                    first(0, i, u)
                for u in range(4):
                    second(0, i, u)
                    one(i * 4 + 4 + u, u, 0)
            i = NT // 4 - 1
            ch.n = c0 + i * 24
            for u in range(4):
                first(0, i, u)
            for u in range(4):
                second(0, i, u)
            one(NT - 1, 0, 0)
            first(0, i + 1, 0)
            second(0, i + 1, 0)
            used.done(v, NT - 1)

        @block.tensor
        def _(pe):
            pe.wait_ge(loaded, 16 * (1 + 2 * H1))
            for oc in range(DC):
                for fc in range(DC):
                    last = nc.tensor.transpose(bank[4][:, oc * D + fc * P:oc * D + (fc + 1) * P], w[:, fc, oc * P:(oc + 1) * P], k.ident[:, :])
            last.then_inc(wt_ps, 1)
            pe.wait_ge(wt_ok, 1)
            for fc in range(DC):
                for oc in range(DC):
                    last = nc.tensor.matmul(bank[5][:, fc * 2 * H1:(fc + 1) * 2 * H1], wT[:, oc, fc * P:(fc + 1) * P], ablk[:, oc, :],
                                            start=(oc == 0), stop=(oc == DC - 1))
            last.then_inc(v_ps, 1)
            pe.wait_ge(v_ok, 1)
            norm.t_ps.start(pe)
            xt_ps.start(pe)

            def body(t, u):
                norm.transpose(pe, t, u)
                norm.t_ok.done(pe, t)
                g_ok.slot(pe, t)
                for c in range(DC):
                    last = nc.tensor.matmul(bank[2 + u][:, 0:W], norm.xT[:, u, c * P:(c + 1) * P], w[:, c, :], start=(c == 0), stop=(c == DC - 1))
                last.then_inc(xt_ps.sem, 1)
            tiles(pe, NT, 2, body)


SPARE = 2 + route_tiles(E1, 2) % 2
T1 = route_tiles(E1, 2) + route_tiles(E1, 2) % 2
MC = F1 // P
XS, WS, HS = 64.0, 256.0, 64.0


def route1(nc, a, k):
    with Stage(nc, "route1") as s:
        bank = s.banks()
        norm = Norm(nc, s, k, bank[0:2])
        route = k.route1
        route.work_in(s, bank)
        wr, br = s.sb("router", [P, DC, E1]), s.sb("router_bias", [P, E1])
        st2, mean2, rstd2, var2, sd2, tmp2 = s.sb("stats2", [P, NT, 6]), *(s.sb(n, [P, NT]) for n in ("mean2", "rstd2", "var2", "sd2", "tmp2"))
        ids, out = s.sb("rows", [P, 4, 2], I32), s.sb("out", [P, 4, D])
        mid = s.sb("mid", [P, 4, D])
        loaded, lg_ps, lg_ok = s.sem("loaded"), Count(s, "logits_in_psum", 2), Count(s, "logits_ready", 2)
        var2_ok, sd2_ok, diff_ok, share_ok, row_ok, begun = (s.sem(n) for n in ("var2_ready", "sd2_ready", "diff_ready", "share_ready", "row_ready", "scatters_begun"))
        scattered = [s.sem(f"scattered{u}") for u in range(4)]
        mid_ok = s.sem("mid_ready")
        saved = s.sem("x_saved")
        block = s.block()

        @block.gpsimd
        def _(pool):
            route.pool()

            def scatter(i, u):
                t = i * 4 + u
                m = P if not isinstance(t, int) or t < NT - 1 else TAIL
                pool.wait_ge(row_ok, t + 1)
                pool.sem_inc(begun, 1)
                for j in range(2):
                    nc.gpsimd.indirect_dma_start(k.xs1, bass.IndirectOffsetOnAxis(ids[0:m, u, j:j + 1], 0), out[0:m, u, :], None).then_inc(scattered[u], 16)
            rounds(pool, NT, 4, scatter)
            for u in range(4):
                pool.wait_ge(scattered[u], 32 * ((NT - u + 3) // 4))

        @block.sync
        def _(sp):
            sp.dma_start(wr[:, :, :], a["L1_ffn_Wr"].rearrange("(c p) e -> p c e", p=P)).then_inc(loaded, 16)
            sp.dma_start(br[:, :], a["L1_ffn_br"].rearrange("(o e) -> o e", o=1).broadcast_to([P, E1])).then_inc(loaded, 16)
            sp.dma_start(k.x3.rearrange("(t p) f -> p t f", p=P), k.x[:, :, :]).then_inc(saved, 16)
            sp.wait_ge(saved, 16)

        @block.scalar
        def _(act):
            norm.root(act)
            tiles(act, NT, 2, lambda t, u: norm.keep(act, t, u, lg_ps))
            act.wait_ge(var2_ok, 1)
            nc.scalar.activation(sd2[:, :], var2[:, :], ACT.Sqrt).then_inc(sd2_ok, 1)
            act.wait_ge(diff_ok, 1)
            nc.scalar.activation(k.share[1][:, :], k.share[1][:, :], ACT.Exp).then_inc(share_ok, 1)

        @block.vector
        def _(v):
            ch = Chain(v, norm.dve)
            norm.statistics(v, ch)
            v.wait_ge(loaded, 32)
            lg_ok.start(v)

            def logits(t, u):
                lg_ps.done(v, t)
                nc.vector.tensor_tensor(col(route.logits, t), bank[2 + u][:, 0:E1], br[:, :], ALU.add).then_inc(lg_ok.sem, 1)

            def normalise(t, u):
                norm.normalise(v, t, u)
                norm.xn_ok.done(v, t)
                nc.vector.bn_stats(col(st2, t), norm.xn[:, u, :]).then_inc(mid_ok, 1)
            normalise(0, 0)
            with v.Fori(0, (NT - 1) // 2) as i:
                for u in range(2):
                    normalise(i * 2 + u + 1, 1 - u)
                    logits(i * 2 + u, u)
            logits(NT - 1, 0)
            lg_ok.done(v, NT - 1)
            v.wait_ge(mid_ok, NT)
            me, ve, mo, vo = (st2[:, :, i] for i in (1, 2, 4, 5))
            tmp, var, mean = tmp2[:, :], var2[:, :], mean2[:, :]
            moments(nc, ch, me, ve, mo, vo, mean, var, tmp)
            v.sem_inc(var2_ok, 1)
            v.wait_ge(sd2_ok, 1)
            rsqrt_newton(nc, ch, rstd2[:, :], tmp, var, sd2[:, :])
            route.vector(v, ch)
            ch.link(nc.vector.tensor_tensor(k.share[1][:, :], route.best[1][:, :], route.best[0][:, :], ALU.subtract))
            v.sem_inc(diff_ok, 1)
            v.wait_ge(share_ok, 1)
            ch.link(nc.vector.tensor_scalar(k.share[0][:, :], k.share[1][:, :], 1.0, None, ALU.add))
            ch.link(nc.vector.reciprocal(k.share[0][:, :], k.share[0][:, :]))
            ch.link(nc.vector.tensor_tensor(k.share[1][:, :], k.share[1][:, :], k.share[0][:, :], ALU.mult))
            c0 = NT

            def send(i, u):
                t = i * 4 + u
                if not isinstance(i, int) or i:
                    v.wait_ge(scattered[u], i * 32)
                nc.vector.tensor_scalar(mid[:, u, :], col(k.x, t), col(norm.mean, t), col(norm.rstd, t), ALU.subtract, ALU.mult).then_inc(mid_ok, 1)
                for j in range(2):
                    nc.vector.tensor_copy(ids[:, u, j:j + 1], col(route.place[j], t))
                v.wait_ge(mid_ok, NT + 1 + t)
                nc.vector.tensor_scalar(out[:, u, :], mid[:, u, :], col(mean2, t), col(rstd2, t), ALU.subtract, ALU.mult).then_inc(row_ok, 1)
            rounds(v, NT, 4, send)

        @block.tensor
        def _(pe):
            pe.wait_ge(loaded, 32)
            norm.t_ps.start(pe)
            lg_ps.start(pe)

            def body(t, u):
                norm.transpose(pe, t, u)
                norm.t_ok.done(pe, t)
                lg_ok.slot(pe, t)
                for c in range(DC):
                    last = nc.tensor.matmul(bank[2 + u][:, 0:E1], norm.xT[:, u, c * P:(c + 1) * P], wr[:, c, :], start=(c == 0), stop=(c == DC - 1))
                last.then_inc(lg_ps.sem, 1)
            tiles(pe, NT, 2, body)
            route.tensor(pe)


def experts1(nc, a, k):
    with Stage(nc, "moe1") as s:
        bank = s.banks()
        route, DVE, PE, SC = k.route1, mybir.EngineType.DVE, mybir.EngineType.PE, mybir.EngineType.Activation
        w1 = [s.sb(f"w1_{n}", [P, DC, E1 * F1], F16) for n in ("high", "low")]
        w2 = [s.sb(f"w2_{n}", [P, MC, E1 * D], F16) for n in ("high", "low")]
        stage = s.sb("stage", [P, 2, 2048])
        lg, lb, b1 = s.sb("gain_T", [P, DC, E1]), s.sb("shift_T", [P, DC, E1]), s.sb("b1_T", [P, E1, MC])
        rows8, rowsb = s.sb("gain_rows", [E1, 2, D]), s.sb("b1_rows", [E1 * MC, P])
        b2 = s.sb("b2", [P, E1, D])
        xi, xe = s.sb("tile", [P, 2, D]), s.sb("tile_T", [P, 2, D])
        xh = [s.sb(f"x_{n}", [P, 2, DC, P], F16) for n in ("high", "low")]
        hg = s.sb("hidden", [P, 2, MC * P])
        hh = [s.sb(f"hidden_{n}", [P, 2, MC * P], F16) for n in ("high", "low")]
        y = s.sb("y", [P, 2, D])
        small, small_ps, small_ok = s.sem("small_loaded"), s.sem("small_in_psum"), s.sem("small_ready")
        staged = [s.sem(f"staged{u}") for u in range(2)]
        high_ok, low_ok = Count(s, "high_ready", 2), Count(s, "low_ready", 2)
        tile_in, tile_out = [s.sem(f"tile_loaded{u}") for u in range(2)], s.sem("tile_written")
        x_ps, xe_ok, xs_ok, y_ps, y_ok, out_ok = (Count(s, n, 2) for n in (
            "x_in_psum", "xe_ready", "x_split", "y_in_psum", "y_ready", "y_written"))
        h_ps, hg_ok, hs_ok = Count(s, "hidden_in_psum", 4), Count(s, "hidden_ready", 4), Count(s, "hidden_split", 4)
        xhi_ok, hhi_ok = Count(s, "x_high", 2), Count(s, "hidden_high", 4)
        PIECES = 2 * E1

        block = s.block()

        def part(n):
            e = n % E1
            if n < E1:
                return [t[:, :, e * F1:(e + 1) * F1] for t in w1], DC, a["L1_ffn_W1"][e].rearrange("(c p) h -> p c h", p=P)
            return [t[:, :, e * D:(e + 1) * D] for t in w2], MC, a["L1_ffn_W2"][e].rearrange("(c p) h -> p c h", p=P)

        @block.sync
        def _(sp):
            sp.dma_start(rows8[:, 0, :], a["L1_ffn_ln_g"]).then_inc(small, 16)
            sp.dma_start(rows8[:, 1, :], a["L1_ffn_ln_b"]).then_inc(small, 16)
            sp.dma_start(rowsb[:, :], a["L1_ffn_b1"].rearrange("e (m p) -> (e m) p", p=P)).then_inc(small, 16)
            v = a["L1_ffn_b2"].rearrange("e h -> (e h)").rearrange("(o n) -> o n", o=1)
            sp.dma_start(flat(b2[:, :, :]), v.broadcast_to([P, v.shape[1]])).then_inc(small, 16)
            for n in range(PIECES):
                low_ok.slot(sp, n)
                _, m, src = part(n)
                sp.dma_start(stage[:, n % 2, :].rearrange("p (c h) -> p c h", c=m), src).then_inc(staged[n % 2], 16)
            out_ok.start(sp)

            def load(i, u):
                x_ps.slot(sp, i * 2 + u)
                sp.dma_start(xi[:, u, :], rows(k.xs1, (i * 2 + u) * P, P)).then_inc(tile_in[u], 16)
            for u in range(2):
                load(0, u)
            with sp.Fori(0, T1 // 2) as i:
                for u in range(2):
                    load(i + 1, u)
                    y_ok.done(sp, i * 2 + u)
                    sp.dma_start(rows(k.ys1, (i * 2 + u) * P, P), y[:, u, :]).then_inc(tile_out, 16)
                    sp.wait_ge(tile_out, (i * 2 + u + 1) * 16)
                    sp.sem_inc(out_ok.sem, 1)

        @block.scalar
        def _(act):
            high_ok.start(act)
            for n in range(PIECES):
                to, m, _ = part(n)
                act.wait_ge(staged[n % 2], 16 * (n // 2 + 1))
                nc.scalar.activation(to[0], stage[:, n % 2, :].rearrange("p (c h) -> p c h", c=m), ACT.Copy, scale=WS).then_inc(high_ok.sem, 1)
            act.wait_ge(small_ok, 1)
            xe_ok.start(act)
            hg_ok.start(act)

            def turn(t, u, e):
                x_ps.done(act, t)
                xs_ok.slot(act, t)
                for c in range(DC):
                    last = nc.scalar.activation(xe[:, u, c * P:(c + 1) * P], bank[4 + u][:, c * P:(c + 1) * P], ACT.Identity,
                                                scale=col(lg[:, c, :], e), bias=col(lb[:, c, :], e))
                last.then_inc(xe_ok.sem, 1)

            def gelu(t, u, e):
                for q in range(2):
                    h_ps.done(act, 2 * t + q)
                    hs_ok.slot(act, 2 * t + q)
                    for m in range(4 * q, 4 * q + 4):
                        last = nc.scalar.activation(hg[:, u, m * P:(m + 1) * P], bank[2 * u + q][:, (m - 4 * q) * P:(m - 4 * q + 1) * P], ACT.Gelu,
                                                    scale=1.0 / (XS * WS), bias=col(b1[:, :, m], e))
                    last.then_inc(hg_ok.sem, 1)
            e = registers(nc, SC, route.expert[0:1, 0:2], E1 - 1)
            turn(0, 0, e[0])
            turn(1, 1, e[1])
            gelu(0, 0, e[0])
            with act.Fori(0, T1 // 2) as i:
                e = registers(nc, SC, route.expert[0:1, bass.ds(i * 2, 4)], E1 - 1)
                for u in range(2):
                    turn(i * 2 + 2 + u, u, e[2 + u])
                    gelu(i * 2 + 1 + u, 1 - u, e[1 + u])

        @block.vector
        def _(v):
            low_ok.start(v)
            v.wait_ge(small, 64)
            v.wait_ge(small_ps, 1)
            for j, t in ((0, lg), (1, lb)):
                nc.vector.tensor_scalar(t[:, :, :], bank[7][:, j * DC * E1:(j + 1) * DC * E1].rearrange("p (c e) -> p c e", c=DC), XS, None, ALU.mult)
            nc.vector.tensor_copy(b1[:, :, :], bank[7][:, 4 * E1:4 * E1 + E1 * MC].rearrange("p (e m) -> p e m", e=E1)).then_inc(small_ok, 1)
            for n in range(PIECES):
                to, m, _ = part(n)
                high_ok.done(v, n)
                nc.vector.scalar_tensor_tensor(to[1], stage[:, n % 2, :].rearrange("p (c h) -> p c h", c=m), WS, to[0], ALU.mult, ALU.subtract).then_inc(low_ok.sem, 1)
            for n in (xs_ok, xhi_ok, hs_ok, hhi_ok, y_ok):
                n.start(v)

            def split_x(t, u):
                xe_ok.done(v, t)
                h_ps.slot(v, 2 * t + 1)
                f = xe[:, u, :].rearrange("p (c q) -> p c q", c=DC)
                nc.vector.tensor_copy(xh[0][:, u], f).then_inc(xhi_ok.sem, 1)
                xhi_ok.done(v, t)
                nc.vector.tensor_tensor(xh[1][:, u], f, xh[0][:, u], ALU.subtract).then_inc(xs_ok.sem, 1)

            def split_h(t, u):
                for q in range(2):
                    hg_ok.done(v, 2 * t + q)
                    if q == 0:
                        y_ps.slot(v, t)
                    f = hg[:, u, q * 512:(q + 1) * 512]
                    nc.vector.tensor_scalar(hh[0][:, u, q * 512:(q + 1) * 512], f, HS, None, ALU.mult).then_inc(hhi_ok.sem, 1)
                    hhi_ok.done(v, 2 * t + q)
                    nc.vector.scalar_tensor_tensor(hh[1][:, u, q * 512:(q + 1) * 512], f, HS, hh[0][:, u, q * 512:(q + 1) * 512], ALU.mult, ALU.subtract).then_inc(hs_ok.sem, 1)

            def result(t, u, e):
                y_ps.done(v, t)
                out_ok.slot(v, t)
                nc.vector.scalar_tensor_tensor(y[:, u, :], bank[6 + u][:, 0:D], 1.0 / (HS * WS), col(b2, e), ALU.mult, ALU.add).then_inc(y_ok.sem, 1)
            split_x(0, 0)
            split_x(1, 1)
            split_h(0, 0)
            with v.Fori(0, T1 // 2) as i:
                e = registers(nc, DVE, route.expert[0:1, bass.ds(i * 2, 2)], E1 - 1)
                for u in range(2):
                    split_x(i * 2 + 2 + u, u)
                    split_h(i * 2 + 1 + u, 1 - u)
                    result(i * 2 + u, u, e[u])

        @block.tensor
        def _(pe):
            pe.wait_ge(small, 64)
            for j in range(2):
                for c in range(DC):
                    o = (j * DC + c) * E1
                    nc.tensor.transpose(bank[7][:, o:o + E1], rows8[:, j, c * P:(c + 1) * P], k.ident[0:E1, 0:E1])
            nc.tensor.transpose(bank[7][:, 4 * E1:4 * E1 + E1 * MC], rowsb[:, :], k.ident[0:E1 * MC, 0:E1 * MC]).then_inc(small_ps, 1)
            pe.wait_ge(small_ok, 1)
            for n in (x_ps, h_ps, y_ps):
                n.start(pe)
            passes = ((0, 0), (0, 1), (1, 0))

            def turn(i, u):
                pe.wait_ge(tile_in[u], (i + 1) * 16)
                xe_ok.slot(pe, i * 2 + u)
                for c in range(DC):
                    last = nc.tensor.transpose(bank[4 + u][:, c * P:(c + 1) * P], xi[:, u, c * P:(c + 1) * P], k.ident[:, :])
                last.then_inc(x_ps.sem, 1)

            def up(t, u, e):
                xs_ok.done(pe, t)
                for q in range(2):
                    hg_ok.slot(pe, 2 * t + q)
                    for m in range(4 * q, 4 * q + 4):
                        o = (m - 4 * q) * P
                        for n, (pw, px) in enumerate(passes):
                            for c in range(DC):
                                last = nc.tensor.matmul(bank[2 * u + q][:, o:o + P], w1[pw][:, c, bass.ds(e * F1 + m * P, P)], xh[px][:, u, c, :],
                                                        start=(n == 0 and c == 0), stop=(n == 2 and c == DC - 1))
                    last.then_inc(h_ps.sem, 1)

            def down(t, u, e):
                y_ok.slot(pe, t)
                for q in range(2):
                    hs_ok.done(pe, 2 * t + q)
                    for m in range(4 * q, 4 * q + 4):
                        for n, (pw, ph) in enumerate(passes):
                            last = nc.tensor.matmul(bank[6 + u][:, 0:D], hh[ph][:, u, m * P:(m + 1) * P], w2[pw][:, m, bass.ds(e * D, D)],
                                                    start=(m == 0 and n == 0), stop=(m == MC - 1 and n == 2))
                last.then_inc(y_ps.sem, 1)
            low_ok.done(pe, PIECES - 1)
            e = registers(nc, PE, route.expert[0:1, 0:2], E1 - 1)
            turn(0, 0)
            turn(0, 1)
            up(0, 0, e[0])
            with pe.Fori(0, T1 // 2) as i:
                e = registers(nc, PE, route.expert[0:1, bass.ds(i * 2, 3)], E1 - 1)
                for u in range(2):
                    turn(i + 1, u)
                    up(i * 2 + 1 + u, 1 - u, e[1 + u])
                    down(i * 2 + u, u, e[u])


def combine1(nc, a, k):
    with Stage(nc, "last") as s:
        ids = s.sb("rows", [P, 4, 2], I32)
        x, y = s.sb("x", [P, 4, D]), s.sb("y", [P, 4, 2, D])
        sent = [s.sem(f"x_loaded{u}") for u in range(4)]
        arrived = [s.sem(f"arrived{u}") for u in range(4)]
        ids_ok, begun, half, out_ok, stored, free = s.sem("ids_ready"), s.sem("gathers_begun"), s.sem("half"), Count(s, "out_ready", 4), s.sem("stored"), Count(s, "out_stored", 4)
        block = s.block()

        def size(t):
            return P if not isinstance(t, int) or t < NT - 1 else TAIL

        @block.gpsimd
        def _(pool):
            def gather(t, u):
                pool.wait_ge(ids_ok, t + 1)
                pool.sem_inc(begun, 1)
                m = size(t)
                for j in range(2):
                    nc.gpsimd.indirect_dma_start(y[0:m, u, j, :], None, k.ys1, bass.IndirectOffsetOnAxis(ids[0:m, u, j:j + 1], 0)).then_inc(arrived[u], 16)
            tiles(pool, NT, 4, gather)

        @block.scalar
        def _(act):
            def load(t, u):
                free.slot(act, t)
                act.dma_start(x[:, u, :], rows(k.x3, t * P, P)).then_inc(sent[u], 16)
            tiles(act, NT, 4, load)

        @block.sync
        def _(sp):
            free.start(sp)

            def save(t, u):
                out_ok.done(sp, t)
                m = size(t)
                sp.dma_start(rows(a["out"], t * P, m), x[0:m, u, :]).then_inc(stored, 16)
                sp.wait_ge(stored, (t + 1) * 16)
                sp.sem_inc(free.sem, 1)
            tiles(sp, NT, 4, save)

        @block.vector
        def _(v):
            out_ok.start(v)

            def address(t, u):
                for j in range(2):
                    last = nc.vector.tensor_copy(ids[:, u, j:j + 1], col(k.route1.place[j], t))
                last.then_inc(ids_ok, 1)

            def add(i, u):
                t = i * 4 + u
                m = size(t)
                v.wait_ge(arrived[u], (i + 1) * 32)
                v.wait_ge(sent[u], (i + 1) * 16)
                nc.vector.scalar_tensor_tensor(x[0:m, u, :], y[0:m, u, 0, :], col(k.share[0], t)[0:m], x[0:m, u, :], ALU.mult, ALU.add).then_inc(half, 1)
                v.wait_ge(half, t + 1)
                nc.vector.scalar_tensor_tensor(x[0:m, u, :], y[0:m, u, 1, :], col(k.share[1], t)[0:m], x[0:m, u, :], ALU.mult, ALU.add).then_inc(out_ok.sem, 1)
            for u in range(4):
                address(u, u)
            with v.Fori(0, NT // 4 - 1) as i:
                for u in range(4):
                    add(i, u)
                    address(i * 4 + 4 + u, u)
            for u in range(4):
                add(NT // 4 - 1, u)
            address(NT - 1, 0)
            add(NT // 4, 0)


def store(nc, a, k):
    with Stage(nc, "store") as s:
        st = s.sem("stored")
        block = s.block()

        @block.sync
        def _(sp):
            sp.dma_start(a["out"][0:(NT - 1) * P, :].rearrange("(t p) f -> p t f", p=P), k.x[:, 0:NT - 1, :]).then_inc(st, 16)
            sp.dma_start(a["out"][(NT - 1) * P:N, :], k.x[0:TAIL, NT - 1, :]).then_inc(st, 16)
            sp.wait_ge(st, 32)


class Kept:
    pass


def build(nc, a, stop=99):
    k = Kept()
    k.span_tab = nc.dram_tensor("span_tab", [2, C * NT], F32).ap()
    k.src_tab = nc.dram_tensor("src_tab", [NPAD * R, H0], F32).ap()
    k.dst_tab = nc.dram_tensor("dst_tab", [NPAD * R, H0], F32).ap()
    k.item_tab = nc.dram_tensor("item_tab", [3, -(-ITEMS // P) * P], F32).ap()
    k.h_tab = nc.dram_tensor("h_tab", [NPAD * R, D], F32).ap()
    k.xs0 = nc.dram_tensor("sorted0", [route_tiles(E0, 1) * P, D], F32).ap()
    k.ys0 = nc.dram_tensor("results0", [route_tiles(E0, 1) * P, D], F32).ap()
    k.xs1 = nc.dram_tensor("sorted1", [(T1 + 2) * P, D], F32).ap()
    k.ys1 = nc.dram_tensor("results1", [T1 * P, D], F32).ap()
    k.x3 = nc.dram_tensor("x3", [NPAD, D], F32).ap()
    k.g_tab = nc.dram_tensor("g_tab", [NPAD, D + 2 * H1], F32).ap()
    k.l_tab = nc.dram_tensor("l_tab", [NPAD, H1], F32).ap()
    k.sorted = [k.xs0, k.xs1]
    with Stage(nc, "all") as s:
        k.iota, k.ident, k.before, k.ones = (s.sb(n, [P, P]) for n in ("iota", "ident", "before", "ones"))
        k.col = s.sb("col", [P, 1])
        k.share = [s.sb(f"share{j}", [P, NT]) for j in range(2)]
        k.route1 = Route(nc, s, k, E1, 2, SPARE)
        with Stage(nc, "nodes") as n:
            k.x = n.sb("x", [P, NT, D])
            k.dst_i, k.src_i = n.sb("dst_i", [P, NT], I32), n.sb("src_i", [P, NT], I32)
            with Stage(nc, "gnn0") as g:
                k.edge_row = g.sb("edge_row", [P, NT * C], I32)
                k.dst_row = g.sb("dst_row", [P, NT * C], I32)
                k.dst_f = g.sb("dst_f", [P, NT * C])
                k.item_f = g.sb("item_f", [1, 2, ITEMS])
                k.item_base = g.sb("item_base", [P, ITEMS])
                k.w = g.sb("edge_w", [P, NPAD])
                with Stage(nc, "scores") as sc:
                    k.score = sc.sb("score", [P, NPAD])
                    with Stage(nc, "att") as w:
                        k.wT = w.sb("wT", [P, DC, R * D])
                        prepare(nc, a, k)
                        edge_scores(nc, a, k)
                    edge_weights(nc, a, k)
                aggregate(nc, a, k)
            if stop == 1:
                return store(nc, a, k)
            moe0(nc, a, k)
            if stop == 2:
                return store(nc, a, k)
            attend1(nc, a, k)
            if stop == 3:
                return store(nc, a, k)
            route1(nc, a, k)
        experts1(nc, a, k)
        combine1(nc, a, k)


_INS = ["x", "src", "dst", "edge_type_8", "L0_gnn_W", "L0_gnn_attn_src", "L0_gnn_attn_dst", "L0_ffn_router_w",
        "L0_ffn_router_b", "L0_ffn_W1", "L0_ffn_b1", "L0_ffn_W2", "L0_ffn_b2", "L1_gnn_weight", "L1_gnn_attn_l",
        "L1_gnn_attn_r", "L1_ffn_Wr", "L1_ffn_br", "L1_ffn_ln_g", "L1_ffn_ln_b", "L1_ffn_W1", "L1_ffn_b1",
        "L1_ffn_W2", "L1_ffn_b2"]


def kernel(**inputs):
    import numpy as _np
    import concourse.bacc as _bacc
    from concourse import mybir as _mybir
    from concourse.bass_utils import run_bass_kernel_spmd as _run

    nc = _bacc.Bacc("TRN2", target_bir_lowering=False, num_devices=1)
    arrays, aps = {}, {}
    for name in _INS:
        array = _np.ascontiguousarray(inputs[name])
        arrays[f"in_{name}_dram"] = array
        aps[name] = nc.dram_tensor(f"in_{name}_dram", array.shape, _mybir.dt.from_np(array.dtype), kind="ExternalInput").ap()
    aps["out"] = nc.dram_tensor("out_0_dram", (N, D), F32, kind="ExternalOutput").ap()
    build(nc, aps)
    r = _run(nc, [arrays], core_ids=[0])
    return r.results[0]["out_0_dram"]
```

```python
import concourse.bass as bass
from concourse import mybir
from contextlib import ExitStack

F32 = mybir.dt.float32
I32 = mybir.dt.int32
F16 = mybir.dt.float16
BF16 = mybir.dt.bfloat16
ALU = mybir.AluOpType
ACT = mybir.ActivationFunctionType
AX = mybir.AxisListType

P = 128
N = 6250
D = 256
DC = D // P
NT = -(-N // P)
TAIL = N - (NT - 1) * P
NPAD = NT * P
E = 100000
C = 16
CE = E // C
R, H0, HD0 = 8, 8, 32
H1, HD1 = 4, 64
E0, F0 = 32, 64
E1, F1 = 8, 1024
EPS = 1e-5
ITEMS = 832
U = 8
UG = 17
BATCH = [0, 5, 9, 13, 17]
BM = 5
ITEMS_MAX = NT * UG + BATCH[2]
assert CE == N and ITEMS_MAX >= ITEMS >= C * NT + NT - 1 and ITEMS % U == 0


class Chain:

    def __init__(self, eng, sem):
        self.eng, self.sem, self.n = eng, sem, 0

    def link(self, ins):
        ins.then_inc(self.sem, 1)
        self.n = self.n + 1
        self.eng.wait_ge(self.sem, self.n)


class Count:

    def __init__(self, stage, name, ahead):
        self.sem, self.ahead = stage.sem(name), ahead

    def start(self, eng):
        eng.sem_inc(self.sem, self.ahead)

    def done(self, eng, t):
        eng.wait_ge(self.sem, t + 1 + self.ahead)

    def slot(self, eng, t):
        eng.wait_ge(self.sem, t + 1)


class Landed:

    def __init__(self, stage, name, slots, dmas=1):
        self.sems, self.step = [stage.sem(f"{name}{u}") for u in range(slots)], 16 * dmas

    def start(self, eng):
        for sem in self.sems:
            eng.sem_inc(sem, self.step)

    def slot(self, eng, i, u):
        eng.wait_ge(self.sems[u], (i + 1) * self.step)

    def all(self, eng, n):
        for u, sem in enumerate(self.sems):
            eng.wait_ge(sem, ((n - u + len(self.sems) - 1) // len(self.sems) + 1) * self.step)


class Stage:

    def __init__(self, nc, name):
        self.nc, self.name, self.ctx, self.sems = nc, name, ExitStack(), []

    def __enter__(self):
        return self

    def __exit__(self, *a):
        self.ctx.close()
        if self.sems:
            self.nc.clear_and_free_semaphores(self.sems)
            self.nc.all_engine_barrier()

    def sb(self, name, shape, dt=F32):
        return self.ctx.enter_context(self.nc.sbuf_tensor(f"{self.name}_{name}", shape, dt))

    def banks(self, n=8):
        return [self.ctx.enter_context(self.nc.psum_tensor(f"{self.name}_bank{i}", [P, 512], F32)) for i in range(n)]

    def sem(self, name):
        self.sems.append(self.nc.alloc_semaphore(f"{self.name}_{name}"))
        return self.sems[-1]

    def block(self):
        return self.ctx.enter_context(self.nc.Block())


def col(ap, start, size=1):
    out = ap[:, start:start + size] if isinstance(start, int) else ap[:, bass.ds(start, size)]
    if size == 1 and len(ap.shape) > 2:
        names = " ".join("abcd"[: len(ap.shape) - 2])
        out = out.rearrange(f"p o {names} -> p (o {names})")
    return out


def flat(ap):
    names = " ".join("abcd"[: len(ap.shape) - 1])
    return ap.rearrange(f"p {names} -> p ({names})")


def rows(ap, start, size):
    return ap[start:start + size, :] if isinstance(start, int) else ap[bass.ds(start, size), :]


def tiles(eng, n, unroll, body, base=0):
    with eng.Fori(0, n // unroll) as i:
        for u in range(unroll):
            body(i * unroll + u, u)
    for t in range(n - n % unroll, n):
        body(t, t % unroll)


def turns(eng, n, unroll, body):
    with eng.Fori(0, n // unroll) as i:
        for u in range(unroll):
            body(i, u)
    for u in range(n % unroll):
        body(n // unroll, u)


def rounds(eng, n, unroll, body):
    for u in range(unroll):
        body(0, u)
    with eng.Fori(1, n // unroll) as i:
        for u in range(unroll):
            body(i, u)
    for u in range(n % unroll):
        body(n // unroll, u)


class Norm:

    def __init__(self, nc, s, k, banks):
        self.nc, self.k, self.banks = nc, k, banks
        self.st6 = s.sb("stats", [P, NT, 6])
        self.mean, self.rstd = s.sb("mean", [P, NT]), s.sb("rstd", [P, NT])
        self.tmp, self.var, self.sd = (s.sb(n, [P, NT]) for n in ("tmp", "var", "sd"))
        self.xn = s.sb("xn", [P, 2, D])
        self.xT = s.sb("xnT", [P, 2, D])
        self.dve = s.sem("dve")
        self.var_ok, self.sd_ok = s.sem("var_ready"), s.sem("sd_ready")
        self.xn_ok = Count(s, "xn_ready", 2)
        self.t_ps = Count(s, "xnT_in_psum", 2)
        self.t_ok = Count(s, "xnT_ready", 2)

    def statistics(self, v, ch):
        nc, c0 = self.nc, ch.n

        def one(t, u):
            nc.vector.bn_stats(col(self.st6, t), col(self.k.x, t)).then_inc(self.dve, 1)
        tiles(v, NT, 7, one)
        ch.n = c0 + NT
        v.wait_ge(self.dve, ch.n)
        me, ve, mo, vo = (self.st6[:, :, i] for i in (1, 2, 4, 5))
        tmp, var, mean = self.tmp[:, :], self.var[:, :], self.mean[:, :]
        moments(nc, ch, me, ve, mo, vo, mean, var, tmp)
        v.sem_inc(self.var_ok, 1)
        v.wait_ge(self.sd_ok, 1)
        rsqrt_newton(nc, ch, self.rstd[:, :], tmp, var, self.sd[:, :])
        self.xn_ok.start(v)

    def root(self, act):
        act.wait_ge(self.var_ok, 1)
        self.nc.scalar.activation(self.sd[:, :], self.var[:, :], ACT.Sqrt).then_inc(self.sd_ok, 1)
        self.t_ok.start(act)

    def normalise(self, v, t, u):
        self.t_ps.slot(v, t)
        self.nc.vector.tensor_scalar(self.xn[:, u, :], col(self.k.x, t), col(self.mean, t), col(self.rstd, t),
                                     ALU.subtract, ALU.mult).then_inc(self.xn_ok.sem, 1)

    def transpose(self, pe, t, u):
        self.xn_ok.done(pe, t)
        self.t_ok.slot(pe, t)
        for c in range(DC):
            last = self.nc.tensor.transpose(self.banks[u][:, c * P:(c + 1) * P], self.xn[:, u, c * P:(c + 1) * P], self.k.ident[:, :])
        last.then_inc(self.t_ps.sem, 1)

    def keep(self, act, t, u, used):
        self.t_ps.done(act, t)
        used.slot(act, t)
        self.nc.scalar.activation(self.xT[:, u, :], self.banks[u][:, 0:D], ACT.Copy).then_inc(self.t_ok.sem, 1)


def moments(nc, ch, me, ve, mo, vo, mean, var, tmp):
    ch.link(nc.vector.tensor_tensor(tmp, me, mo, ALU.add))
    ch.link(nc.vector.tensor_scalar(mean, tmp, 0.5, None, ALU.mult))
    ch.link(nc.vector.tensor_tensor(tmp, me, mo, ALU.subtract))
    ch.link(nc.vector.tensor_tensor(tmp, tmp, tmp, ALU.mult))
    ch.link(nc.vector.tensor_scalar(tmp, tmp, 0.25, EPS, ALU.mult, ALU.add))
    ch.link(nc.vector.tensor_tensor(var, ve, vo, ALU.add))
    ch.link(nc.vector.scalar_tensor_tensor(var, var, 1.0 / D, tmp, ALU.mult, ALU.add))


def rsqrt_newton(nc, ch, out, tmp, var, sd):
    ch.link(nc.vector.reciprocal(out, sd))
    ch.link(nc.vector.tensor_tensor(tmp, out, out, ALU.mult))
    ch.link(nc.vector.tensor_tensor(tmp, tmp, var, ALU.mult))
    ch.link(nc.vector.tensor_scalar(tmp, tmp, -0.5, 1.5, ALU.mult, ALU.add))
    ch.link(nc.vector.tensor_tensor(out, out, tmp, ALU.mult))


def prepare(nc, a, k):
    with Stage(nc, "prep") as s:
        names = ("src", "dst", "edge_type_8")
        ints = [s.sb(f"{n}_i", [NT, C, P], I32) for n in names]
        floats = [k.score[0:NT, j * C * P:(j + 1) * C * P].rearrange("g (c p) -> g c p", c=C) for j in range(3)]
        idx = k.w[:, 0:3 * NT * C].rearrange("p (j q) -> p j q", j=3)
        iota_i, col_i = s.sb("iota_i", [P, P], I32), s.sb("col_i", [P, 1], I32)
        wn = s.sb("w_natural", [P, R, DC, D])
        ablk = s.sb("attn_blocks", [P, DC, 2 * H0])
        vst = s.sb("score_weights", [P, DC, 2 * R * H0])
        scores = s.sb("scores", [P, 2, R * H0])
        first = s.sb("first_last", [NT, 2, C])
        first_i = s.sb("first_last_i", [NT, 2, C], I32)
        bank = s.banks()
        norm = Norm(nc, s, k, bank[0:2])
        rel_i = s.sb("relation_i", [P, R, H0], I32)
        cleared, loaded, edges, weights = (s.sem(n) for n in ("cleared", "x_loaded", "edges_loaded", "weights_loaded"))
        iotas, consts, edges_f = s.sem("iotas"), s.sem("consts"), s.sem("edges_as_floats")
        wt_ps, wt_free, v_ps, v_ok = (s.sem(n) for n in ("wT_in_psum", "wT_bank_free", "v_in_psum", "v_ready"))
        e_ps, e_free = s.sem("edges_in_psum"), s.sem("edges_bank_free")
        sc_ps, sc_ok, stored = Count(s, "scores_in_psum", 2), Count(s, "scores_ready", 2), Landed(s, "scores_stored", 2)
        spans, spans_st = s.sem("spans_ready"), s.sem("spans_written")
        block = s.block()

        @block.gpsimd
        def _(pool):
            nc.gpsimd.memset(k.x[:, NT - 1, :], 0.0).then_inc(cleared, 1)
            nc.gpsimd.memset(ablk[:, :, :], 0.0).then_inc(cleared, 1)
            for t in ints:
                nc.gpsimd.memset(t[:, :, :], 0).then_inc(cleared, 1)
            nc.gpsimd.iota(iota_i[:, :], [[1, P]], base=0, channel_multiplier=0).then_inc(iotas, 1)
            nc.gpsimd.iota(col_i[:, :], [[0, 1]], base=0, channel_multiplier=1).then_inc(iotas, 1)
            nc.gpsimd.iota(rel_i[:, :, :], [[1, R], [0, H0]], base=0, channel_multiplier=0).then_inc(iotas, 1)

        @block.sync
        def _(sp):
            sp.wait_ge(cleared, 5)
            for t, name in zip(ints, names):
                e = a[name].rearrange("(c e) -> c e", c=C)
                sp.dma_start(t[0:NT - 1, :, :], e[:, 0:(NT - 1) * P].rearrange("c (g p) -> g c p", p=P)).then_inc(edges, 16)
                sp.dma_start(t[NT - 1:NT, :, 0:TAIL], e[:, (NT - 1) * P:].rearrange("c (o p) -> o c p", o=1)).then_inc(edges, 16)
            sp.dma_start(wn[:, :, :, :], a["L0_gnn_W"].rearrange("r (c p) f -> p r c f", p=P)).then_inc(weights, 16)
            with nc.allow_non_contiguous_dma(reason="short vectors onto partitions"):
                for j, name in enumerate(("L0_gnn_attn_src", "L0_gnn_attn_dst")):
                    for h in range(H0):
                        p0 = h * HD0 % P
                        sp.dma_start(ablk[p0:p0 + HD0, h * HD0 // P, j * H0 + h:j * H0 + h + 1],
                                     a[name][h:h + 1, :].rearrange("a b -> b a")).then_inc(weights, 16)
                sp.wait_ge(spans, 1)
                for j in range(2):
                    sp.dma_start(k.span_tab[j:j + 1, :].rearrange("o (c g) -> (o g) c", c=C), first[:, j, :]).then_inc(spans_st, 16)
            stored.start(sp)

            def store(t, u):
                sc_ok.done(sp, t)
                sp.dma_start(rows(k.src_tab.rearrange("(n r) h -> n (r h)", r=R), t * P, P), scores[:, u, :]).then_inc(stored.sems[u], 16)
            tiles(sp, NT, 2, store)
            stored.all(sp, NT)
            sp.wait_ge(spans_st, 32)

        @block.scalar
        def _(act):
            act.wait_ge(cleared, 1)
            act.dma_start(k.x[:, 0:NT - 1, :], a["x"][0:(NT - 1) * P, :].rearrange("(t p) f -> p t f", p=P)).then_inc(loaded, 16)
            act.dma_start(k.x[0:TAIL, NT - 1, :], a["x"][(NT - 1) * P:N, :]).then_inc(loaded, 16)
            norm.root(act)
            tiles(act, NT, 2, lambda t, u: norm.keep(act, t, u, sc_ps))

        @block.vector
        def _(v):
            ch = Chain(v, norm.dve)
            v.wait_ge(iotas, 3)
            ch.link(nc.vector.tensor_copy(k.relation[:, :], rel_i[:, :, :].rearrange("p r h -> p (r h)")))
            ch.link(nc.vector.tensor_copy(k.iota[:, :], iota_i[:, :]))
            ch.link(nc.vector.tensor_copy(k.col[:, :], col_i[:, :]))
            ch.link(nc.vector.memset(k.ones[:, :], 1.0))
            ch.link(nc.vector.tensor_scalar(k.ident[:, :], k.iota[:, :], k.col[:, 0:1], None, ALU.is_equal))
            ch.link(nc.vector.tensor_scalar(k.before[:, :], k.iota[:, :], k.col[:, 0:1], None, ALU.is_gt))
            v.sem_inc(consts, 1)
            v.wait_ge(edges, 96)
            for t, f in zip(ints, floats):
                ch.link(nc.vector.tensor_copy(f[:, :, :], t[:, :, :]))
            v.sem_inc(edges_f, 1)
            ch.link(nc.vector.tensor_copy(first[:, 0, :], floats[1][:, :, 0]))
            ch.link(nc.vector.reduce_max(first[:, 1, :], floats[1][:, :, :], AX.X))
            ch.link(nc.vector.tensor_copy(first_i[:, :, :], first[:, :, :]))
            ch.link(nc.vector.tensor_scalar(first_i[:, :, :], first_i[:, :, :], 7, None, ALU.arith_shift_right))
            nc.vector.tensor_copy(first[:, :, :], first_i[:, :, :]).then_inc(spans, 1)
            for n in range(6):
                j, half = divmod(n, 2)
                v.wait_ge(e_ps, n + 1)
                nc.vector.tensor_copy(idx[:, j, :].rearrange("p (g c) -> p g c", c=C)[:, :, half * 8:half * 8 + 8],
                                      bank[n % 4][:, 0:8 * NT].rearrange("p (c g) -> p g c", c=8)).then_inc(e_free, 1)
            v.wait_ge(e_free, 6)
            nc.vector.scalar_tensor_tensor(k.edge_row[:, :], idx[:, 0, :], float(R), idx[:, 2, :], ALU.mult, ALU.add)
            nc.vector.tensor_copy(k.type_f[:, :], idx[:, 2, :])
            nc.vector.tensor_copy(k.dst_f[:, :], idx[:, 1, :])
            nc.vector.tensor_copy(k.dst_i[:, :], idx[:, 1, :].rearrange("p (g c) -> p g c", c=C)[:, :, 0])
            nc.vector.tensor_copy(k.src_i[:, :], idx[:, 0, :].rearrange("p (g c) -> p g c", c=C)[:, :, 0])
            for r in range(R):
                v.wait_ge(wt_ps, r + 1)
                nc.vector.tensor_copy(k.wT[:, :, r * D:(r + 1) * D], bank[r % 4][:, :].rearrange("p (c o) -> p c o", c=DC)).then_inc(wt_free, 1)
            v.wait_ge(v_ps, 1)
            got = bank[4][:, 0:DC * R * 2 * H0].rearrange("p (c r j h) -> p c r j h", c=DC, r=R, j=2)
            for c in range(DC):
                for j in range(2):
                    nc.vector.tensor_copy(vst[:, c, j * R * H0:(j + 1) * R * H0].rearrange("p (r h) -> p r h", r=R), got[:, c, :, j, :]).then_inc(v_ok, 1)
            v.wait_ge(loaded, 32)
            norm.statistics(v, ch)
            sc_ok.start(v)

            def evacuate(i, u):
                sc_ps.done(v, i * 2 + u)
                stored.slot(v, i, u)
                nc.vector.tensor_copy(scores[:, u, :], bank[2 + u][:, 0:R * H0])
                nc.vector.tensor_copy(col(k.dst_half, i * 2 + u), bank[2 + u][:, R * H0:2 * R * H0]).then_inc(sc_ok.sem, 1)

            norm.normalise(v, 0, 0)
            with v.Fori(0, (NT - 1) // 2) as i:
                for u in range(2):
                    norm.normalise(v, i * 2 + u + 1, 1 - u)
                    evacuate(i, u)
            evacuate(NT // 2, 0)

        @block.tensor
        def _(pe):
            pe.wait_ge(consts, 1)
            pe.wait_ge(edges_f, 1)
            for n in range(6):
                j, half = divmod(n, 2)
                if n >= 4:
                    pe.wait_ge(e_free, n - 3)
                for c in range(8):
                    last = nc.tensor.transpose(bank[n % 4][:, c * NT:(c + 1) * NT], floats[j][:, half * 8 + c, :], k.ident[0:NT, 0:NT])
                last.then_inc(e_ps, 1)
            pe.wait_ge(weights, 16 * 17)
            pe.wait_ge(e_free, 6)
            for r in range(R):
                if r >= 4:
                    pe.wait_ge(wt_free, r - 3)
                for fc in range(DC):
                    for oc in range(DC):
                        last = nc.tensor.transpose(bank[r % 4][:, fc * D + oc * P:fc * D + (oc + 1) * P],
                                                   wn[:, r, oc, fc * P:(fc + 1) * P], k.ident[:, :])
                last.then_inc(wt_ps, 1)
            for fc in range(DC):
                for r in range(R):
                    o = (fc * R + r) * 2 * H0
                    for oc in range(DC):
                        last = nc.tensor.matmul(bank[4][:, o:o + 2 * H0], wn[:, r, oc, fc * P:(fc + 1) * P], ablk[:, oc, :],
                                                start=(oc == 0), stop=(oc == DC - 1))
            last.then_inc(v_ps, 1)
            pe.wait_ge(v_ok, 4)
            pe.wait_ge(wt_free, R)
            norm.t_ps.start(pe)
            sc_ps.start(pe)

            def body(t, u):
                norm.transpose(pe, t, u)
                norm.t_ok.done(pe, t)
                sc_ok.slot(pe, t)
                for c in range(DC):
                    last = nc.tensor.matmul(bank[2 + u][:, 0:P], norm.xT[:, u, c * P:(c + 1) * P], vst[:, c, :],
                                            start=(c == 0), stop=(c == DC - 1))
                last.then_inc(sc_ps.sem, 1)
            tiles(pe, NT, 2, body)
        k.norm0 = None


def list_items(nc, a, k):
    with Stage(nc, "items") as s:
        Q = C * NT
        IC = -(-ITEMS_MAX // P)
        span = s.sb("span", [P, 2, Q])
        n_of, before, junk = s.sb("blocks_of_tile", [P, Q]), s.sb("items_before", [P, Q]), s.sb("junk", [P, Q])
        place_i, q_i, item_i = s.sb("place_i", [P, Q], I32), s.sb("tile_i", [P, Q], I32), s.sb("item_i", [P, IC], I32)
        place, q_f, item = s.sb("place", [P, Q]), s.sb("tile_f", [P, Q]), s.sb("item", [P, IC])
        zero, zero_ok, zeroed = s.sb("zero", [P, D]), s.sem("zero_ready"), s.sem("zeroed")
        got = s.sb("got", [P, 4, IC])
        res = s.sb("result", [P, 3, IC])
        item_f = s.sb("item_f", [1, 2, ITEMS_MAX])
        loaded, iotas, dve, done, st = (s.sem(n) for n in ("span_loaded", "iotas", "dve", "result_ready", "tables_moved"))
        block = s.block()

        @block.gpsimd
        def _(pool):
            nc.gpsimd.memset(zero[:, :], 0.0).then_inc(zero_ok, 1)
            nc.gpsimd.memset(k.w[:, :], 0.0)
            nc.gpsimd.iota(place_i[:, :], [[1, C], [C, NT]], base=0, channel_multiplier=0).then_inc(iotas, 1)
            nc.gpsimd.iota(q_i[:, :], [[1, Q]], base=0, channel_multiplier=0).then_inc(iotas, 1)
            nc.gpsimd.iota(item_i[:, :], [[P, IC]], base=0, channel_multiplier=1).then_inc(iotas, 1)

        @block.sync
        def _(sp):
            sp.wait_ge(zero_ok, 1)
            for tab in k.sorted:
                sp.dma_start(tab.rearrange("(t p) f -> p t f", p=P), zero[:, :].rearrange("p (o f) -> p o f", o=1).broadcast_to([P, tab.shape[0] // P, D])).then_inc(zeroed, 16)
            sp.dma_start(span[:, :, :], k.span_tab.rearrange("(o j) q -> o j q", o=1).broadcast_to([P, 2, Q])).then_inc(loaded, 16)
            with nc.allow_non_contiguous_dma(reason="item tables, a few words of each partition"):
                sp.wait_ge(done, 1)
                sp.dma_start(k.item_tab.rearrange("j (c p) -> p j c", p=P), res[:, :, :]).then_inc(st, 16)
            sp.wait_ge(st, 16)
            sp.dma_start(item_f[:, :, :], k.item_tab.rearrange("(o j) c -> o j c", o=1)[:, 0:2, 0:ITEMS_MAX]).then_inc(st, 16)
            sp.dma_start(k.item_base[:, :], k.item_tab[2:3, 0:ITEMS_MAX].broadcast_to([P, ITEMS_MAX])).then_inc(st, 16)
            sp.wait_ge(st, 48)
            sp.wait_ge(zeroed, 16 * len(k.sorted))

        @block.vector
        def _(v):
            ch = Chain(v, dve)
            v.wait_ge(loaded, 16)
            v.wait_ge(iotas, 3)
            for o, i in ((place, place_i), (q_f, q_i), (item, item_i)):
                ch.link(nc.vector.tensor_copy(o[:, :], i[:, :]))
            ch.link(nc.vector.tensor_tensor(n_of[:, :], span[:, 1, :], span[:, 0, :], ALU.subtract))
            ch.link(nc.vector.tensor_scalar(n_of[:, :], n_of[:, :], 1.0, None, ALU.add))
            ch.link(nc.vector.tensor_tensor_scan(before[:, :], n_of[:, :], n_of[:, :], 0.0, ALU.add, ALU.bypass))
            ch.link(nc.vector.tensor_tensor(before[:, :], before[:, :], n_of[:, :], ALU.subtract))
            for c in range(IC):
                ch.link(nc.vector.tensor_scalar(junk[:, :], before[:, :], item[:, c:c + 1], -1.0, ALU.is_le, ALU.add, accum_out=got[:, 0, c:c + 1]))
                for j, t in ((1, before), (2, span[:, 0, :]), (3, place)):
                    ch.link(nc.vector.scalar_tensor_tensor(junk[:, :], q_f[:, :], got[:, 0, c:c + 1], t[:, :] if j != 2 else t, ALU.is_equal, ALU.mult,
                                                           accum_out=got[:, j, c:c + 1]))
            ch.link(nc.vector.tensor_tensor(got[:, 0, :], item[:, :], got[:, 1, :], ALU.subtract))
            ch.link(nc.vector.tensor_tensor(got[:, 0, :], got[:, 0, :], got[:, 2, :], ALU.add))
            ch.link(nc.vector.tensor_copy(res[:, 0, :], got[:, 3, :]))
            ch.link(nc.vector.tensor_scalar(res[:, 1, :], got[:, 0, :], float(NT - 1), None, ALU.min))
            ch.link(nc.vector.tensor_scalar(res[:, 2, :], got[:, 0, :], float(P), None, ALU.mult))
            v.sem_inc(done, 1)
            v.wait_ge(st, 48)
            ch.link(nc.vector.tensor_copy(k.item_i[:, :, :], item_f[:, :, :]))


def edge_scores(nc, a, k):
    with Stage(nc, "score") as s:
        bank = s.banks(6)
        turn_ps = [s.ctx.enter_context(nc.psum_tensor(f"score_turned{j}", [P, 8, P], BF16)) for j in range(2)]
        norm = Norm(nc, s, k, bank[0:2])
        hb = s.sb("h_rows", [P, 2, R * D])
        ids = s.sb("rows", [P, 2, C], I32)
        half = s.sb("halves", [P, 2, C * H0])
        hot, hotT = s.sb("one_hot", [P, 2, BM, P], BF16), s.sb("one_hot_T", [P, 2, BM, P])
        ident = s.sb("ident_bf16", [P, P], BF16)
        kept_r, part = s.sb("kept_relation", [P, BM, R * H0]), s.sb("dst_part", [P, BM, H0])
        products = Count(s, "h_tile_in_psum", 2)
        h_ps, h_ok, stored = s.sem("h_bank_full"), s.sem("h_bank_empty"), Landed(s, "h_rows_stored", 2)
        ids_ok, begun = s.sem("rows_ready"), s.sem("gathers_begun")
        gathered = [s.sem(f"halves_gathered{u}") for u in range(2)]
        hot_ok, turned, hotT_ok, picked, selected = (Count(s, n, 2) for n in (
            "one_hot_ready", "one_hot_turned", "one_hot_T_ready", "dst_half_in_psum", "relation_kept"))
        part_ok, ident_ok = s.sem("parts_ready"), s.sem("ident_ready")
        STEPS = UG + 1
        added = Count(s, "added", 2 * STEPS)
        leaky, full, kept = s.sem("leaky_done"), s.sem("scores_turned"), s.sem("scores_kept")
        block = s.block()
        GROUPS = -(-NT // 4)

        @block.gpsimd
        def _(pool):
            def body(t, u):
                pool.wait_ge(added.sem, (t + 1) * STEPS)
                nc.gpsimd.tensor_copy(ids[:, u, :], col(k.edge_row, t * C, C)).then_inc(ids_ok, 1)
                pool.wait_ge(ids_ok, t + 1)
                pool.sem_inc(begun, 1)
                for c in range(C):
                    nc.gpsimd.indirect_dma_start(half[:, u, c * H0:(c + 1) * H0], None, k.src_tab,
                                                 bass.IndirectOffsetOnAxis(ids[:, u, c:c + 1], 0)).then_inc(gathered[u], 16)
            tiles(pool, NT, 2, body)

        @block.vector
        def _(v):
            ch = Chain(v, norm.dve)
            for n in (hot_ok, selected, added):
                n.start(v)
            ch.link(nc.vector.tensor_copy(ident[:, :], k.ident[:, :]))
            v.sem_inc(ident_ok, 1)
            norm.statistics(v, ch)

            def tiles_of(t, b0, b1):
                edge = lambda b: b // 4 * UG + BATCH[b % 4]
                o, m = t * UG + edge(b0), edge(b1) - edge(b0)
                return registers(nc, mybir.EngineType.DVE, k.item_i[0:1, 0, o:o + m] if isinstance(o, int) else k.item_i[0:1, 0, bass.ds(o, m)], NT * C - 1)

            def one_hot(t, j, w, z):
                return nc.vector.tensor_scalar(hot[:, j % 2, w, :], k.iota[:, :], col(k.item_base, t * UG + BATCH[j] + w), col(k.dst_f, z),
                                               ALU.add, ALU.is_equal)

            def items(t):
                for j in range(4):
                    m = BATCH[j + 1] - BATCH[j]
                    tn, jn = (t, j + 2) if j < 2 else (t + 1, j - 2)
                    mn = BATCH[jn + 1] - BATCH[jn]
                    z = tiles_of(t, j, j + 3)
                    picked.done(v, t * 4 + j)
                    for w in range(m):
                        o = w * R * H0
                        last = nc.vector.scalar_tensor_tensor(kept_r[:, w, :], k.relation[:, :], col(k.type_f, z[w]),
                                                              bank[4 + j % 2][:, o:o + R * H0], ALU.is_equal, ALU.mult)
                    last.then_inc(selected.sem, 1)
                    turned.slot(v, tn * 4 + jn)
                    hots = [one_hot(tn, jn, 0, z[len(z) - mn])]
                    selected.done(v, t * 4 + j)
                    added.slot(v, t * STEPS + BATCH[j] + 2 * STEPS - 1)
                    nc.vector.reduce_sum(part[:, 0:m, :], kept_r[:, 0:m, :].rearrange("p u (r h) -> p u h r", h=H0), AX.X).then_inc(part_ok, 1)
                    for w in range(max(m, mn)):
                        if 0 < w < mn:
                            hots.append(one_hot(tn, jn, w, z[len(z) - mn + w]))
                            if w == mn - 1:
                                hots[-1].then_inc(hot_ok.sem, 1)
                        if w == 0:
                            v.wait_ge(part_ok, t * 4 + j + 1)
                        if w < m:
                            added.slot(v, t * STEPS + BATCH[j] + w + 2 * STEPS - 1)
                            to = k.w[:, bass.ds(z[w] * H0, H0)]
                            nc.vector.tensor_tensor(to, to, part[:, w, :], ALU.add).then_inc(added.sem, 1)

            def source(i, u):
                t = i * 2 + u
                v.wait_ge(gathered[u], (i + 1) * C * 16)
                added.slot(v, t * STEPS + UG + 2 * STEPS - 1)
                w = col(k.w, t * P, P)
                nc.vector.tensor_tensor(w, w, half[:, u, :], ALU.add).then_inc(added.sem, 1)

            norm.normalise(v, 0, 0)
            for j in range(2):
                z = tiles_of(0, j, j + 1)
                for w in range(len(z)):
                    last = one_hot(0, j, w, z[w])
                last.then_inc(hot_ok.sem, 1)
            with v.Fori(0, (NT - 1) // 2) as i:
                for u in range(2):
                    norm.normalise(v, i * 2 + u + 1, 1 - u)
                    items(i * 2 + u)
                    source(i, u)
            items(NT - 1)
            source((NT - 1) // 2, 0)
            added.slot(v, NT * STEPS + 2 * STEPS - 1)
            for n in range(GROUPS):
                c0, c1 = n * 4 * P, min((n + 1) * 4, NT) * P
                nc.vector.scalar_tensor_tensor(k.w[:, c0:c1], k.w[:, c0:c1], 0.2, k.w[:, c0:c1], ALU.mult, ALU.max).then_inc(leaky, 1)

        @block.tensor
        def _(pe):
            for n in (norm.t_ps, products, turned, picked):
                n.start(pe)
            pe.sem_inc(h_ps, 2)
            pe.wait_ge(ident_ok, 1)

            def body(t, u):
                norm.transpose(pe, t, u)
                o = t * UG
                b = registers(nc, mybir.EngineType.PE, k.item_i[0:1, 1, o:o + UG] if isinstance(o, int) else k.item_i[0:1, 1, bass.ds(o, UG)], NT - 1)
                norm.t_ok.done(pe, t)
                for j in range(4):
                    n = t * 4 + j
                    hot_ok.done(pe, n)
                    hotT_ok.slot(pe, n)
                    for w in range(BATCH[j + 1] - BATCH[j]):
                        last = nc.tensor.transpose(turn_ps[j % 2][:, w, :], hot[:, j % 2, w, :], ident[:, :])
                    last.then_inc(turned.sem, 1)
                    pe.wait_ge(h_ok, n + 1)
                    for c in range(DC):
                        last = nc.tensor.matmul(bank[2 + j % 2][:, :], norm.xT[:, u, c * P:(c + 1) * P], k.wT[:, c, j * 512:(j + 1) * 512],
                                                start=(c == 0), stop=(c == DC - 1))
                    last.then_inc(h_ps, 1)
                    hotT_ok.done(pe, n)
                    selected.slot(pe, n)
                    for w in range(BATCH[j], BATCH[j + 1]):
                        o = (w - BATCH[j]) * R * H0
                        last = nc.tensor.matmul(bank[4 + j % 2][:, o:o + R * H0], hotT[:, j % 2, w - BATCH[j], :], col(k.dst_half, b[w]), start=True, stop=True)
                    last.then_inc(picked.sem, 1)
                pe.sem_inc(products.sem, 1)
            tiles(pe, NT, 2, body)
            pe.wait_ge(h_ok, 2 + 4 * NT)
            for n in range(GROUPS):
                pe.wait_ge(leaky, n + 1)
                if n >= 4:
                    pe.wait_ge(kept, n - 3)
                for t in range(4 * n, min(4 * n + 4, NT)):
                    last = nc.tensor.transpose(bank[n % 4][:, t % 4 * P:(t % 4 + 1) * P], k.w[:, t * P:(t + 1) * P], k.ident[:, :])
                last.then_inc(full, 1)

        @block.scalar
        def _(act):
            norm.root(act)
            act.sem_inc(h_ok, 2)
            hotT_ok.start(act)

            def body(i, u):
                t = i * 2 + u
                norm.keep(act, t, u, products)
                stored.slot(act, i, u)
                for j in range(4):
                    n, m = t * 4 + j, BATCH[j + 1] - BATCH[j]
                    turned.done(act, n)
                    picked.slot(act, n)
                    nc.scalar.activation(hotT[:, j % 2, 0:m, :], turn_ps[j % 2][:, 0:m, :], ACT.Copy).then_inc(hotT_ok.sem, 1)
                    act.wait_ge(h_ps, 2 + n + 1)
                    nc.scalar.activation(hb[:, u, j * 512:(j + 1) * 512], bank[2 + j % 2][:, :], ACT.Copy).then_inc(h_ok, 1)
            turns(act, NT, 2, body)
            for n in range(GROUPS):
                act.wait_ge(full, n + 1)
                m = min(4, NT - 4 * n) * P
                nc.scalar.activation(k.score[:, 4 * n * P:4 * n * P + m], bank[n % 4][:, 0:m], ACT.Copy).then_inc(kept, 1)

        @block.sync
        def _(sp):
            stored.start(sp)

            def body(t, u):
                sp.wait_ge(h_ok, 2 + 4 * t + 4)
                sp.dma_start(rows(k.h_tab.rearrange("(n r) o -> n (r o)", r=R), t * P, P), hb[:, u, :]).then_inc(stored.sems[u], 16)
            tiles(sp, NT, 2, body)
            stored.all(sp, NT)


def edge_weights(nc, a, k):
    with Stage(nc, "weight") as s:
        bank = s.banks()
        d = s.sb("dst", [P, CE], I32)
        same = s.sb("same", [P, CE + 1])
        seg = s.sb("segment_max", [P, CE])
        ends = s.sb("ends", [P, 4])
        row = s.sb("rows", [1, 4, H0 * C])
        link, one, nxt, g, fc, bc = (s.sb(n, [1, H0, C]) for n in ("link", "one", "next", "gate", "forward", "backward"))
        carry = s.sb("carry", [1, 2, C * H0])
        carry_c = s.sb("carry_col", [P, 2])
        loaded, dve, ends_ps, ends_ok, carry_ok, carry_ps = (s.sem(n) for n in ("dst_loaded", "dve", "ends_in_psum", "ends_ready", "carry_ready", "carry_in_psum"))
        diff_ok, exp_ok, w_ps, w_ok, cleared = (s.sem(n) for n in ("diff_ready", "exp_ready", "w_in_psum", "w_ready", "cleared"))
        block = s.block()

        @block.sync
        def _(sp):
            for c in range(C):
                sp.dma_start(d[c * H0:(c + 1) * H0, :], a["dst"][c * CE:(c + 1) * CE].rearrange("(o e) -> o e", o=1).broadcast_to([H0, CE])).then_inc(loaded, 16)

        @block.gpsimd
        def _(pool):
            nc.gpsimd.memset(k.w[:, (NT - 1) * P:], 0.0).then_inc(cleared, 1)
            nc.gpsimd.memset(same[:, 0:1], 0.0).then_inc(cleared, 1)
            nc.gpsimd.memset(same[:, CE:CE + 1], 0.0).then_inc(cleared, 1)
            for t in (link, nxt, carry):
                nc.gpsimd.memset(t[:, :, :], 0.0).then_inc(cleared, 1)

        @block.vector
        def _(v):
            ch = Chain(v, dve)
            v.wait_ge(loaded, 16 * C)
            v.wait_ge(cleared, 6)
            ch.link(nc.vector.tensor_tensor(same[:, 1:CE], d[:, 1:CE], d[:, 0:CE - 1], ALU.is_equal))
            ch.link(nc.vector.tensor_tensor_scan(seg[:, :], same[:, 0:CE], k.score[:, 0:CE], 0.0, ALU.mult, ALU.max))
            ch.link(nc.vector.tensor_tensor_scan(seg[:, ::-1], same[:, CE:0:-1], seg[:, ::-1], 0.0, ALU.mult, ALU.max))
            ch.link(nc.vector.tensor_copy(ends[:, 0:1], seg[:, 0:1]))
            ch.link(nc.vector.tensor_copy(ends[:, 1:2], seg[:, CE - 1:CE]))
            ch.link(nc.vector.tensor_copy(ends[:, 2:3], d[:, 0:1]))
            ch.link(nc.vector.tensor_copy(ends[:, 3:4], d[:, CE - 1:CE]))
            v.sem_inc(ends_ok, 1)
            v.wait_ge(ends_ps, 1)
            ch.link(nc.vector.tensor_copy(row[:, :, :].rearrange("o j (h c) -> o j h c", c=C), bank[0][0:1, :].rearrange("o (j c h) -> o j h c", j=4, h=H0)))
            r4 = row[:, :, :].rearrange("o j (h c) -> o j h c", c=C)
            ch.link(nc.vector.tensor_tensor(link[:, :, 1:C], r4[:, 2, :, 1:C], r4[:, 3, :, 0:C - 1], ALU.is_equal))
            ch.link(nc.vector.tensor_copy(nxt[:, :, 0:C - 1], link[:, :, 1:C]))
            ch.link(nc.vector.tensor_tensor(one[:, :, :], r4[:, 2], r4[:, 3], ALU.is_equal))
            ch.link(nc.vector.tensor_tensor(g[:, :, :], one[:, :, :], link[:, :, :], ALU.mult))
            ch.link(nc.vector.tensor_tensor_scan(flat(fc[:, :, :]), flat(g[:, :, :]), row[:, 1, :], 0.0, ALU.mult, ALU.max))
            ch.link(nc.vector.tensor_tensor(g[:, :, :], one[:, :, :], nxt[:, :, :], ALU.mult))
            ch.link(nc.vector.tensor_tensor_scan(flat(bc[:, :, :])[:, ::-1], flat(g[:, :, :])[:, ::-1], row[:, 0, ::-1], 0.0, ALU.mult, ALU.max))
            cr = carry[:, :, :].rearrange("o j (c h) -> o j h c", h=H0)
            ch.link(nc.vector.tensor_tensor(cr[:, 0, :, 1:C], fc[:, :, 0:C - 1], link[:, :, 1:C], ALU.mult))
            ch.link(nc.vector.tensor_tensor(cr[:, 1, :, 0:C - 1], bc[:, :, 1:C], nxt[:, :, 0:C - 1], ALU.mult))
            v.sem_inc(carry_ok, 1)
            v.wait_ge(carry_ps, 1)
            ch.link(nc.vector.tensor_copy(carry_c[:, :], bank[1][:, 0:2]))
            for j in range(2):
                ch.link(nc.vector.tensor_scalar(same[:, 0:CE], d[:, :], ends[:, 2 + j:3 + j], carry_c[:, j:j + 1], ALU.is_equal, ALU.mult))
                ch.link(nc.vector.tensor_tensor(seg[:, :], seg[:, :], same[:, 0:CE], ALU.max))
            nc.vector.tensor_tensor(seg[:, :], k.score[:, 0:CE], seg[:, :], ALU.subtract).then_inc(diff_ok, 1)
            for n in range(-(-NT // 4)):
                v.wait_ge(w_ps, n + 1)
                if 4 * n + 4 <= NT:
                    nc.vector.tensor_copy(k.w[:, 4 * n * P:(4 * n + 4) * P], bank[2 + n % 4][:, :]).then_inc(w_ok, 1)
                else:
                    nc.vector.tensor_copy(k.w[0:TAIL, 4 * n * P:], bank[2 + n % 4][0:TAIL, 0:P]).then_inc(w_ok, 1)

        @block.scalar
        def _(act):
            act.wait_ge(diff_ok, 1)
            nc.scalar.activation(k.score[:, 0:CE], seg[:, :], ACT.Exp).then_inc(exp_ok, 1)

        @block.tensor
        def _(pe):
            pe.wait_ge(ends_ok, 1)
            for j in range(4):
                last = nc.tensor.transpose(bank[0][0:1, j * P:(j + 1) * P], ends[:, j:j + 1], k.ident[:, :])
            last.then_inc(ends_ps, 1)
            pe.wait_ge(carry_ok, 1)
            for j in range(2):
                last = nc.tensor.transpose(bank[1][:, j:j + 1], carry[0:1, j, :], k.ident[0:1, 0:1])
            last.then_inc(carry_ps, 1)
            pe.wait_ge(exp_ok, 1)
            for n in range(-(-NT // 4)):
                if n >= 4:
                    pe.wait_ge(w_ok, n - 3)
                for t in range(4 * n, min(4 * n + 4, NT)):
                    m = P if t < NT - 1 else TAIL
                    last = nc.tensor.transpose(bank[2 + n % 4][0:m, t % 4 * P:(t % 4 + 1) * P], k.score[:, t * P:t * P + m], k.ident[:, :])
                last.then_inc(w_ps, 1)


def registers(nc, eng, ap, top):
    return nc.values_load_multi_w_load_instructions(ap, engines=(eng,), min_val=0, max_val=top,
                                                    skip_runtime_bounds_check_because="the tables are built on the chip, within the bound")[1]


def aggregate(nc, a, k):
    with Stage(nc, "sum") as s:
        bank = s.banks()
        acc = s.sb("acc", [P, NT, D + H0])
        got = s.sb("gathered", [P, U, D])
        ids = s.sb("rows", [P, U], I32)
        msg, hot = s.sb("messages", [P, U, D + H0]), s.sb("one_hot", [P, U, P])
        den = s.sb("denominator", [P, NT, H0])
        ids_ok, used = s.sem("rows_ready"), Count(s, "rows_used", U)
        arrived = [s.sem(f"gathered{u}") for u in range(U)]
        off, far = s.sb("offset", [P, U]), s.sb("distance", [P, U, P])
        off_ok, far_ok, hot_ok = s.sem("offset_ready"), s.sem("distance_ready"), s.sem("one_hot_ready")
        summed, added = Count(s, "summed", U), Count(s, "added", 1)
        begun, cleared, dve = s.sem("gathers_begun"), s.sem("cleared"), s.sem("dve")
        block = s.block()

        @block.gpsimd
        def _(pool):
            nc.gpsimd.memset(acc[:, :, :], 0.0).then_inc(cleared, 1)
            with pool.Fori(0, ITEMS // U) as i:
                for u in range(U):
                    if u % 4 == 0:
                        pool.wait_ge(ids_ok, i * U + u + 4)
                        pool.sem_inc(begun, 1)
                    nc.gpsimd.indirect_dma_start(got[:, u, :], None, k.h_tab, bass.IndirectOffsetOnAxis(ids[:, u:u + 1], 0)).then_inc(arrived[u], 16)

        @block.scalar
        def _(act):
            with act.Fori(0, ITEMS // U) as i:
                z = registers(nc, mybir.EngineType.Activation, k.item_i[0:1, 0, bass.ds(i * U, U)], NT * C - 1)
                for q in range(0, U, 4):
                    n = i * U + q
                    used.slot(act, n + 3)
                    for u in range(q, q + 4):
                        last = nc.scalar.activation(ids[:, u:u + 1], col(k.edge_row, z[u]), ACT.Copy)
                    last.then_inc(ids_ok, 4)
                    for u in range(q, q + 4):
                        last = nc.scalar.activation(off[:, u:u + 1], col(k.dst_f, z[u]), ACT.Identity, scale=-1.0, bias=col(k.item_base, n + u - q))
                    last.then_inc(off_ok, 1)
                    act.wait_ge(off_ok, i * (U // 4) + q // 4 + 1)
                    for u in range(q, q + 4):
                        last = nc.scalar.activation(far[:, u, :], k.iota[:, :], ACT.Abs, bias=off[:, u:u + 1])
                    last.then_inc(far_ok, 1)
                    act.wait_ge(far_ok, i * (U // 4) + q // 4 + 1)
                    summed.slot(act, n + 3)
                    nc.scalar.activation(hot[:, q:q + 4, :], far[:, q:q + 4, :], ACT.Relu, scale=-1.0, bias=k.ones[:, 0:1]).then_inc(hot_ok, 4)

        @block.vector
        def _(v):
            used.start(v)
            added.start(v)
            v.wait_ge(cleared, 1)
            LAG = 3

            def add(n, u, b):
                summed.done(v, n)
                added.slot(v, n)
                nc.vector.tensor_tensor(col(acc, b), bank[u][:, 0:D + H0], col(acc, b), ALU.add).then_inc(added.sem, 1)

            def blocks(first, m):
                return registers(nc, mybir.EngineType.DVE, k.item_i[0:1, 1, first:first + m] if isinstance(first, int)
                                 else k.item_i[0:1, 1, bass.ds(first, m)], NT - 1)

            def round_(i, peeled):
                z = registers(nc, mybir.EngineType.DVE, k.item_i[0:1, 0, bass.ds(i * U, U)] if not peeled else k.item_i[0:1, 0, 0:U], NT * C - 1)
                b = blocks(0, U - LAG) if peeled else blocks(i * U - LAG, U)
                for u in range(U):
                    w = k.w[:, bass.ds(z[u] * H0, H0)]
                    v.wait_ge(arrived[u], (i + 1) * 16)
                    summed.slot(v, i * U + u)
                    nc.vector.tensor_copy(msg[:, u, D:D + H0], w)
                    nc.vector.tensor_tensor(msg[:, u, 0:D].rearrange("p (h d) -> p h d", h=H0), got[:, u, :].rearrange("p (h d) -> p h d", h=H0),
                                            w.rearrange("p (h o) -> p h o", o=1).broadcast_to([P, H0, HD0]), ALU.mult).then_inc(used.sem, 1)
                    if not peeled:
                        add(i * U + u - LAG, (u - LAG) % U, b[u])
                    elif u >= LAG:
                        add(u - LAG, u - LAG, b[u - LAG])
            round_(0, True)
            with v.Fori(1, ITEMS // U) as i:
                round_(i, False)
            b = blocks(ITEMS - LAG, LAG)
            for u in range(LAG):
                add(ITEMS - LAG + u, U - LAG + u, b[u])
            ch = Chain(v, dve)
            added.done(v, ITEMS - 1)
            ch.link(nc.vector.tensor_scalar(den[:, :, :], acc[:, :, D:D + H0], 1e-12, None, ALU.add))
            ch.link(nc.vector.reciprocal(den[:, :, :], den[:, :, :]))

            def finish(t, u):
                m = col(acc, t)[:, 0:D].rearrange("p (h d) -> p h d", h=H0)
                nc.vector.tensor_tensor(m, m, col(den, t).rearrange("p (h o) -> p h o", o=1).broadcast_to([P, H0, HD0]), ALU.mult).then_inc(dve, 1)
            c0 = ch.n
            tiles(v, NT, 7, finish)
            ch.n = c0 + NT
            v.wait_ge(dve, ch.n)
            ch.link(nc.vector.tensor_tensor(k.x[:, :, :], k.x[:, :, :], acc[:, :, 0:D], ALU.add))

        @block.tensor
        def _(pe):
            summed.start(pe)
            with pe.Fori(0, ITEMS // U) as i:
                for u in range(U):
                    used.done(pe, i * U + u)
                    pe.wait_ge(hot_ok, i * U + u + 1)
                    nc.tensor.matmul(bank[u][:, 0:D + H0], hot[:, u, :], msg[:, u, :], start=True, stop=True).then_inc(summed.sem, 1)


def route_tiles(experts, top):
    return (N * top + experts * (P - 1)) // P


class Route:

    def __init__(self, nc, s, k, experts, top, spare=0):
        self.nc, self.k, self.K, self.top = nc, k, experts, top
        self.tiles = route_tiles(experts, top) + spare
        self.place = [s.sb(f"place{j}", [P, NT]) for j in range(top)]
        self.expert = s.sb("expert", [1, self.tiles], I32)

    def work_in(self, s, bank):
        experts, top, self.bank = self.K, self.top, bank
        K, T = experts, self.tiles
        self.logits = s.sb("logits", [P, NT, K])
        self.pick = [s.sb(f"pick{j}", [P, NT, K]) for j in range(top)]
        self.best = [s.sb(f"best{j}", [P, NT]) for j in range(top)]
        self.at = s.sb("at", [P, NT])
        self.work = s.sb("work", [P, NT, K])
        self.mask = self.logits
        self.reset = self.work[:, :, :].rearrange("p t e -> p (t e)").rearrange("p (e t) -> p e t", e=K)
        self.number, self.total = s.sb("number", [P, K]), s.sb("total", [P, K, NT])
        self.running = s.sb("running", [P, K, NT])
        self.count, self.start_row, self.count_i = s.sb("count", [P, K]), s.sb("start_row", [P, K]), s.sb("count_i", [P, K], I32)
        self.valid = s.sb("valid", [P, 1])
        self.tile_row_i, self.tile_row = s.sb("tile_row_i", [1, T], I32), s.sb("tile_row", [1, T])
        self.tile_cmp, self.expert_f = s.sb("tile_cmp", [1, T, K]), s.sb("expert_f", [1, T])
        self.iotas, self.picked, self.counted = s.sem("route_iotas"), s.sem("picked"), s.sem("counted")
        self.per = NT * K // 4 if NT * K > 512 else NT * K
        self.chunks = NT * K // self.per
        assert self.per <= 512 and self.chunks * self.per == NT * K

    def pool(self):
        nc = self.nc
        nc.gpsimd.iota(self.tile_row_i[:, :], [[P, self.tiles]], base=0, channel_multiplier=0).then_inc(self.iotas, 1)

    def choose(self, v, ch):
        nc, K = self.nc, self.K
        b3 = lambda x: x.rearrange("p (t o) -> p t o", o=1).broadcast_to([P, NT, K])
        bk = lambda x: x.rearrange("p (o e) -> p o e", o=1).broadcast_to([P, NT, K])
        ch.link(nc.vector.tensor_copy(self.number[:, :], self.k.iota[:, 0:K]))
        for j in range(self.top):
            ch.link(nc.vector.reduce_max(self.best[j][:, :], self.logits[:, :, :], AX.X))
            ch.link(nc.vector.tensor_tensor(self.work[:, :, :], self.logits[:, :, :], b3(self.best[j][:, :]), ALU.is_equal))
            ch.link(nc.vector.scalar_tensor_tensor(self.work[:, :, :], self.work[:, :, :], -1000.0, bk(self.number[:, :]), ALU.mult, ALU.add))
            ch.link(nc.vector.tensor_reduce(self.at[:, :], self.work[:, :, :], AX.X, ALU.min))
            ch.link(nc.vector.scalar_tensor_tensor(self.pick[j][:, :, :], bk(self.number[:, :]), -1000.0, b3(self.at[:, :]), ALU.add, ALU.is_equal))
            if j + 1 < self.top:
                ch.link(nc.vector.scalar_tensor_tensor(self.logits[:, :, :], self.pick[j][:, :, :], -3e38, self.logits[:, :, :], ALU.mult, ALU.add))

    def vector(self, v, ch):
        nc, K = self.nc, self.K
        v.wait_ge(self.iotas, 1)
        self.choose(v, ch)
        ch.link(nc.vector.tensor_scalar(self.valid[:, :], self.k.col[:, :], float(TAIL), None, ALU.is_lt))
        ch.link(nc.vector.tensor_copy(self.mask[:, :, :], self.pick[0][:, :, :]))
        for j in range(1, self.top):
            ch.link(nc.vector.tensor_tensor(self.mask[:, :, :], self.mask[:, :, :], self.pick[j][:, :, :], ALU.add))
        ch.link(nc.vector.tensor_scalar(self.mask[:, NT - 1, :], self.mask[:, NT - 1, :], self.valid[:, 0:1], None, ALU.mult))
        v.sem_inc(self.picked, 1)
        ch.link(nc.vector.tensor_copy(self.tile_row[:, :], self.tile_row_i[:, :]))
        v.wait_ge(self.counted, 1)
        w = flat(self.work[:, :, :])
        for n in range(self.chunks):
            ch.link(nc.vector.tensor_copy(w[:, n * self.per:(n + 1) * self.per], self.bank[4 + n][:, 0:self.per]))
        ch.link(nc.vector.tensor_copy(self.total[:, :, :], self.work[:, :, :].rearrange("p t e -> p e t")))
        ch.link(nc.vector.memset(self.reset, 1.0))
        ch.link(nc.vector.memset(self.reset[:, :, 0:1], 0.0))
        ch.link(nc.vector.tensor_tensor_scan(flat(self.running[:, :, :]), flat(self.reset), flat(self.total[:, :, :]), 0.0, ALU.mult, ALU.add))
        ch.link(nc.vector.tensor_scalar(self.count[:, :], self.running[:, :, NT - 1], float(P - 1), None, ALU.add))
        ch.link(nc.vector.tensor_copy(self.count_i[:, :], self.count[:, :]))
        ch.link(nc.vector.tensor_scalar(self.count_i[:, :], self.count_i[:, :], 7, 7, ALU.arith_shift_right, ALU.logical_shift_left))
        ch.link(nc.vector.tensor_copy(self.count[:, :], self.count_i[:, :]))
        ch.link(nc.vector.tensor_tensor_scan(self.start_row[:, :], self.count[:, :], self.count[:, :], 0.0, ALU.add, ALU.bypass))
        ch.link(nc.vector.tensor_tensor(self.start_row[:, :], self.start_row[:, :], self.count[:, :], ALU.subtract))
        ch.link(nc.vector.tensor_tensor(self.running[:, :, :], self.running[:, :, :], self.total[:, :, :], ALU.subtract))
        sr = self.start_row[:, :].rearrange("p (e o) -> p e o", o=1).broadcast_to([P, K, NT])
        ch.link(nc.vector.tensor_tensor(self.running[:, :, :], self.running[:, :, :], sr, ALU.add))
        ch.link(nc.vector.tensor_copy(self.work[:, :, :], self.running[:, :, :].rearrange("p e t -> p t e")))
        for n in range(self.chunks):
            c = w[:, n * self.per:(n + 1) * self.per]
            ch.link(nc.vector.tensor_tensor(c, self.bank[n][:, 0:self.per], c, ALU.add))
        for j in range(self.top):
            ch.link(nc.vector.tensor_tensor(self.mask[:, :, :], self.pick[j][:, :, :], self.work[:, :, :], ALU.mult))
            ch.link(nc.vector.reduce_sum(self.place[j][:, :], self.mask[:, :, :], AX.X))
        T = self.tiles
        ch.link(nc.vector.tensor_tensor(self.tile_cmp[:, :, :], self.tile_row[:, :].rearrange("p (t o) -> p t o", o=1).broadcast_to([1, T, K]),
                                        self.start_row[0:1, :].rearrange("p (o e) -> p o e", o=1).broadcast_to([1, T, K]), ALU.is_ge))
        ch.link(nc.vector.reduce_sum(self.expert_f[:, :], self.tile_cmp[:, :, :], AX.X))
        ch.link(nc.vector.tensor_scalar(self.expert_f[:, :], self.expert_f[:, :], -1.0, None, ALU.add))
        ch.link(nc.vector.tensor_copy(self.expert[:, :], self.expert_f[:, :]))

    def tensor(self, pe):
        nc = self.nc
        pe.wait_ge(self.picked, 1)
        m = flat(self.mask[:, :, :])
        for n in range(self.chunks):
            c = m[:, n * self.per:(n + 1) * self.per]
            nc.tensor.matmul(self.bank[n][:, 0:self.per], self.k.before[:, :], c, start=True, stop=True)
            last = nc.tensor.matmul(self.bank[4 + n][:, 0:self.per], self.k.ones[:, :], c, start=True, stop=True)
        last.then_inc(self.counted, 1)


def moe0(nc, a, k):
    with Stage(nc, "moe0") as s:
        bank = s.banks()
        norm = Norm(nc, s, k, bank[0:2])
        route = Route(nc, s, k, E0, 1)
        route.work_in(s, bank)
        T = route.tiles
        rw_n, rw = s.sb("router_natural", [E0, D]), s.sb("router", [P, DC, E0])
        rb = s.sb("router_bias", [P, E0])
        w1, w2 = s.sb("w1", [P, DC, E0, F0]), s.sb("w2", [F0, E0, D])
        b1, b2 = s.sb("b1", [P, E0, F0]), s.sb("b2", [P, E0, D])
        ids = s.sb("rows", [P, 4], I32)
        xi, xT = s.sb("tile", [P, 4, D]), s.sb("tile_T", [P, 4, D])
        hid, hT = s.sb("hidden", [P, 4, P]), s.sb("hidden_T", [F0, 4, P])
        y = s.sb("y", [P, 4, D])
        loaded, rw_ps, rw_ok = s.sem("weights_loaded"), s.sem("router_in_psum"), s.sem("router_ready")
        lg_ps, lg_ok = Count(s, "logits_in_psum", 2), Count(s, "logits_ready", 2)
        route_ok, row_ok = s.sem("route_ready"), s.sem("row_ready")
        scattered, gathered = [s.sem(f"scattered{u}") for u in range(4)], [s.sem(f"gathered{u}") for u in range(4)]
        begun, all_out = s.sem("dma_begun"), s.sem("all_results_written")
        tile_in = [s.sem(f"tile_loaded{u}") for u in range(4)]
        out_ok = Landed(s, "y_written", 4)
        x_ps, x_ok, h_ps, h_ok, ht_ps, ht_ok, y_ps, y_add, y_ok = (Count(s, n, 4) for n in (
            "x_in_psum", "xT_ready", "hidden_in_psum", "hidden_ready", "hidden_T_in_psum", "hidden_T_ready", "y_in_psum", "y_biased", "y_ready"))
        block = s.block()

        @block.gpsimd
        def _(pool):
            route.pool()

            def scatter(i, u):
                t = i * 4 + u
                m = P if not isinstance(t, int) or t < NT - 1 else TAIL
                pool.wait_ge(row_ok, t + 1)
                pool.sem_inc(begun, 1)
                nc.gpsimd.indirect_dma_start(k.xs0, bass.IndirectOffsetOnAxis(ids[0:m, u:u + 1], 0), xi[0:m, u, :], None).then_inc(scattered[u], 16)
            rounds(pool, NT, 4, scatter)
            for u in range(4):
                pool.wait_ge(scattered[u], 16 * ((NT - u + 3) // 4))

            def load(i, u):
                x_ps.slot(pool, i * 4 + u)
                pool.dma_start(xi[:, u, :], rows(k.xs0, (i * 4 + u) * P, P)).then_inc(tile_in[u], 16)
            turns(pool, T, 4, load)
            pool.wait_ge(all_out, 1)

            def gather(i, u):
                t = i * 4 + u
                m = P if not isinstance(t, int) or t < NT - 1 else TAIL
                pool.wait_ge(row_ok, NT + t + 1)
                pool.sem_inc(begun, 1)
                nc.gpsimd.indirect_dma_start(y[0:m, u, :], None, k.ys0, bass.IndirectOffsetOnAxis(ids[0:m, u:u + 1], 0)).then_inc(gathered[u], 16)
            rounds(pool, NT, 4, gather)

        @block.sync
        def _(sp):
            sp.dma_start(rw_n[:, :], a["L0_ffn_router_w"]).then_inc(loaded, 16)
            sp.dma_start(rb[:, :], a["L0_ffn_router_b"].rearrange("(o e) -> o e", o=1).broadcast_to([P, E0])).then_inc(loaded, 16)
            for c in range(DC):
                sp.dma_start(w1[:, c, :, :], a["L0_ffn_W1"][:, c * P:(c + 1) * P, :].rearrange("e p h -> p e h")).then_inc(loaded, 16)
            sp.dma_start(w2[:, :, :], a["L0_ffn_W2"].rearrange("e h d -> h e d")).then_inc(loaded, 16)
            for t, name in ((b1, "L0_ffn_b1"), (b2, "L0_ffn_b2")):
                v = a[name].rearrange("e h -> (e h)").rearrange("(o n) -> o n", o=1)
                sp.dma_start(flat(t[:, :, :]), v.broadcast_to([P, v.shape[1]])).then_inc(loaded, 16)
            out_ok.start(sp)

            def save(i, u):
                y_ok.done(sp, i * 4 + u)
                sp.dma_start(rows(k.ys0, (i * 4 + u) * P, P), y[:, u, :]).then_inc(out_ok.sems[u], 16)
            turns(sp, T, 4, save)
            out_ok.all(sp, T)
            sp.sem_inc(all_out, 1)

        @block.scalar
        def _(act):
            norm.root(act)
            tiles(act, NT, 2, lambda t, u: norm.keep(act, t, u, lg_ps))
            act.wait_ge(route_ok, 1)
            for n in (x_ok, ht_ok, y_ok):
                n.start(act)
            with act.Fori(0, T // 4) as i:
                for u in range(4):
                    x_ps.done(act, i * 4 + u)
                    nc.scalar.activation(xT[:, u, :], bank[2 * u][:, 0:D], ACT.Copy).then_inc(x_ok.sem, 1)
                for u in range(4):
                    ht_ps.done(act, i * 4 + u)
                    nc.scalar.activation(hT[:, u, :], bank[2 * u][0:F0, 3 * P:4 * P], ACT.Relu).then_inc(ht_ok.sem, 1)
                for u in range(4):
                    y_add.done(act, i * 4 + u)
                    nc.scalar.activation(y[:, u, :], y[:, u, :], ACT.Relu).then_inc(y_ok.sem, 1)

        @block.vector
        def _(v):
            ch = Chain(v, norm.dve)
            ch.link(nc.vector.memset(hid[:, :, :], 0.0))
            norm.statistics(v, ch)
            v.wait_ge(loaded, 7 * 16)
            v.wait_ge(rw_ps, 1)
            nc.vector.tensor_copy(rw[:, :, :], bank[4][:, 0:DC * E0].rearrange("p (c e) -> p c e", c=DC)).then_inc(rw_ok, 1)
            lg_ok.start(v)

            def logits(t, u):
                lg_ps.done(v, t)
                nc.vector.tensor_tensor(col(route.logits, t), bank[2 + u][:, 0:E0], rb[:, :], ALU.add).then_inc(lg_ok.sem, 1)
            norm.normalise(v, 0, 0)
            with v.Fori(0, (NT - 1) // 2) as i:
                for u in range(2):
                    norm.normalise(v, i * 2 + u + 1, 1 - u)
                    logits(i * 2 + u, u)
            logits(NT - 1, 0)
            lg_ok.done(v, NT - 1)
            route.vector(v, ch)
            v.sem_inc(route_ok, 1)

            def send(i, u):
                t = i * 4 + u
                if not isinstance(i, int) or i:
                    v.wait_ge(scattered[u], i * 16)
                nc.vector.tensor_scalar(xi[:, u, :], col(k.x, t), col(norm.mean, t), col(norm.rstd, t), ALU.subtract, ALU.mult)
                nc.vector.tensor_copy(ids[:, u:u + 1], col(route.place[0], t)).then_inc(row_ok, 1)
            rounds(v, NT, 4, send)
            for n in (h_ok, y_add):
                n.start(v)
            with v.Fori(0, T // 4) as i:
                e = registers(nc, mybir.EngineType.DVE, route.expert[0:1, bass.ds(i * 4, 4)], E0 - 1)
                for u in range(4):
                    h_ps.done(v, i * 4 + u)
                    nc.vector.tensor_tensor(hid[:, u, 0:F0], bank[2 * u][:, D:D + F0], col(b1, e[u]), ALU.add).then_inc(h_ok.sem, 1)
                for u in range(4):
                    y_ps.done(v, i * 4 + u)
                    out_ok.slot(v, i, u)
                    nc.vector.tensor_tensor(y[:, u, :], bank[2 * u + 1][:, 0:D], col(b2, e[u]), ALU.add).then_inc(y_add.sem, 1)
            for u in range(4):
                v.wait_ge(scattered[u], 16 * ((NT - u + 3) // 4))

            def address(i, u):
                nc.vector.tensor_copy(ids[:, u:u + 1], col(route.place[0], i * 4 + u)).then_inc(row_ok, 1)

            def add(i, u):
                v.wait_ge(gathered[u], i * 16 + 16)
                m = P if not isinstance(i, int) or i * 4 + u < NT - 1 else TAIL
                x = col(k.x, i * 4 + u)[0:m]
                nc.vector.tensor_tensor(x, x, y[0:m, u, :], ALU.add).then_inc(norm.dve, 1)
            for u in range(4):
                address(0, u)
            with v.Fori(0, NT // 4 - 1) as i:
                for u in range(4):
                    add(i, u)
                    address(i + 1, u)
            for u in range(4):
                add(NT // 4 - 1, u)
            address(NT // 4, 0)
            add(NT // 4, 0)

        @block.tensor
        def _(pe):
            pe.wait_ge(loaded, 7 * 16)
            for c in range(DC):
                last = nc.tensor.transpose(bank[4][:, c * E0:(c + 1) * E0], rw_n[:, c * P:(c + 1) * P], k.ident[0:E0, 0:E0])
            last.then_inc(rw_ps, 1)
            pe.wait_ge(rw_ok, 1)
            norm.t_ps.start(pe)
            lg_ps.start(pe)

            def body(t, u):
                norm.transpose(pe, t, u)
                norm.t_ok.done(pe, t)
                lg_ok.slot(pe, t)
                for c in range(DC):
                    last = nc.tensor.matmul(bank[2 + u][:, 0:E0], norm.xT[:, u, c * P:(c + 1) * P], rw[:, c, :], start=(c == 0), stop=(c == DC - 1))
                last.then_inc(lg_ps.sem, 1)
            tiles(pe, NT, 2, body)
            route.tensor(pe)
            pe.wait_ge(route_ok, 1)
            for n in (x_ps, h_ps, ht_ps, y_ps):
                n.start(pe)
            with pe.Fori(0, T // 4) as i:
                e = registers(nc, mybir.EngineType.PE, route.expert[0:1, bass.ds(i * 4, 4)], E0 - 1)
                for u in range(4):
                    pe.wait_ge(tile_in[u], (i + 1) * 16)
                    for c in range(DC):
                        last = nc.tensor.transpose(bank[2 * u][:, c * P:(c + 1) * P], xi[:, u, c * P:(c + 1) * P], k.ident[:, :])
                    last.then_inc(x_ps.sem, 1)
                for u in range(4):
                    x_ok.done(pe, i * 4 + u)
                    for c in range(DC):
                        last = nc.tensor.matmul(bank[2 * u][:, D:D + F0], xT[:, u, c * P:(c + 1) * P], col(w1[:, c], e[u]),
                                                start=(c == 0), stop=(c == DC - 1))
                    last.then_inc(h_ps.sem, 1)
                for u in range(4):
                    h_ok.done(pe, i * 4 + u)
                    nc.tensor.transpose(bank[2 * u][:, 3 * P:4 * P], hid[:, u, :], k.ident[:, :]).then_inc(ht_ps.sem, 1)
                for u in range(4):
                    ht_ok.done(pe, i * 4 + u)
                    y_add.slot(pe, i * 4 + u)
                    nc.tensor.matmul(bank[2 * u + 1][:, 0:D], hT[:, u, :], col(w2, e[u]), start=True, stop=True).then_inc(y_ps.sem, 1)


def attend1(nc, a, k):
    with Stage(nc, "gnn1") as s:
        bank = s.banks()
        norm = Norm(nc, s, k, bank[0:2])
        W = D + 2 * H1
        w, wT = s.sb("w", [P, DC, W]), s.sb("wT", [P, DC, D])
        ablk = s.sb("attn_blocks", [P, DC, 2 * H1])
        g = s.sb("rows_out", [P, 2, W])
        ids = s.sb("rows", [P, 4, 2], I32)
        got, left = s.sb("gathered", [P, 4, W]), s.sb("row_half", [P, 4, H1])
        al, mx, ex, sm, prod, red = (s.sb(n, [P, 4, m]) for n, m in (("alpha", H1), ("max", 1), ("exp", H1), ("sum", 1), ("products", D), ("reduced", HD1)))
        loaded, cleared, wt_ps, wt_ok, v_ps, v_ok = (s.sem(n) for n in ("weights_loaded", "cleared", "wT_in_psum", "wT_ready", "v_in_psum", "v_ready"))
        xt_ps, g_ok, stored = Count(s, "products_in_psum", 2), Count(s, "rows_ready", 2), Landed(s, "rows_stored", 2, 2)
        tables, begun, ids_ok = s.sem("tables_written"), s.sem("gathers_begun"), s.sem("ids_ready")
        arrived = [s.sem(f"arrived{u}") for u in range(4)]
        used, al_ok, ex_ok = Count(s, "used", 4), Count(s, "alpha_ready", 4), Count(s, "exp_ready", 4)
        block = s.block()

        @block.gpsimd
        def _(pool):
            nc.gpsimd.memset(ablk[:, :, :], 0.0).then_inc(cleared, 1)
            pool.wait_ge(tables, 1)

            def gather(t, u):
                pool.wait_ge(ids_ok, t + 1)
                pool.sem_inc(begun, 1)
                nc.gpsimd.indirect_dma_start(got[:, u, :], None, k.g_tab, bass.IndirectOffsetOnAxis(ids[:, u, 0:1], 0)).then_inc(arrived[u], 16)
                nc.gpsimd.indirect_dma_start(left[:, u, :], None, k.l_tab, bass.IndirectOffsetOnAxis(ids[:, u, 1:2], 0)).then_inc(arrived[u], 16)
            tiles(pool, NT, 4, gather)

        @block.sync
        def _(sp):
            sp.dma_start(w[:, :, 0:D], a["L1_gnn_weight"].rearrange("(c p) o -> p c o", p=P)).then_inc(loaded, 16)
            sp.wait_ge(cleared, 1)
            with nc.allow_non_contiguous_dma(reason="short vectors onto partitions"):
                for j, name in enumerate(("L1_gnn_attn_r", "L1_gnn_attn_l")):
                    for h in range(H1):
                        p0 = h * HD1 % P
                        sp.dma_start(ablk[p0:p0 + HD1, h * HD1 // P, j * H1 + h:j * H1 + h + 1],
                                     a[name][h:h + 1, :].rearrange("a b -> b a")).then_inc(loaded, 16)
            stored.start(sp)

            def save(t, u):
                g_ok.done(sp, t)
                sp.dma_start(rows(k.g_tab, t * P, P), g[:, u, :]).then_inc(stored.sems[u], 16)
                sp.dma_start(rows(k.l_tab, t * P, P), g[:, u, D + H1:W]).then_inc(stored.sems[u], 16)
            tiles(sp, NT, 2, save)
            stored.all(sp, NT)
            sp.sem_inc(tables, 1)

        @block.scalar
        def _(act):
            norm.root(act)
            g_ok.start(act)

            def body(i, u):
                t = i * 2 + u
                norm.keep(act, t, u, xt_ps)
                xt_ps.done(act, t)
                stored.slot(act, i, u)
                nc.scalar.activation(g[:, u, :], bank[2 + u][:, 0:W], ACT.Copy).then_inc(g_ok.sem, 1)
            turns(act, NT, 2, body)
            ex_ok.start(act)

            def exps(t, u):
                al_ok.done(act, t)
                nc.scalar.activation(ex[:, u, :], al[:, u, :], ACT.Exp, accum_out=sm[:, u, :]).then_inc(ex_ok.sem, 1)
            tiles(act, NT, 4, exps)

        @block.vector
        def _(v):
            ch = Chain(v, norm.dve)
            norm.statistics(v, ch)
            v.wait_ge(wt_ps, 1)
            nc.vector.tensor_copy(wT[:, :, :], bank[4][:, :].rearrange("p (c f) -> p c f", c=DC)).then_inc(wt_ok, 1)
            v.wait_ge(v_ps, 1)
            nc.vector.tensor_copy(w[:, :, D:W], bank[5][:, 0:DC * 2 * H1].rearrange("p (c j) -> p c j", c=DC)).then_inc(v_ok, 1)
            tiles(v, NT, 2, lambda t, u: norm.normalise(v, t, u))
            used.start(v)
            al_ok.start(v)
            c0 = ch.n

            def one(t, u, m):
                used.slot(v, t)
                nc.vector.tensor_copy(ids[:, u, 0:1], col(k.dst_i, t))
                nc.vector.tensor_copy(ids[:, u, 1:2], col(k.src_i, t)).then_inc(ids_ok, 1)

            def first(n, i, u):
                t = i * 4 + u
                v.wait_ge(arrived[u], (i + 1) * 32)
                ch.link(nc.vector.tensor_tensor(al[:, u, :], left[:, u, :], got[:, u, D:D + H1], ALU.add))
                ch.link(nc.vector.scalar_tensor_tensor(al[:, u, :], al[:, u, :], 0.01, al[:, u, :], ALU.mult, ALU.max))
                ch.link(nc.vector.reduce_max(mx[:, u, :], al[:, u, :], AX.X))
                nc.vector.tensor_scalar(al[:, u, :], al[:, u, :], mx[:, u, :], None, ALU.subtract).then_inc(al_ok.sem, 1)

            def second(n, i, u):
                t = i * 4 + u
                ex_ok.done(v, t)
                ch.link(nc.vector.reciprocal(mx[:, u, :], sm[:, u, :]))
                p4 = prod[:, u, :].rearrange("p (h d) -> p h d", h=H1)
                ch.link(nc.vector.tensor_tensor(p4, got[:, u, 0:D].rearrange("p (h d) -> p h d", h=H1),
                                                ex[:, u, :].rearrange("p (h o) -> p h o", o=1).broadcast_to([P, H1, HD1]), ALU.mult))
                ch.link(nc.vector.reduce_sum(red[:, u, :], p4.rearrange("p h d -> p d h"), AX.X))
                x4 = col(k.x, t).rearrange("p (h d) -> p h d", h=H1)
                nc.vector.scalar_tensor_tensor(x4, red[:, u, :].rearrange("p (o d) -> p o d", o=1).broadcast_to([P, H1, HD1]),
                                               mx[:, u, :], x4, ALU.mult, ALU.add).then_inc(used.sem, 1)
            for u in range(4):
                one(u, u, 0)
            with v.Fori(0, NT // 4 - 1) as i:
                ch.n = c0 + i * 24
                for u in range(4):
                    first(0, i, u)
                for u in range(4):
                    second(0, i, u)
                    one(i * 4 + 4 + u, u, 0)
            i = NT // 4 - 1
            ch.n = c0 + i * 24
            for u in range(4):
                first(0, i, u)
            for u in range(4):
                second(0, i, u)
            one(NT - 1, 0, 0)
            first(0, i + 1, 0)
            second(0, i + 1, 0)
            used.done(v, NT - 1)

        @block.tensor
        def _(pe):
            pe.wait_ge(loaded, 16 * (1 + 2 * H1))
            for oc in range(DC):
                for fc in range(DC):
                    last = nc.tensor.transpose(bank[4][:, oc * D + fc * P:oc * D + (fc + 1) * P], w[:, fc, oc * P:(oc + 1) * P], k.ident[:, :])
            last.then_inc(wt_ps, 1)
            pe.wait_ge(wt_ok, 1)
            for fc in range(DC):
                for oc in range(DC):
                    last = nc.tensor.matmul(bank[5][:, fc * 2 * H1:(fc + 1) * 2 * H1], wT[:, oc, fc * P:(fc + 1) * P], ablk[:, oc, :],
                                            start=(oc == 0), stop=(oc == DC - 1))
            last.then_inc(v_ps, 1)
            pe.wait_ge(v_ok, 1)
            norm.t_ps.start(pe)
            xt_ps.start(pe)

            def body(t, u):
                norm.transpose(pe, t, u)
                norm.t_ok.done(pe, t)
                g_ok.slot(pe, t)
                for c in range(DC):
                    last = nc.tensor.matmul(bank[2 + u][:, 0:W], norm.xT[:, u, c * P:(c + 1) * P], w[:, c, :], start=(c == 0), stop=(c == DC - 1))
                last.then_inc(xt_ps.sem, 1)
            tiles(pe, NT, 2, body)


SPARE = 2 + route_tiles(E1, 2) % 2
T1 = route_tiles(E1, 2) + route_tiles(E1, 2) % 2
MC = F1 // P
XS, WS, HS = 64.0, 256.0, 64.0


def route1(nc, a, k):
    with Stage(nc, "route1") as s:
        bank = s.banks()
        norm = Norm(nc, s, k, bank[0:2])
        route = k.route1
        route.work_in(s, bank)
        wr, br = s.sb("router", [P, DC, E1]), s.sb("router_bias", [P, E1])
        st2, mean2, rstd2, var2, sd2, tmp2 = s.sb("stats2", [P, NT, 6]), *(s.sb(n, [P, NT]) for n in ("mean2", "rstd2", "var2", "sd2", "tmp2"))
        ids, out = s.sb("rows", [P, 4, 2], I32), s.sb("out", [P, 4, D])
        mid = s.sb("mid", [P, 4, D])
        loaded, lg_ps, lg_ok = s.sem("loaded"), Count(s, "logits_in_psum", 2), Count(s, "logits_ready", 2)
        var2_ok, sd2_ok, diff_ok, share_ok, row_ok, begun = (s.sem(n) for n in ("var2_ready", "sd2_ready", "diff_ready", "share_ready", "row_ready", "scatters_begun"))
        scattered = [s.sem(f"scattered{u}") for u in range(4)]
        mid_ok = s.sem("mid_ready")
        saved = s.sem("x_saved")
        block = s.block()

        @block.gpsimd
        def _(pool):
            route.pool()

            def scatter(i, u):
                t = i * 4 + u
                m = P if not isinstance(t, int) or t < NT - 1 else TAIL
                pool.wait_ge(row_ok, t + 1)
                pool.sem_inc(begun, 1)
                for j in range(2):
                    nc.gpsimd.indirect_dma_start(k.xs1, bass.IndirectOffsetOnAxis(ids[0:m, u, j:j + 1], 0), out[0:m, u, :], None).then_inc(scattered[u], 16)
            rounds(pool, NT, 4, scatter)
            for u in range(4):
                pool.wait_ge(scattered[u], 32 * ((NT - u + 3) // 4))

        @block.sync
        def _(sp):
            sp.dma_start(wr[:, :, :], a["L1_ffn_Wr"].rearrange("(c p) e -> p c e", p=P)).then_inc(loaded, 16)
            sp.dma_start(br[:, :], a["L1_ffn_br"].rearrange("(o e) -> o e", o=1).broadcast_to([P, E1])).then_inc(loaded, 16)
            sp.dma_start(k.x3.rearrange("(t p) f -> p t f", p=P), k.x[:, :, :]).then_inc(saved, 16)
            sp.wait_ge(saved, 16)

        @block.scalar
        def _(act):
            norm.root(act)
            tiles(act, NT, 2, lambda t, u: norm.keep(act, t, u, lg_ps))
            act.wait_ge(var2_ok, 1)
            nc.scalar.activation(sd2[:, :], var2[:, :], ACT.Sqrt).then_inc(sd2_ok, 1)
            act.wait_ge(diff_ok, 1)
            nc.scalar.activation(k.share[1][:, :], k.share[1][:, :], ACT.Exp).then_inc(share_ok, 1)

        @block.vector
        def _(v):
            ch = Chain(v, norm.dve)
            norm.statistics(v, ch)
            v.wait_ge(loaded, 32)
            lg_ok.start(v)

            def logits(t, u):
                lg_ps.done(v, t)
                nc.vector.tensor_tensor(col(route.logits, t), bank[2 + u][:, 0:E1], br[:, :], ALU.add).then_inc(lg_ok.sem, 1)

            def normalise(t, u):
                norm.normalise(v, t, u)
                norm.xn_ok.done(v, t)
                nc.vector.bn_stats(col(st2, t), norm.xn[:, u, :]).then_inc(mid_ok, 1)
            normalise(0, 0)
            with v.Fori(0, (NT - 1) // 2) as i:
                for u in range(2):
                    normalise(i * 2 + u + 1, 1 - u)
                    logits(i * 2 + u, u)
            logits(NT - 1, 0)
            lg_ok.done(v, NT - 1)
            v.wait_ge(mid_ok, NT)
            me, ve, mo, vo = (st2[:, :, i] for i in (1, 2, 4, 5))
            tmp, var, mean = tmp2[:, :], var2[:, :], mean2[:, :]
            moments(nc, ch, me, ve, mo, vo, mean, var, tmp)
            v.sem_inc(var2_ok, 1)
            v.wait_ge(sd2_ok, 1)
            rsqrt_newton(nc, ch, rstd2[:, :], tmp, var, sd2[:, :])
            route.vector(v, ch)
            ch.link(nc.vector.tensor_tensor(k.share[1][:, :], route.best[1][:, :], route.best[0][:, :], ALU.subtract))
            v.sem_inc(diff_ok, 1)
            v.wait_ge(share_ok, 1)
            ch.link(nc.vector.tensor_scalar(k.share[0][:, :], k.share[1][:, :], 1.0, None, ALU.add))
            ch.link(nc.vector.reciprocal(k.share[0][:, :], k.share[0][:, :]))
            ch.link(nc.vector.tensor_tensor(k.share[1][:, :], k.share[1][:, :], k.share[0][:, :], ALU.mult))
            c0 = NT

            def send(i, u):
                t = i * 4 + u
                if not isinstance(i, int) or i:
                    v.wait_ge(scattered[u], i * 32)
                nc.vector.tensor_scalar(mid[:, u, :], col(k.x, t), col(norm.mean, t), col(norm.rstd, t), ALU.subtract, ALU.mult).then_inc(mid_ok, 1)
                for j in range(2):
                    nc.vector.tensor_copy(ids[:, u, j:j + 1], col(route.place[j], t))
                v.wait_ge(mid_ok, NT + 1 + t)
                nc.vector.tensor_scalar(out[:, u, :], mid[:, u, :], col(mean2, t), col(rstd2, t), ALU.subtract, ALU.mult).then_inc(row_ok, 1)
            rounds(v, NT, 4, send)

        @block.tensor
        def _(pe):
            pe.wait_ge(loaded, 32)
            norm.t_ps.start(pe)
            lg_ps.start(pe)

            def body(t, u):
                norm.transpose(pe, t, u)
                norm.t_ok.done(pe, t)
                lg_ok.slot(pe, t)
                for c in range(DC):
                    last = nc.tensor.matmul(bank[2 + u][:, 0:E1], norm.xT[:, u, c * P:(c + 1) * P], wr[:, c, :], start=(c == 0), stop=(c == DC - 1))
                last.then_inc(lg_ps.sem, 1)
            tiles(pe, NT, 2, body)
            route.tensor(pe)


def experts1(nc, a, k):
    with Stage(nc, "moe1") as s:
        bank = s.banks()
        route, DVE, PE, SC = k.route1, mybir.EngineType.DVE, mybir.EngineType.PE, mybir.EngineType.Activation
        w1 = [s.sb(f"w1_{n}", [P, DC, E1 * F1], F16) for n in ("high", "low")]
        w2 = [s.sb(f"w2_{n}", [P, MC, E1 * D], F16) for n in ("high", "low")]
        stage = s.sb("stage", [P, 2, 2048])
        lg, lb, b1 = s.sb("gain_T", [P, DC, E1]), s.sb("shift_T", [P, DC, E1]), s.sb("b1_T", [P, E1, MC])
        rows8, rowsb = s.sb("gain_rows", [E1, 2, D]), s.sb("b1_rows", [E1 * MC, P])
        b2 = s.sb("b2", [P, E1, D])
        xi, xe = s.sb("tile", [P, 2, D]), s.sb("tile_T", [P, 2, D])
        xh = [s.sb(f"x_{n}", [P, 2, DC, P], F16) for n in ("high", "low")]
        hg = s.sb("hidden", [P, 2, MC * P])
        hh = [s.sb(f"hidden_{n}", [P, 2, MC * P], F16) for n in ("high", "low")]
        y = s.sb("y", [P, 2, D])
        small, small_ps, small_ok = s.sem("small_loaded"), s.sem("small_in_psum"), s.sem("small_ready")
        staged = [s.sem(f"staged{u}") for u in range(2)]
        high_ok, low_ok = Count(s, "high_ready", 2), Count(s, "low_ready", 2)
        tile_in, out_ok = [s.sem(f"tile_loaded{u}") for u in range(2)], Landed(s, "y_written", 2)
        x_ps, xe_ok, xs_ok, y_ps, y_ok = (Count(s, n, 2) for n in (
            "x_in_psum", "xe_ready", "x_split", "y_in_psum", "y_ready"))
        h_ps, hg_ok, hs_ok = Count(s, "hidden_in_psum", 4), Count(s, "hidden_ready", 4), Count(s, "hidden_split", 4)
        xhi_ok, hhi_ok = Count(s, "x_high", 2), Count(s, "hidden_high", 4)
        PIECES = 2 * E1

        block = s.block()

        def part(n):
            e = n % E1
            if n < E1:
                return [t[:, :, e * F1:(e + 1) * F1] for t in w1], DC, a["L1_ffn_W1"][e].rearrange("(c p) h -> p c h", p=P)
            return [t[:, :, e * D:(e + 1) * D] for t in w2], MC, a["L1_ffn_W2"][e].rearrange("(c p) h -> p c h", p=P)

        @block.sync
        def _(sp):
            sp.dma_start(rows8[:, 0, :], a["L1_ffn_ln_g"]).then_inc(small, 16)
            sp.dma_start(rows8[:, 1, :], a["L1_ffn_ln_b"]).then_inc(small, 16)
            sp.dma_start(rowsb[:, :], a["L1_ffn_b1"].rearrange("e (m p) -> (e m) p", p=P)).then_inc(small, 16)
            v = a["L1_ffn_b2"].rearrange("e h -> (e h)").rearrange("(o n) -> o n", o=1)
            sp.dma_start(flat(b2[:, :, :]), v.broadcast_to([P, v.shape[1]])).then_inc(small, 16)
            for n in range(PIECES):
                low_ok.slot(sp, n)
                _, m, src = part(n)
                sp.dma_start(stage[:, n % 2, :].rearrange("p (c h) -> p c h", c=m), src).then_inc(staged[n % 2], 16)
            out_ok.start(sp)
            with sp.Fori(0, T1 // 2) as i:
                for u in range(2):
                    y_ok.done(sp, i * 2 + u)
                    sp.dma_start(rows(k.ys1, (i * 2 + u) * P, P), y[:, u, :]).then_inc(out_ok.sems[u], 16)
            out_ok.all(sp, T1)

        @block.gpsimd
        def _(pool):
            def load(i, u):
                x_ps.slot(pool, i * 2 + u)
                pool.dma_start(xi[:, u, :], rows(k.xs1, (i * 2 + u) * P, P)).then_inc(tile_in[u], 16)
            turns(pool, T1 + 2, 2, load)

        @block.scalar
        def _(act):
            high_ok.start(act)
            for n in range(PIECES):
                to, m, _ = part(n)
                act.wait_ge(staged[n % 2], 16 * (n // 2 + 1))
                nc.scalar.activation(to[0], stage[:, n % 2, :].rearrange("p (c h) -> p c h", c=m), ACT.Copy, scale=WS).then_inc(high_ok.sem, 1)
            act.wait_ge(small_ok, 1)
            xe_ok.start(act)
            hg_ok.start(act)

            def turn(t, u, e):
                x_ps.done(act, t)
                xs_ok.slot(act, t)
                for c in range(DC):
                    last = nc.scalar.activation(xe[:, u, c * P:(c + 1) * P], bank[4 + u][:, c * P:(c + 1) * P], ACT.Identity,
                                                scale=col(lg[:, c, :], e), bias=col(lb[:, c, :], e))
                last.then_inc(xe_ok.sem, 1)

            def gelu(t, u, e):
                for q in range(2):
                    h_ps.done(act, 2 * t + q)
                    hs_ok.slot(act, 2 * t + q)
                    for m in range(4 * q, 4 * q + 4):
                        last = nc.scalar.activation(hg[:, u, m * P:(m + 1) * P], bank[2 * u + q][:, (m - 4 * q) * P:(m - 4 * q + 1) * P], ACT.Gelu,
                                                    scale=1.0 / (XS * WS), bias=col(b1[:, :, m], e))
                    last.then_inc(hg_ok.sem, 1)
            e = registers(nc, SC, route.expert[0:1, 0:2], E1 - 1)
            turn(0, 0, e[0])
            turn(1, 1, e[1])
            gelu(0, 0, e[0])
            with act.Fori(0, T1 // 2) as i:
                e = registers(nc, SC, route.expert[0:1, bass.ds(i * 2, 4)], E1 - 1)
                for u in range(2):
                    turn(i * 2 + 2 + u, u, e[2 + u])
                    gelu(i * 2 + 1 + u, 1 - u, e[1 + u])

        @block.vector
        def _(v):
            low_ok.start(v)
            v.wait_ge(small, 64)
            v.wait_ge(small_ps, 1)
            for j, t in ((0, lg), (1, lb)):
                nc.vector.tensor_scalar(t[:, :, :], bank[7][:, j * DC * E1:(j + 1) * DC * E1].rearrange("p (c e) -> p c e", c=DC), XS, None, ALU.mult)
            nc.vector.tensor_copy(b1[:, :, :], bank[7][:, 4 * E1:4 * E1 + E1 * MC].rearrange("p (e m) -> p e m", e=E1)).then_inc(small_ok, 1)
            for n in range(PIECES):
                to, m, _ = part(n)
                high_ok.done(v, n)
                nc.vector.scalar_tensor_tensor(to[1], stage[:, n % 2, :].rearrange("p (c h) -> p c h", c=m), WS, to[0], ALU.mult, ALU.subtract).then_inc(low_ok.sem, 1)
            for n in (xs_ok, xhi_ok, hs_ok, hhi_ok, y_ok):
                n.start(v)

            def split_x(t, u):
                xe_ok.done(v, t)
                h_ps.slot(v, 2 * t + 1)
                f = xe[:, u, :].rearrange("p (c q) -> p c q", c=DC)
                nc.vector.tensor_copy(xh[0][:, u], f).then_inc(xhi_ok.sem, 1)
                xhi_ok.done(v, t)
                nc.vector.tensor_tensor(xh[1][:, u], f, xh[0][:, u], ALU.subtract).then_inc(xs_ok.sem, 1)

            def split_h(t, u):
                for q in range(2):
                    hg_ok.done(v, 2 * t + q)
                    if q == 0:
                        y_ps.slot(v, t)
                    f = hg[:, u, q * 512:(q + 1) * 512]
                    nc.vector.tensor_scalar(hh[0][:, u, q * 512:(q + 1) * 512], f, HS, None, ALU.mult).then_inc(hhi_ok.sem, 1)
                    hhi_ok.done(v, 2 * t + q)
                    nc.vector.scalar_tensor_tensor(hh[1][:, u, q * 512:(q + 1) * 512], f, HS, hh[0][:, u, q * 512:(q + 1) * 512], ALU.mult, ALU.subtract).then_inc(hs_ok.sem, 1)

            def result(i, u, e):
                y_ps.done(v, i * 2 + u)
                out_ok.slot(v, i, u)
                nc.vector.scalar_tensor_tensor(y[:, u, :], bank[6 + u][:, 0:D], 1.0 / (HS * WS), col(b2, e), ALU.mult, ALU.add).then_inc(y_ok.sem, 1)
            split_x(0, 0)
            split_x(1, 1)
            split_h(0, 0)
            with v.Fori(0, T1 // 2) as i:
                e = registers(nc, DVE, route.expert[0:1, bass.ds(i * 2, 2)], E1 - 1)
                for u in range(2):
                    split_x(i * 2 + 2 + u, u)
                    split_h(i * 2 + 1 + u, 1 - u)
                    result(i, u, e[u])

        @block.tensor
        def _(pe):
            pe.wait_ge(small, 64)
            for j in range(2):
                for c in range(DC):
                    o = (j * DC + c) * E1
                    nc.tensor.transpose(bank[7][:, o:o + E1], rows8[:, j, c * P:(c + 1) * P], k.ident[0:E1, 0:E1])
            nc.tensor.transpose(bank[7][:, 4 * E1:4 * E1 + E1 * MC], rowsb[:, :], k.ident[0:E1 * MC, 0:E1 * MC]).then_inc(small_ps, 1)
            pe.wait_ge(small_ok, 1)
            for n in (x_ps, h_ps, y_ps):
                n.start(pe)
            passes = ((0, 0), (0, 1), (1, 0))

            def turn(i, u):
                pe.wait_ge(tile_in[u], (i + 1) * 16)
                xe_ok.slot(pe, i * 2 + u)
                for c in range(DC):
                    last = nc.tensor.transpose(bank[4 + u][:, c * P:(c + 1) * P], xi[:, u, c * P:(c + 1) * P], k.ident[:, :])
                last.then_inc(x_ps.sem, 1)

            def up(t, u, e):
                xs_ok.done(pe, t)
                for q in range(2):
                    hg_ok.slot(pe, 2 * t + q)
                    for m in range(4 * q, 4 * q + 4):
                        o = (m - 4 * q) * P
                        for n, (pw, px) in enumerate(passes):
                            for c in range(DC):
                                last = nc.tensor.matmul(bank[2 * u + q][:, o:o + P], w1[pw][:, c, bass.ds(e * F1 + m * P, P)], xh[px][:, u, c, :],
                                                        start=(n == 0 and c == 0), stop=(n == 2 and c == DC - 1))
                    last.then_inc(h_ps.sem, 1)

            def down(t, u, e):
                y_ok.slot(pe, t)
                for q in range(2):
                    hs_ok.done(pe, 2 * t + q)
                    for m in range(4 * q, 4 * q + 4):
                        for n, (pw, ph) in enumerate(passes):
                            last = nc.tensor.matmul(bank[6 + u][:, 0:D], hh[ph][:, u, m * P:(m + 1) * P], w2[pw][:, m, bass.ds(e * D, D)],
                                                    start=(m == 0 and n == 0), stop=(m == MC - 1 and n == 2))
                last.then_inc(y_ps.sem, 1)
            low_ok.done(pe, PIECES - 1)
            e = registers(nc, PE, route.expert[0:1, 0:2], E1 - 1)
            turn(0, 0)
            turn(0, 1)
            up(0, 0, e[0])
            with pe.Fori(0, T1 // 2) as i:
                e = registers(nc, PE, route.expert[0:1, bass.ds(i * 2, 3)], E1 - 1)
                for u in range(2):
                    turn(i + 1, u)
                    up(i * 2 + 1 + u, 1 - u, e[1 + u])
                    down(i * 2 + u, u, e[u])


def combine1(nc, a, k):
    with Stage(nc, "last") as s:
        ids = s.sb("rows", [P, 4, 2], I32)
        x, y = s.sb("x", [P, 4, D]), s.sb("y", [P, 4, 2, D])
        sent = [s.sem(f"x_loaded{u}") for u in range(4)]
        arrived = [s.sem(f"arrived{u}") for u in range(4)]
        ids_ok, begun, half, out_ok, free = s.sem("ids_ready"), s.sem("gathers_begun"), s.sem("half"), Count(s, "out_ready", 4), Landed(s, "out_stored", 4)
        block = s.block()

        def size(t):
            return P if not isinstance(t, int) or t < NT - 1 else TAIL

        @block.gpsimd
        def _(pool):
            def gather(t, u):
                pool.wait_ge(ids_ok, t + 1)
                pool.sem_inc(begun, 1)
                m = size(t)
                for j in range(2):
                    nc.gpsimd.indirect_dma_start(y[0:m, u, j, :], None, k.ys1, bass.IndirectOffsetOnAxis(ids[0:m, u, j:j + 1], 0)).then_inc(arrived[u], 16)
            tiles(pool, NT, 4, gather)

        @block.scalar
        def _(act):
            def load(i, u):
                free.slot(act, i, u)
                act.dma_start(x[:, u, :], rows(k.x3, (i * 4 + u) * P, P)).then_inc(sent[u], 16)
            turns(act, NT, 4, load)

        @block.sync
        def _(sp):
            free.start(sp)

            def save(t, u):
                out_ok.done(sp, t)
                m = size(t)
                sp.dma_start(rows(a["out"], t * P, m), x[0:m, u, :]).then_inc(free.sems[u], 16)
            tiles(sp, NT, 4, save)
            free.all(sp, NT)

        @block.vector
        def _(v):
            out_ok.start(v)

            def address(t, u):
                for j in range(2):
                    last = nc.vector.tensor_copy(ids[:, u, j:j + 1], col(k.route1.place[j], t))
                last.then_inc(ids_ok, 1)

            def add(i, u):
                t = i * 4 + u
                m = size(t)
                v.wait_ge(arrived[u], (i + 1) * 32)
                v.wait_ge(sent[u], (i + 1) * 16)
                nc.vector.scalar_tensor_tensor(x[0:m, u, :], y[0:m, u, 0, :], col(k.share[0], t)[0:m], x[0:m, u, :], ALU.mult, ALU.add).then_inc(half, 1)
                v.wait_ge(half, t + 1)
                nc.vector.scalar_tensor_tensor(x[0:m, u, :], y[0:m, u, 1, :], col(k.share[1], t)[0:m], x[0:m, u, :], ALU.mult, ALU.add).then_inc(out_ok.sem, 1)
            for u in range(4):
                address(u, u)
            with v.Fori(0, NT // 4 - 1) as i:
                for u in range(4):
                    add(i, u)
                    address(i * 4 + 4 + u, u)
            for u in range(4):
                add(NT // 4 - 1, u)
            address(NT - 1, 0)
            add(NT // 4, 0)


def store(nc, a, k):
    with Stage(nc, "store") as s:
        st = s.sem("stored")
        block = s.block()

        @block.sync
        def _(sp):
            sp.dma_start(a["out"][0:(NT - 1) * P, :].rearrange("(t p) f -> p t f", p=P), k.x[:, 0:NT - 1, :]).then_inc(st, 16)
            sp.dma_start(a["out"][(NT - 1) * P:N, :], k.x[0:TAIL, NT - 1, :]).then_inc(st, 16)
            sp.wait_ge(st, 32)


class Kept:
    pass


def build(nc, a, stop=99):
    k = Kept()
    k.span_tab = nc.dram_tensor("span_tab", [2, C * NT], F32).ap()
    k.src_tab = nc.dram_tensor("src_tab", [NPAD * R, H0], F32).ap()
    k.item_tab = nc.dram_tensor("item_tab", [3, -(-ITEMS_MAX // P) * P], F32).ap()
    k.h_tab = nc.dram_tensor("h_tab", [NPAD * R, D], F32).ap()
    k.xs0 = nc.dram_tensor("sorted0", [route_tiles(E0, 1) * P, D], F32).ap()
    k.ys0 = nc.dram_tensor("results0", [route_tiles(E0, 1) * P, D], F32).ap()
    k.xs1 = nc.dram_tensor("sorted1", [(T1 + 2) * P, D], F32).ap()
    k.ys1 = nc.dram_tensor("results1", [T1 * P, D], F32).ap()
    k.x3 = nc.dram_tensor("x3", [NPAD, D], F32).ap()
    k.g_tab = nc.dram_tensor("g_tab", [NPAD, D + 2 * H1], F32).ap()
    k.l_tab = nc.dram_tensor("l_tab", [NPAD, H1], F32).ap()
    k.sorted = [k.xs0, k.xs1]
    with Stage(nc, "all") as s:
        k.iota, k.ident, k.before, k.ones = (s.sb(n, [P, P]) for n in ("iota", "ident", "before", "ones"))
        k.col = s.sb("col", [P, 1])
        k.share = [s.sb(f"share{j}", [P, NT]) for j in range(2)]
        k.route1 = Route(nc, s, k, E1, 2, SPARE)
        with Stage(nc, "nodes") as n:
            k.x = n.sb("x", [P, NT, D])
            k.dst_i, k.src_i = n.sb("dst_i", [P, NT], I32), n.sb("src_i", [P, NT], I32)
            with Stage(nc, "gnn0") as g:
                k.edge_row = g.sb("edge_row", [P, NT * C], I32)
                k.dst_f = g.sb("dst_f", [P, NT * C])
                k.item_i = g.sb("item_i", [1, 2, ITEMS_MAX], I32)
                k.item_base = g.sb("item_base", [P, ITEMS_MAX])
                k.w = g.sb("edge_w", [P, NPAD])
                with Stage(nc, "scores") as sc:
                    k.score = sc.sb("score", [P, NPAD])
                    with Stage(nc, "att") as w:
                        k.wT = w.sb("wT", [P, DC, R * D])
                        k.dst_half, k.type_f = w.sb("dst_half", [P, NT, R * H0]), w.sb("type_f", [P, NT * C])
                        k.relation = w.sb("relation", [P, R * H0])
                        prepare(nc, a, k)
                        list_items(nc, a, k)
                        edge_scores(nc, a, k)
                    edge_weights(nc, a, k)
                aggregate(nc, a, k)
            if stop == 1:
                return store(nc, a, k)
            moe0(nc, a, k)
            if stop == 2:
                return store(nc, a, k)
            attend1(nc, a, k)
            if stop == 3:
                return store(nc, a, k)
            route1(nc, a, k)
        experts1(nc, a, k)
        combine1(nc, a, k)


_INS = ["x", "src", "dst", "edge_type_8", "L0_gnn_W", "L0_gnn_attn_src", "L0_gnn_attn_dst", "L0_ffn_router_w",
        "L0_ffn_router_b", "L0_ffn_W1", "L0_ffn_b1", "L0_ffn_W2", "L0_ffn_b2", "L1_gnn_weight", "L1_gnn_attn_l",
        "L1_gnn_attn_r", "L1_ffn_Wr", "L1_ffn_br", "L1_ffn_ln_g", "L1_ffn_ln_b", "L1_ffn_W1", "L1_ffn_b1",
        "L1_ffn_W2", "L1_ffn_b2"]


def kernel(**inputs):
    import numpy as _np
    import concourse.bacc as _bacc
    from concourse import mybir as _mybir
    from concourse.bass_utils import run_bass_kernel_spmd as _run

    nc = _bacc.Bacc("TRN2", target_bir_lowering=False, num_devices=1)
    arrays, aps = {}, {}
    for name in _INS:
        array = _np.ascontiguousarray(inputs[name])
        arrays[f"in_{name}_dram"] = array
        aps[name] = nc.dram_tensor(f"in_{name}_dram", array.shape, _mybir.dt.from_np(array.dtype), kind="ExternalInput").ap()
    aps["out"] = nc.dram_tensor("out_0_dram", (N, D), F32, kind="ExternalOutput").ap()
    build(nc, aps)
    r = _run(nc, [arrays], core_ids=[0])
    return r.results[0]["out_0_dram"]
```

```python
import concourse.bass as bass
from concourse import mybir
from contextlib import ExitStack

F32 = mybir.dt.float32
I32 = mybir.dt.int32
F16 = mybir.dt.float16
BF16 = mybir.dt.bfloat16
ALU = mybir.AluOpType
ACT = mybir.ActivationFunctionType
AX = mybir.AxisListType

P = 128
N = 6250
D = 256
DC = D // P
NT = -(-N // P)
TAIL = N - (NT - 1) * P
NPAD = NT * P
E = 100000
C = 16
CE = E // C
R, H0, HD0 = 8, 8, 32
H1, HD1 = 4, 64
E0, F0 = 32, 64
E1, F1 = 8, 1024
EPS = 1e-5
ITEMS = 832
U = 8
UG = 17
BATCH = [0, 5, 9, 13, 17]
BM = 5
ITEMS_MAX = NT * UG + BATCH[2]
assert CE == N and ITEMS_MAX >= ITEMS >= C * NT + NT - 1 and ITEMS % U == 0


class Chain:

    def __init__(self, eng, sem):
        self.eng, self.sem, self.n = eng, sem, 0

    def link(self, ins):
        ins.then_inc(self.sem, 1)
        self.n = self.n + 1
        self.eng.wait_ge(self.sem, self.n)


class Count:

    def __init__(self, stage, name, ahead):
        self.sem, self.ahead = stage.sem(name), ahead

    def start(self, eng):
        eng.sem_inc(self.sem, self.ahead)

    def done(self, eng, t):
        eng.wait_ge(self.sem, t + 1 + self.ahead)

    def slot(self, eng, t):
        eng.wait_ge(self.sem, t + 1)


class Landed:

    def __init__(self, stage, name, slots, dmas=1):
        self.sems, self.step = [stage.sem(f"{name}{u}") for u in range(slots)], 16 * dmas

    def start(self, eng):
        for sem in self.sems:
            eng.sem_inc(sem, self.step)

    def slot(self, eng, i, u):
        eng.wait_ge(self.sems[u], (i + 1) * self.step)

    def all(self, eng, n):
        for u, sem in enumerate(self.sems):
            eng.wait_ge(sem, ((n - u + len(self.sems) - 1) // len(self.sems) + 1) * self.step)


class Stage:

    def __init__(self, nc, name):
        self.nc, self.name, self.ctx, self.sems = nc, name, ExitStack(), []

    def __enter__(self):
        return self

    def __exit__(self, *a):
        self.ctx.close()
        if self.sems:
            self.nc.clear_and_free_semaphores(self.sems)
            self.nc.all_engine_barrier()

    def sb(self, name, shape, dt=F32):
        return self.ctx.enter_context(self.nc.sbuf_tensor(f"{self.name}_{name}", shape, dt))

    def banks(self, n=8):
        return [self.ctx.enter_context(self.nc.psum_tensor(f"{self.name}_bank{i}", [P, 512], F32)) for i in range(n)]

    def sem(self, name):
        self.sems.append(self.nc.alloc_semaphore(f"{self.name}_{name}"))
        return self.sems[-1]

    def block(self):
        return self.ctx.enter_context(self.nc.Block())


def col(ap, start, size=1):
    out = ap[:, start:start + size] if isinstance(start, int) else ap[:, bass.ds(start, size)]
    if size == 1 and len(ap.shape) > 2:
        names = " ".join("abcd"[: len(ap.shape) - 2])
        out = out.rearrange(f"p o {names} -> p (o {names})")
    return out


def flat(ap):
    names = " ".join("abcd"[: len(ap.shape) - 1])
    return ap.rearrange(f"p {names} -> p ({names})")


def rows(ap, start, size):
    return ap[start:start + size, :] if isinstance(start, int) else ap[bass.ds(start, size), :]


def tiles(eng, n, unroll, body, base=0):
    with eng.Fori(0, n // unroll) as i:
        for u in range(unroll):
            body(i * unroll + u, u)
    for t in range(n - n % unroll, n):
        body(t, t % unroll)


def turns(eng, n, unroll, body):
    with eng.Fori(0, n // unroll) as i:
        for u in range(unroll):
            body(i, u)
    for u in range(n % unroll):
        body(n // unroll, u)


def rounds(eng, n, unroll, body):
    for u in range(unroll):
        body(0, u)
    with eng.Fori(1, n // unroll) as i:
        for u in range(unroll):
            body(i, u)
    for u in range(n % unroll):
        body(n // unroll, u)


class Norm:

    def __init__(self, nc, s, k, banks, known=None):
        self.nc, self.k, self.banks = nc, k, banks
        self.mean, self.rstd = known or (s.sb("mean", [P, NT]), s.sb("rstd", [P, NT]))
        self.tmp, self.var, self.sd = (s.sb(n, [P, NT]) for n in ("tmp", "var", "sd"))
        self.xn = s.sb("xn", [P, 2, D])
        self.xT = s.sb("xnT", [P, 2, D])
        self.dve = s.sem("dve")
        self.var_ok, self.sd_ok = s.sem("var_ready"), s.sem("sd_ready")
        self.xn_ok = Count(s, "xn_ready", 2)
        self.t_ps = Count(s, "xnT_in_psum", 2)
        self.t_ok = Count(s, "xnT_ready", 2)

    def tile_stats(self, v, ch, t0, t1):
        with v.Fori(0, (t1 - t0) // 6) as i:
            for u in range(6):
                self.nc.vector.bn_stats(col(self.k.stats, i * 6 + t0 + u), col(self.k.x, i * 6 + t0 + u)).then_inc(self.dve, 1)
        for t in range(t1 - (t1 - t0) % 6, t1):
            self.nc.vector.bn_stats(col(self.k.stats, t), col(self.k.x, t)).then_inc(self.dve, 1)
        ch.n = ch.n + t1 - t0
        v.wait_ge(self.dve, ch.n)

    def statistics(self, v, ch):
        nc = self.nc
        me, ve, mo, vo = (self.k.stats[:, :, i] for i in (1, 2, 4, 5))
        tmp, var, mean = self.tmp[:, :], self.var[:, :], self.mean[:, :]
        moments(nc, ch, me, ve, mo, vo, mean, var, tmp)
        v.sem_inc(self.var_ok, 1)
        v.wait_ge(self.sd_ok, 1)
        rsqrt_newton(nc, ch, self.rstd[:, :], tmp, var, self.sd[:, :])
        self.xn_ok.start(v)

    def root(self, act):
        act.wait_ge(self.var_ok, 1)
        self.nc.scalar.activation(self.sd[:, :], self.var[:, :], ACT.Sqrt).then_inc(self.sd_ok, 1)
        self.t_ok.start(act)

    def normalise(self, v, t, u):
        self.t_ps.slot(v, t)
        self.nc.vector.tensor_scalar(self.xn[:, u, :], col(self.k.x, t), col(self.mean, t), col(self.rstd, t),
                                     ALU.subtract, ALU.mult).then_inc(self.xn_ok.sem, 1)

    def transpose(self, pe, t, u):
        self.xn_ok.done(pe, t)
        self.t_ok.slot(pe, t)
        for c in range(DC):
            last = self.nc.tensor.transpose(self.banks[u][:, c * P:(c + 1) * P], self.xn[:, u, c * P:(c + 1) * P], self.k.ident[:, :])
        last.then_inc(self.t_ps.sem, 1)

    def feed(self, pe, product):
        self.transpose(pe, 0, 0)
        with pe.Fori(0, (NT - 1) // 2) as i:
            for u in range(2):
                self.transpose(pe, i * 2 + u + 1, 1 - u)
                product(i * 2 + u, u)
        product(NT - 1, 0)

    def lead(self, v, normalise, after):
        normalise(0, 0)
        normalise(1, 1)
        with v.Fori(0, (NT - 3) // 2) as i:
            for u in range(2):
                normalise(i * 2 + u + 2, u)
                after(i, u)
        normalise(NT - 1, 0)
        after((NT - 3) // 2, 0)
        after((NT - 3) // 2, 1)
        after((NT - 1) // 2, 0)

    def keep(self, act, t, u, used):
        self.t_ps.done(act, t)
        used.slot(act, t)
        self.nc.scalar.activation(self.xT[:, u, :], self.banks[u][:, 0:D], ACT.Copy).then_inc(self.t_ok.sem, 1)


def moments(nc, ch, me, ve, mo, vo, mean, var, tmp):
    ch.link(nc.vector.tensor_tensor(tmp, me, mo, ALU.add))
    ch.link(nc.vector.tensor_scalar(mean, tmp, 0.5, None, ALU.mult))
    ch.link(nc.vector.tensor_tensor(tmp, me, mo, ALU.subtract))
    ch.link(nc.vector.tensor_tensor(tmp, tmp, tmp, ALU.mult))
    ch.link(nc.vector.tensor_scalar(tmp, tmp, 0.25, EPS, ALU.mult, ALU.add))
    ch.link(nc.vector.tensor_tensor(var, ve, vo, ALU.add))
    ch.link(nc.vector.scalar_tensor_tensor(var, var, 1.0 / D, tmp, ALU.mult, ALU.add))


def rsqrt_newton(nc, ch, out, tmp, var, sd):
    ch.link(nc.vector.reciprocal(out, sd))
    ch.link(nc.vector.tensor_tensor(tmp, out, out, ALU.mult))
    ch.link(nc.vector.tensor_tensor(tmp, tmp, var, ALU.mult))
    ch.link(nc.vector.tensor_scalar(tmp, tmp, -0.5, 1.5, ALU.mult, ALU.add))
    ch.link(nc.vector.tensor_tensor(out, out, tmp, ALU.mult))


def prepare(nc, a, k):
    with Stage(nc, "prep") as s:
        names = ("src", "dst", "edge_type_8")
        ints = [k.dst_rows[0:NT, j * C * P:(j + 1) * C * P].rearrange("g (c p) -> g c p", c=C) for j in range(3)]
        floats = [k.score[0:NT, j * C * P:(j + 1) * C * P].rearrange("g (c p) -> g c p", c=C) for j in range(3)]
        idx = k.w[:, 0:3 * NT * C].rearrange("p (j q) -> p j q", j=3)
        iota_i, col_i = s.sb("iota_i", [P, P], I32), s.sb("col_i", [P, 1], I32)
        wn = s.sb("w_natural", [P, R, DC, D])
        ablk = s.sb("attn_blocks", [P, DC, 2 * H0])
        vst = s.sb("score_weights", [P, DC, 2 * R * H0])
        scores = s.sb("scores", [P, 2, R * H0])
        first = s.sb("first_last", [NT, 2, C])
        first_i = s.sb("first_last_i", [NT, 2, C], I32)
        bank = s.banks()
        norm = Norm(nc, s, k, bank[0:2], k.moments0)
        rel_i = s.sb("relation_i", [P, R, H0], I32)
        cleared, edges, weights = (s.sem(n) for n in ("cleared", "edges_loaded", "weights_loaded"))
        loaded = [s.sem(f"x_loaded{j}") for j in range(4)]
        iotas, consts, edges_f = s.sem("iotas"), s.sem("consts"), s.sem("edges_as_floats")
        wt_ps, wt_free, v_ps, v_ok = (s.sem(n) for n in ("wT_in_psum", "wT_bank_free", "v_in_psum", "v_ready"))
        e_ps, e_free = s.sem("edges_in_psum"), s.sem("edges_bank_free")
        sc_ps, sc_ok, stored = Count(s, "scores_in_psum", 2), Count(s, "scores_ready", 2), Landed(s, "scores_stored", 2)
        spans, spans_st = s.sem("spans_ready"), s.sem("spans_written")
        block = s.block()

        @block.gpsimd
        def _(pool):
            nc.gpsimd.memset(k.x[:, NT - 1, :], 0.0).then_inc(cleared, 1)
            nc.gpsimd.memset(ablk[:, :, :], 0.0).then_inc(cleared, 1)
            for t in ints:
                nc.gpsimd.memset(t[:, :, :], 0).then_inc(cleared, 1)
            nc.gpsimd.iota(iota_i[:, :], [[1, P]], base=0, channel_multiplier=0).then_inc(iotas, 1)
            nc.gpsimd.iota(col_i[:, :], [[0, 1]], base=0, channel_multiplier=1).then_inc(iotas, 1)
            nc.gpsimd.iota(rel_i[:, :, :], [[1, R], [0, H0]], base=0, channel_multiplier=0).then_inc(iotas, 1)

        @block.sync
        def _(sp):
            sp.wait_ge(cleared, 5)
            for t, name in zip(ints, names):
                e = a[name].rearrange("(c e) -> c e", c=C)
                sp.dma_start(t[0:NT - 1, :, :], e[:, 0:(NT - 1) * P].rearrange("c (g p) -> g c p", p=P)).then_inc(edges, 16)
                sp.dma_start(t[NT - 1:NT, :, 0:TAIL], e[:, (NT - 1) * P:].rearrange("c (o p) -> o c p", o=1)).then_inc(edges, 16)
            sp.dma_start(wn[:, :, :, :], a["L0_gnn_W"].rearrange("r (c p) f -> p r c f", p=P)).then_inc(weights, 16)
            with nc.allow_non_contiguous_dma(reason="short vectors onto partitions"):
                for j, name in enumerate(("L0_gnn_attn_src", "L0_gnn_attn_dst")):
                    for h in range(H0):
                        p0 = h * HD0 % P
                        sp.dma_start(ablk[p0:p0 + HD0, h * HD0 // P, j * H0 + h:j * H0 + h + 1],
                                     a[name][h:h + 1, :].rearrange("a b -> b a")).then_inc(weights, 16)
                sp.wait_ge(spans, 1)
                for j in range(2):
                    sp.dma_start(k.span_tab[j:j + 1, :].rearrange("o (c g) -> (o g) c", c=C), first[:, j, :]).then_inc(spans_st, 16)
            stored.start(sp)

            def store(t, u):
                sc_ok.done(sp, t)
                sp.dma_start(rows(k.src_tab.rearrange("(n r) h -> n (r h)", r=R), t * P, P), scores[:, u, :]).then_inc(stored.sems[u], 16)
            tiles(sp, NT, 2, store)
            stored.all(sp, NT)
            sp.wait_ge(spans_st, 32)

        @block.scalar
        def _(act):
            act.wait_ge(cleared, 1)
            for j in range(4):
                t0 = j * (NT - 1) // 4
                t1 = (j + 1) * (NT - 1) // 4
                act.dma_start(k.x[:, t0:t1, :], a["x"][t0 * P:t1 * P, :].rearrange("(t p) f -> p t f", p=P)).then_inc(loaded[j], 16)
            act.dma_start(k.x[0:TAIL, NT - 1, :], a["x"][(NT - 1) * P:N, :]).then_inc(loaded[3], 16)
            norm.root(act)
            tiles(act, NT, 2, lambda t, u: norm.keep(act, t, u, sc_ps))

        @block.vector
        def _(v):
            ch = Chain(v, norm.dve)
            v.wait_ge(iotas, 3)
            ch.link(nc.vector.tensor_copy(k.relation[:, :], rel_i[:, :, :].rearrange("p r h -> p (r h)")))
            ch.link(nc.vector.tensor_copy(k.iota[:, :], iota_i[:, :]))
            ch.link(nc.vector.tensor_copy(k.col[:, :], col_i[:, :]))
            ch.link(nc.vector.memset(k.ones[:, :], 1.0))
            ch.link(nc.vector.tensor_scalar(k.ident[:, :], k.iota[:, :], k.col[:, 0:1], None, ALU.is_equal))
            ch.link(nc.vector.tensor_scalar(k.before[:, :], k.iota[:, :], k.col[:, 0:1], None, ALU.is_gt))
            v.sem_inc(consts, 1)
            for j in range(2):
                v.wait_ge(loaded[j], 16)
                norm.tile_stats(v, ch, j * (NT - 1) // 4, (j + 1) * (NT - 1) // 4)
            v.wait_ge(edges, 96)
            for t, f in zip(ints, floats):
                ch.link(nc.vector.tensor_copy(f[:, :, :], t[:, :, :]))
            v.sem_inc(edges_f, 1)
            ch.link(nc.vector.tensor_copy(first[:, 0, :], floats[1][:, :, 0]))
            ch.link(nc.vector.reduce_max(first[:, 1, :], floats[1][:, :, :], AX.X))
            ch.link(nc.vector.tensor_copy(first_i[:, :, :], first[:, :, :]))
            ch.link(nc.vector.tensor_scalar(first_i[:, :, :], first_i[:, :, :], 7, None, ALU.arith_shift_right))
            nc.vector.tensor_copy(first[:, :, :], first_i[:, :, :]).then_inc(spans, 1)
            for n in range(6):
                j, half = divmod(n, 2)
                v.wait_ge(e_ps, n + 1)
                nc.vector.tensor_copy(idx[:, j, :].rearrange("p (g c) -> p g c", c=C)[:, :, half * 8:half * 8 + 8],
                                      bank[n % 4][:, 0:8 * NT].rearrange("p (c g) -> p g c", c=8)).then_inc(e_free, 1)
            v.wait_ge(e_free, 6)
            nc.vector.scalar_tensor_tensor(k.edge_row[:, :], idx[:, 0, :], float(R), idx[:, 2, :], ALU.mult, ALU.add)
            nc.vector.tensor_copy(k.type_f[:, :], idx[:, 2, :])
            nc.vector.tensor_copy(k.dst_f[:, :], idx[:, 1, :])
            nc.vector.tensor_copy(k.dst_i[:, :], idx[:, 1, :].rearrange("p (g c) -> p g c", c=C)[:, :, 0])
            nc.vector.tensor_copy(k.src_i[:, :], idx[:, 0, :].rearrange("p (g c) -> p g c", c=C)[:, :, 0])
            for j in range(2, 4):
                v.wait_ge(loaded[j], 16 if j == 2 else 32)
                norm.tile_stats(v, ch, j * (NT - 1) // 4, (j + 1) * (NT - 1) // 4 if j == 2 else NT)
            for r in range(R):
                v.wait_ge(wt_ps, r + 1)
                nc.vector.tensor_copy(k.wT[:, :, r * D:(r + 1) * D], bank[r % 4][:, :].rearrange("p (c o) -> p c o", c=DC)).then_inc(wt_free, 1)
            v.wait_ge(v_ps, 1)
            got = bank[4][:, 0:DC * R * 2 * H0].rearrange("p (c r j h) -> p c r j h", c=DC, r=R, j=2)
            for c in range(DC):
                for j in range(2):
                    nc.vector.tensor_copy(vst[:, c, j * R * H0:(j + 1) * R * H0].rearrange("p (r h) -> p r h", r=R), got[:, c, :, j, :]).then_inc(v_ok, 1)
            norm.statistics(v, ch)
            sc_ok.start(v)

            def evacuate(i, u):
                sc_ps.done(v, i * 2 + u)
                stored.slot(v, i, u)
                nc.vector.tensor_copy(scores[:, u, :], bank[2 + u][:, 0:R * H0])
                nc.vector.tensor_copy(col(k.dst_half, i * 2 + u), bank[2 + u][:, R * H0:2 * R * H0]).then_inc(sc_ok.sem, 1)

            norm.lead(v, lambda t, u: norm.normalise(v, t, u), evacuate)

        @block.tensor
        def _(pe):
            pe.wait_ge(consts, 1)
            pe.wait_ge(edges_f, 1)
            for n in range(6):
                j, half = divmod(n, 2)
                if n >= 4:
                    pe.wait_ge(e_free, n - 3)
                for c in range(8):
                    last = nc.tensor.transpose(bank[n % 4][:, c * NT:(c + 1) * NT], floats[j][:, half * 8 + c, :], k.ident[0:NT, 0:NT])
                last.then_inc(e_ps, 1)
            pe.wait_ge(weights, 16 * 17)
            pe.wait_ge(e_free, 6)
            for r in range(R):
                if r >= 4:
                    pe.wait_ge(wt_free, r - 3)
                for fc in range(DC):
                    for oc in range(DC):
                        last = nc.tensor.transpose(bank[r % 4][:, fc * D + oc * P:fc * D + (oc + 1) * P],
                                                   wn[:, r, oc, fc * P:(fc + 1) * P], k.ident[:, :])
                last.then_inc(wt_ps, 1)
            for fc in range(DC):
                for r in range(R):
                    o = (fc * R + r) * 2 * H0
                    for oc in range(DC):
                        last = nc.tensor.matmul(bank[4][:, o:o + 2 * H0], wn[:, r, oc, fc * P:(fc + 1) * P], ablk[:, oc, :],
                                                start=(oc == 0), stop=(oc == DC - 1))
            last.then_inc(v_ps, 1)
            pe.wait_ge(v_ok, 4)
            pe.wait_ge(wt_free, R)
            norm.t_ps.start(pe)
            sc_ps.start(pe)

            def product(t, u):
                norm.t_ok.done(pe, t)
                sc_ok.slot(pe, t)
                for c in range(DC):
                    last = nc.tensor.matmul(bank[2 + u][:, 0:P], norm.xT[:, u, c * P:(c + 1) * P], vst[:, c, :],
                                            start=(c == 0), stop=(c == DC - 1))
                last.then_inc(sc_ps.sem, 1)
            norm.feed(pe, product)


def list_items(nc, a, k):
    with Stage(nc, "items") as s:
        Q = C * NT
        IC = -(-ITEMS_MAX // P)
        span = s.sb("span", [P, 2, Q])
        n_of, before, junk = s.sb("blocks_of_tile", [P, Q]), s.sb("items_before", [P, Q]), s.sb("junk", [P, Q])
        place_i, q_i, item_i = k.dst_rows[:, 0:Q], k.dst_rows[:, Q:2 * Q], s.sb("item_i", [P, IC], I32)
        place, q_f, item = s.sb("place", [P, Q]), s.sb("tile_f", [P, Q]), s.sb("item", [P, IC])
        got = s.sb("got", [P, 4, IC])
        res = s.sb("result", [P, 3, IC])
        item_f = s.sb("item_f", [1, 2, ITEMS_MAX])
        loaded, iotas, dve, done, st = (s.sem(n) for n in ("span_loaded", "iotas", "dve", "result_ready", "tables_moved"))
        block = s.block()

        @block.gpsimd
        def _(pool):
            nc.gpsimd.memset(k.w[:, :], 0.0)
            nc.gpsimd.iota(place_i[:, :], [[1, C], [C, NT]], base=0, channel_multiplier=0).then_inc(iotas, 1)
            nc.gpsimd.iota(q_i[:, :], [[1, Q]], base=0, channel_multiplier=0).then_inc(iotas, 1)
            nc.gpsimd.iota(item_i[:, :], [[P, IC]], base=0, channel_multiplier=1).then_inc(iotas, 1)

        @block.sync
        def _(sp):
            sp.dma_start(span[:, :, :], k.span_tab.rearrange("(o j) q -> o j q", o=1).broadcast_to([P, 2, Q])).then_inc(loaded, 16)
            with nc.allow_non_contiguous_dma(reason="item tables, a few words of each partition"):
                sp.wait_ge(done, 1)
                sp.dma_start(k.item_tab.rearrange("j (c p) -> p j c", p=P), res[:, :, :]).then_inc(st, 16)
            sp.wait_ge(st, 16)
            sp.dma_start(item_f[:, :, :], k.item_tab.rearrange("(o j) c -> o j c", o=1)[:, 0:2, 0:ITEMS_MAX]).then_inc(st, 16)
            sp.dma_start(k.item_base[:, :], k.item_tab[2:3, 0:ITEMS_MAX].broadcast_to([P, ITEMS_MAX])).then_inc(st, 16)
            sp.wait_ge(st, 48)

        @block.vector
        def _(v):
            ch = Chain(v, dve)
            v.wait_ge(loaded, 16)
            v.wait_ge(iotas, 3)
            for o, i in ((place, place_i), (q_f, q_i), (item, item_i)):
                ch.link(nc.vector.tensor_copy(o[:, :], i[:, :]))
            ch.link(nc.vector.tensor_tensor(n_of[:, :], span[:, 1, :], span[:, 0, :], ALU.subtract))
            ch.link(nc.vector.tensor_scalar(n_of[:, :], n_of[:, :], 1.0, None, ALU.add))
            ch.link(nc.vector.tensor_tensor_scan(before[:, :], n_of[:, :], n_of[:, :], 0.0, ALU.add, ALU.bypass))
            ch.link(nc.vector.tensor_tensor(before[:, :], before[:, :], n_of[:, :], ALU.subtract))
            for c in range(IC):
                ch.link(nc.vector.tensor_scalar(junk[:, :], before[:, :], item[:, c:c + 1], -1.0, ALU.is_le, ALU.add, accum_out=got[:, 0, c:c + 1]))
                for j, t in ((1, before), (2, span[:, 0, :]), (3, place)):
                    ch.link(nc.vector.scalar_tensor_tensor(junk[:, :], q_f[:, :], got[:, 0, c:c + 1], t[:, :] if j != 2 else t, ALU.is_equal, ALU.mult,
                                                           accum_out=got[:, j, c:c + 1]))
            ch.link(nc.vector.tensor_tensor(got[:, 0, :], item[:, :], got[:, 1, :], ALU.subtract))
            ch.link(nc.vector.tensor_tensor(got[:, 0, :], got[:, 0, :], got[:, 2, :], ALU.add))
            ch.link(nc.vector.tensor_copy(res[:, 0, :], got[:, 3, :]))
            ch.link(nc.vector.tensor_scalar(res[:, 1, :], got[:, 0, :], float(NT - 1), None, ALU.min))
            ch.link(nc.vector.tensor_scalar(res[:, 2, :], got[:, 0, :], float(P), None, ALU.mult))
            v.sem_inc(done, 1)
            v.wait_ge(st, 48)
            ch.link(nc.vector.tensor_copy(k.item_i[:, :, :], item_f[:, :, :]))


def edge_scores(nc, a, k):
    with Stage(nc, "score") as s:
        bank = s.banks(6)
        turn_ps = [s.ctx.enter_context(nc.psum_tensor(f"score_turned{j}", [P, 8, P], BF16)) for j in range(2)]
        norm = Norm(nc, s, k, bank[0:2], k.moments0)
        hb = s.sb("h_rows", [P, 2, R * D])
        ids = s.sb("rows", [P, 2, C], I32)
        half = s.sb("halves", [P, 2, C * H0])
        hot, hotT = s.sb("one_hot", [P, 2, BM, P], BF16), s.sb("one_hot_T", [P, 2, BM, P])
        ident, number = s.sb("ident_bf16", [P, P], BF16), s.sb("numbers_bf16", [P, P], BF16)
        kept_r, part = s.sb("kept_relation", [P, BM, R * H0]), s.sb("dst_part", [P, BM, H0])
        products = Count(s, "h_tile_in_psum", 2)
        h_ps, h_ok, stored = s.sem("h_bank_full"), s.sem("h_bank_empty"), Landed(s, "h_rows_stored", 2)
        ids_ok, begun = s.sem("rows_ready"), s.sem("gathers_begun")
        gathered = [s.sem(f"halves_gathered{u}") for u in range(2)]
        hot_ok, turned, hotT_ok, picked, selected = (Count(s, n, 2) for n in (
            "one_hot_ready", "one_hot_turned", "one_hot_T_ready", "dst_half_in_psum", "relation_kept"))
        part_ok, ident_ok = s.sem("parts_ready"), s.sem("ident_ready")
        STEPS = UG + 1
        added = Count(s, "added", 2 * STEPS)
        zero, zero_ok, zeroed, dst_in = s.sb("zero", [P, D]), s.sem("zero_ready"), s.sem("zeroed"), s.sem("dst_loaded")
        leaky, full, kept = s.sem("leaky_done"), s.sem("scores_turned"), s.sem("scores_kept")
        block = s.block()
        GROUPS = -(-NT // 4)

        @block.gpsimd
        def _(pool):
            nc.gpsimd.memset(zero[:, :], 0.0).then_inc(zero_ok, 1)

            def body(t, u):
                pool.wait_ge(ids_ok, t + 1)
                pool.sem_inc(begun, 1)
                for c in range(C):
                    nc.gpsimd.indirect_dma_start(half[:, u, c * H0:(c + 1) * H0], None, k.src_tab,
                                                 bass.IndirectOffsetOnAxis(ids[:, u, c:c + 1], 0)).then_inc(gathered[u], 16)
            tiles(pool, NT, 2, body)

        @block.vector
        def _(v):
            ch = Chain(v, norm.dve)
            for n in (hot_ok, selected, added):
                n.start(v)
            ch.link(nc.vector.tensor_copy(ident[:, :], k.ident[:, :]))
            ch.link(nc.vector.tensor_copy(number[:, :], k.iota[:, :]))
            v.sem_inc(ident_ok, 1)
            norm.xn_ok.start(v)

            def tiles_of(t, b0, b1):
                edge = lambda b: b // 4 * UG + BATCH[b % 4]
                o, m = t * UG + edge(b0), edge(b1) - edge(b0)
                return registers(nc, mybir.EngineType.DVE, k.item_i[0:1, 0, o:o + m] if isinstance(o, int) else k.item_i[0:1, 0, bass.ds(o, m)], NT * C - 1)

            def one_hot(t, j, w, z):
                return nc.vector.tensor_scalar(hot[:, j % 2, w, :], number[:, :], col(k.item_base, t * UG + BATCH[j] + w), col(k.dst_f, z),
                                               ALU.add, ALU.is_equal)

            def items(t):
                for j in range(4):
                    m = BATCH[j + 1] - BATCH[j]
                    tn, jn = (t, j + 2) if j < 2 else (t + 1, j - 2)
                    mn = BATCH[jn + 1] - BATCH[jn]
                    z = tiles_of(t, j, j + 3)
                    picked.done(v, t * 4 + j)
                    for w in range(m):
                        o = w * R * H0
                        last = nc.vector.scalar_tensor_tensor(kept_r[:, w, :], k.relation[:, :], col(k.type_f, z[w]),
                                                              bank[4 + j % 2][:, o:o + R * H0], ALU.is_equal, ALU.mult)
                    last.then_inc(selected.sem, 1)
                    turned.slot(v, tn * 4 + jn)
                    hots = [one_hot(tn, jn, 0, z[len(z) - mn])]
                    selected.done(v, t * 4 + j)
                    added.slot(v, t * STEPS + BATCH[j] + 2 * STEPS - 1)
                    nc.vector.reduce_sum(part[:, 0:m, :], kept_r[:, 0:m, :].rearrange("p u (r h) -> p u h r", h=H0), AX.X).then_inc(part_ok, 1)
                    for w in range(max(m, mn)):
                        if 0 < w < mn:
                            hots.append(one_hot(tn, jn, w, z[len(z) - mn + w]))
                            if w == mn - 1:
                                hots[-1].then_inc(hot_ok.sem, 1)
                        if w == 0:
                            v.wait_ge(part_ok, t * 4 + j + 1)
                        if w < m:
                            added.slot(v, t * STEPS + BATCH[j] + w + 2 * STEPS - 1)
                            to = k.w[:, bass.ds(z[w] * H0, H0)]
                            nc.vector.tensor_tensor(to, to, part[:, w, :], ALU.add).then_inc(added.sem, 1)

            def source(i, u):
                t = i * 2 + u
                v.wait_ge(gathered[u], (i + 1) * C * 16)
                added.slot(v, t * STEPS + UG + 2 * STEPS - 1)
                w = col(k.w, t * P, P)
                nc.vector.tensor_tensor(w, w, half[:, u, :], ALU.add).then_inc(added.sem, 1)

            def address(t, u):
                v.wait_ge(added.sem, (t + 1) * STEPS)
                nc.vector.tensor_copy(ids[:, u, :], col(k.edge_row, t * C, C)).then_inc(ids_ok, 1)

            for t in range(2):
                address(t, t)
            norm.normalise(v, 0, 0)
            for j in range(2):
                z = tiles_of(0, j, j + 1)
                for w in range(len(z)):
                    last = one_hot(0, j, w, z[w])
                last.then_inc(hot_ok.sem, 1)
            with v.Fori(0, (NT - 3) // 2) as i:
                for u in range(2):
                    norm.normalise(v, i * 2 + u + 1, 1 - u)
                    items(i * 2 + u)
                    source(i, u)
                    address(i * 2 + u + 2, u)
            for u in range(2):
                norm.normalise(v, NT - 2 + u, 1 - u)
                items(NT - 3 + u)
                source((NT - 3) // 2, u)
                if u == 0:
                    address(NT - 1, 0)
            items(NT - 1)
            source((NT - 1) // 2, 0)
            added.slot(v, NT * STEPS + 2 * STEPS - 1)
            for n in range(GROUPS):
                c0, c1 = n * 4 * P, min((n + 1) * 4, NT) * P
                nc.vector.scalar_tensor_tensor(k.w[:, c0:c1], k.w[:, c0:c1], 0.2, k.w[:, c0:c1], ALU.mult, ALU.max).then_inc(leaky, 1)

        @block.tensor
        def _(pe):
            for n in (norm.t_ps, products, turned, picked):
                n.start(pe)
            pe.sem_inc(h_ps, 2)
            pe.wait_ge(ident_ok, 1)

            def body(t, u):
                norm.transpose(pe, t, u)
                o = t * UG
                b = registers(nc, mybir.EngineType.PE, k.item_i[0:1, 1, o:o + UG] if isinstance(o, int) else k.item_i[0:1, 1, bass.ds(o, UG)], NT - 1)
                norm.t_ok.done(pe, t)
                for j in range(4):
                    n = t * 4 + j
                    hot_ok.done(pe, n)
                    hotT_ok.slot(pe, n)
                    for w in range(BATCH[j + 1] - BATCH[j]):
                        last = nc.tensor.transpose(turn_ps[j % 2][:, w, :], hot[:, j % 2, w, :], ident[:, :])
                    last.then_inc(turned.sem, 1)
                    pe.wait_ge(h_ok, n + 1)
                    for c in range(DC):
                        last = nc.tensor.matmul(bank[2 + j % 2][:, :], norm.xT[:, u, c * P:(c + 1) * P], k.wT[:, c, j * 512:(j + 1) * 512],
                                                start=(c == 0), stop=(c == DC - 1))
                    last.then_inc(h_ps, 1)
                    hotT_ok.done(pe, n)
                    selected.slot(pe, n)
                    for w in range(BATCH[j], BATCH[j + 1]):
                        o = (w - BATCH[j]) * R * H0
                        last = nc.tensor.matmul(bank[4 + j % 2][:, o:o + R * H0], hotT[:, j % 2, w - BATCH[j], :], col(k.dst_half, b[w]), start=True, stop=True)
                    last.then_inc(picked.sem, 1)
                pe.sem_inc(products.sem, 1)
            tiles(pe, NT, 2, body)
            pe.wait_ge(h_ok, 2 + 4 * NT)
            for n in range(GROUPS):
                pe.wait_ge(leaky, n + 1)
                if n >= 4:
                    pe.wait_ge(kept, n - 3)
                for t in range(4 * n, min(4 * n + 4, NT)):
                    last = nc.tensor.transpose(bank[n % 4][:, t % 4 * P:(t % 4 + 1) * P], k.w[:, t * P:(t + 1) * P], k.ident[:, :])
                last.then_inc(full, 1)

        @block.scalar
        def _(act):
            norm.t_ok.start(act)
            act.sem_inc(h_ok, 2)
            hotT_ok.start(act)

            def body(i, u):
                t = i * 2 + u
                norm.keep(act, t, u, products)
                stored.slot(act, i, u)
                for j in range(4):
                    n, m = t * 4 + j, BATCH[j + 1] - BATCH[j]
                    turned.done(act, n)
                    picked.slot(act, n)
                    nc.scalar.activation(hotT[:, j % 2, 0:m, :], turn_ps[j % 2][:, 0:m, :], ACT.Copy).then_inc(hotT_ok.sem, 1)
                    act.wait_ge(h_ps, 2 + n + 1)
                    nc.scalar.activation(hb[:, u, j * 512:(j + 1) * 512], bank[2 + j % 2][:, :], ACT.Copy).then_inc(h_ok, 1)
            turns(act, NT, 2, body)
            for n in range(GROUPS):
                act.wait_ge(full, n + 1)
                m = min(4, NT - 4 * n) * P
                nc.scalar.activation(k.score[:, 4 * n * P:4 * n * P + m], bank[n % 4][:, 0:m], ACT.Copy).then_inc(kept, 1)

        @block.sync
        def _(sp):
            stored.start(sp)
            for c in range(C):
                sp.dma_start(k.dst_rows[c * H0:(c + 1) * H0, :], a["dst"][c * CE:(c + 1) * CE].rearrange("(o e) -> o e", o=1).broadcast_to([H0, CE])).then_inc(dst_in, 16)
            sp.wait_ge(zero_ok, 1)

            def body(t, u):
                for tab, m in k.sorted:
                    sp.dma_start(rows(tab, t * m * P, m * P).rearrange("(m p) f -> p m f", p=P),
                                 zero[:, :].rearrange("p (o f) -> p o f", o=1).broadcast_to([P, m, D])).then_inc(zeroed, 16)
                sp.wait_ge(h_ok, 2 + 4 * t + 4)
                sp.dma_start(rows(k.h_tab.rearrange("(n r) o -> n (r o)", r=R), t * P, P), hb[:, u, :]).then_inc(stored.sems[u], 16)
            tiles(sp, NT, 2, body)
            stored.all(sp, NT)
            sp.wait_ge(zeroed, 16 * NT * len(k.sorted))
            sp.wait_ge(dst_in, 16 * C)


def edge_weights(nc, a, k):
    with Stage(nc, "weight") as s:
        bank = s.banks()
        d = k.dst_rows
        same = s.sb("same", [P, CE + 1])
        seg = s.sb("segment_max", [P, CE])
        last_seg = k.w
        PIECES = [(n * 12 * P, min((n + 1) * 12 * P if n < 3 else CE, CE)) for n in range(4)]
        ends = s.sb("ends", [P, 4])
        row = s.sb("rows", [1, 4, H0 * C])
        link, one, nxt, g, fc, bc = (s.sb(n, [1, H0, C]) for n in ("link", "one", "next", "gate", "forward", "backward"))
        carry = s.sb("carry", [1, 2, C * H0])
        carry_c = s.sb("carry_col", [P, 2])
        dve, ends_ps, ends_ok, carry_ok, carry_ps = (s.sem(n) for n in ("dve", "ends_in_psum", "ends_ready", "carry_ready", "carry_in_psum"))
        carry_in, last_ok = s.sem("carry_columns_ready"), s.sem("last_segment_ready")
        diff_ok, exp_ok, w_ps, w_ok, cleared = (s.sem(n) for n in ("diff_ready", "exp_ready", "w_in_psum", "w_ready", "cleared"))
        block = s.block()

        @block.gpsimd
        def _(pool):
            nc.gpsimd.memset(same[:, 0:1], 0.0).then_inc(cleared, 1)
            nc.gpsimd.memset(same[:, CE:CE + 1], 0.0).then_inc(cleared, 1)
            for t in (link, nxt, carry):
                nc.gpsimd.memset(t[:, :, :], 0.0).then_inc(cleared, 1)
            pool.wait_ge(carry_in, 1)
            for c0, c1 in PIECES:
                nc.gpsimd.tensor_scalar(last_seg[:, c0:c1], d[:, c0:c1], ends[:, 3:4], carry_c[:, 1:2], ALU.is_equal, ALU.mult).then_inc(last_ok, 1)

        @block.vector
        def _(v):
            ch = Chain(v, dve)
            v.wait_ge(cleared, 5)
            ch.link(nc.vector.tensor_tensor(same[:, 1:CE], d[:, 1:CE], d[:, 0:CE - 1], ALU.is_equal))
            ch.link(nc.vector.tensor_tensor_scan(seg[:, :], same[:, 0:CE], k.score[:, 0:CE], 0.0, ALU.mult, ALU.max))
            ch.link(nc.vector.tensor_tensor_scan(seg[:, ::-1], same[:, CE:0:-1], seg[:, ::-1], 0.0, ALU.mult, ALU.max))
            ch.link(nc.vector.tensor_copy(ends[:, 0:1], seg[:, 0:1]))
            ch.link(nc.vector.tensor_copy(ends[:, 1:2], seg[:, CE - 1:CE]))
            ch.link(nc.vector.tensor_copy(ends[:, 2:3], d[:, 0:1]))
            ch.link(nc.vector.tensor_copy(ends[:, 3:4], d[:, CE - 1:CE]))
            v.sem_inc(ends_ok, 1)
            v.wait_ge(ends_ps, 1)
            ch.link(nc.vector.tensor_copy(row[:, :, :].rearrange("o j (h c) -> o j h c", c=C), bank[0][0:1, :].rearrange("o (j c h) -> o j h c", j=4, h=H0)))
            r4 = row[:, :, :].rearrange("o j (h c) -> o j h c", c=C)
            ch.link(nc.vector.tensor_tensor(link[:, :, 1:C], r4[:, 2, :, 1:C], r4[:, 3, :, 0:C - 1], ALU.is_equal))
            ch.link(nc.vector.tensor_copy(nxt[:, :, 0:C - 1], link[:, :, 1:C]))
            ch.link(nc.vector.tensor_tensor(one[:, :, :], r4[:, 2], r4[:, 3], ALU.is_equal))
            ch.link(nc.vector.tensor_tensor(g[:, :, :], one[:, :, :], link[:, :, :], ALU.mult))
            ch.link(nc.vector.tensor_tensor_scan(flat(fc[:, :, :]), flat(g[:, :, :]), row[:, 1, :], 0.0, ALU.mult, ALU.max))
            ch.link(nc.vector.tensor_tensor(g[:, :, :], one[:, :, :], nxt[:, :, :], ALU.mult))
            ch.link(nc.vector.tensor_tensor_scan(flat(bc[:, :, :])[:, ::-1], flat(g[:, :, :])[:, ::-1], row[:, 0, ::-1], 0.0, ALU.mult, ALU.max))
            cr = carry[:, :, :].rearrange("o j (c h) -> o j h c", h=H0)
            ch.link(nc.vector.tensor_tensor(cr[:, 0, :, 1:C], fc[:, :, 0:C - 1], link[:, :, 1:C], ALU.mult))
            ch.link(nc.vector.tensor_tensor(cr[:, 1, :, 0:C - 1], bc[:, :, 1:C], nxt[:, :, 0:C - 1], ALU.mult))
            v.sem_inc(carry_ok, 1)
            v.wait_ge(carry_ps, 1)
            ch.link(nc.vector.tensor_copy(carry_c[:, :], bank[1][:, 0:2]))
            v.sem_inc(carry_in, 1)
            for n, (c0, c1) in enumerate(PIECES):
                for j in range(2):
                    other = same if j == 0 else last_seg
                    if j == 0:
                        ch.link(nc.vector.tensor_scalar(same[:, c0:c1], d[:, c0:c1], ends[:, 2:3], carry_c[:, 0:1], ALU.is_equal, ALU.mult))
                    else:
                        v.wait_ge(last_ok, n + 1)
                    ch.link(nc.vector.tensor_tensor(seg[:, c0:c1], seg[:, c0:c1], other[:, c0:c1], ALU.max))
                nc.vector.tensor_tensor(seg[:, c0:c1], k.score[:, c0:c1], seg[:, c0:c1], ALU.subtract).then_inc(diff_ok, 1)
            v.wait_ge(diff_ok, len(PIECES))
            ch.link(nc.vector.memset(k.w[:, (NT - 1) * P:], 0.0))
            for n in range(-(-NT // 4)):
                v.wait_ge(w_ps, n + 1)
                if 4 * n + 4 <= NT:
                    nc.vector.tensor_copy(k.w[:, 4 * n * P:(4 * n + 4) * P], bank[2 + n % 4][:, :]).then_inc(w_ok, 1)
                else:
                    nc.vector.tensor_copy(k.w[0:TAIL, 4 * n * P:], bank[2 + n % 4][0:TAIL, 0:P]).then_inc(w_ok, 1)

        @block.scalar
        def _(act):
            for n, (c0, c1) in enumerate(PIECES):
                act.wait_ge(diff_ok, n + 1)
                nc.scalar.activation(k.score[:, c0:c1], seg[:, c0:c1], ACT.Exp).then_inc(exp_ok, 1)

        @block.tensor
        def _(pe):
            pe.wait_ge(ends_ok, 1)
            for j in range(4):
                last = nc.tensor.transpose(bank[0][0:1, j * P:(j + 1) * P], ends[:, j:j + 1], k.ident[:, :])
            last.then_inc(ends_ps, 1)
            pe.wait_ge(carry_ok, 1)
            for j in range(2):
                last = nc.tensor.transpose(bank[1][:, j:j + 1], carry[0:1, j, :], k.ident[0:1, 0:1])
            last.then_inc(carry_ps, 1)
            for n in range(-(-NT // 4)):
                pe.wait_ge(exp_ok, min(n // 3, len(PIECES) - 1) + 1)
                if n >= 4:
                    pe.wait_ge(w_ok, n - 3)
                for t in range(4 * n, min(4 * n + 4, NT)):
                    m = P if t < NT - 1 else TAIL
                    last = nc.tensor.transpose(bank[2 + n % 4][0:m, t % 4 * P:(t % 4 + 1) * P], k.score[:, t * P:t * P + m], k.ident[:, :])
                last.then_inc(w_ps, 1)


def registers(nc, eng, ap, top):
    return nc.values_load_multi_w_load_instructions(ap, engines=(eng,), min_val=0, max_val=top,
                                                    skip_runtime_bounds_check_because="the tables are built on the chip, within the bound")[1]


def aggregate(nc, a, k):
    with Stage(nc, "sum") as s:
        bank = s.banks()
        acc = s.sb("acc", [P, NT, D + H0])
        got = s.sb("gathered", [P, U, D])
        ids = s.sb("rows", [P, U], I32)
        msg, hot = s.sb("messages", [P, U, D + H0]), s.sb("one_hot", [P, U, P])
        den = s.sb("denominator", [P, NT, H0])
        ids_ok, used = s.sem("rows_ready"), Count(s, "rows_used", U)
        arrived = [s.sem(f"gathered{u}") for u in range(U)]
        off, far = s.sb("offset", [P, U]), s.sb("distance", [P, U, P])
        off_ok, far_ok, hot_ok = s.sem("offset_ready"), s.sem("distance_ready"), s.sem("one_hot_ready")
        summed, added = Count(s, "summed", U), Count(s, "added", 1)
        begun, cleared, dve, mean_ok, x_ok = (s.sem(n) for n in ("gathers_begun", "cleared", "dve", "mean_ready", "x_ready"))
        block = s.block()

        @block.gpsimd
        def _(pool):
            nc.gpsimd.memset(acc[:, :, :], 0.0).then_inc(cleared, 1)
            with pool.Fori(0, ITEMS // U) as i:
                for u in range(U):
                    if u % 4 == 0:
                        pool.wait_ge(ids_ok, i * U + u + 4)
                        pool.sem_inc(begun, 1)
                    nc.gpsimd.indirect_dma_start(got[:, u, :], None, k.h_tab, bass.IndirectOffsetOnAxis(ids[:, u:u + 1], 0)).then_inc(arrived[u], 16)

            def onto_nodes(t, u):
                pool.wait_ge(mean_ok, t + 1)
                pool.sem_inc(begun, 1)
                nc.gpsimd.tensor_tensor(col(k.x, t), col(k.x, t), col(acc, t)[:, 0:D], ALU.add).then_inc(x_ok, 1)
            tiles(pool, NT, 7, onto_nodes)

        @block.scalar
        def _(act):
            with act.Fori(0, ITEMS // U) as i:
                z = registers(nc, mybir.EngineType.Activation, k.item_i[0:1, 0, bass.ds(i * U, U)], NT * C - 1)
                for q in range(0, U, 4):
                    n = i * U + q
                    used.slot(act, n + 3)
                    for u in range(q, q + 4):
                        last = nc.scalar.activation(ids[:, u:u + 1], col(k.edge_row, z[u]), ACT.Copy)
                    last.then_inc(ids_ok, 4)
                    for u in range(q, q + 4):
                        last = nc.scalar.activation(off[:, u:u + 1], col(k.dst_f, z[u]), ACT.Identity, scale=-1.0, bias=col(k.item_base, n + u - q))
                    last.then_inc(off_ok, 1)
                    act.wait_ge(off_ok, i * (U // 4) + q // 4 + 1)
                    for u in range(q, q + 4):
                        last = nc.scalar.activation(far[:, u, :], k.iota[:, :], ACT.Abs, bias=off[:, u:u + 1])
                    last.then_inc(far_ok, 1)
                    act.wait_ge(far_ok, i * (U // 4) + q // 4 + 1)
                    summed.slot(act, n + 3)
                    nc.scalar.activation(hot[:, q:q + 4, :], far[:, q:q + 4, :], ACT.Relu, scale=-1.0, bias=k.ones[:, 0:1]).then_inc(hot_ok, 4)

        @block.vector
        def _(v):
            used.start(v)
            added.start(v)
            v.wait_ge(cleared, 1)
            LAG = 3

            def add(n, u, b):
                summed.done(v, n)
                added.slot(v, n)
                nc.vector.tensor_tensor(col(acc, b), bank[u][:, 0:D + H0], col(acc, b), ALU.add).then_inc(added.sem, 1)

            def blocks(first, m):
                return registers(nc, mybir.EngineType.DVE, k.item_i[0:1, 1, first:first + m] if isinstance(first, int)
                                 else k.item_i[0:1, 1, bass.ds(first, m)], NT - 1)

            def round_(i, peeled):
                z = registers(nc, mybir.EngineType.DVE, k.item_i[0:1, 0, bass.ds(i * U, U)] if not peeled else k.item_i[0:1, 0, 0:U], NT * C - 1)
                b = blocks(0, U - LAG) if peeled else blocks(i * U - LAG, U)
                for u in range(U):
                    w = k.w[:, bass.ds(z[u] * H0, H0)]
                    v.wait_ge(arrived[u], (i + 1) * 16)
                    summed.slot(v, i * U + u)
                    nc.vector.tensor_copy(msg[:, u, D:D + H0], w)
                    nc.vector.tensor_tensor(msg[:, u, 0:D].rearrange("p (h d) -> p h d", h=H0), got[:, u, :].rearrange("p (h d) -> p h d", h=H0),
                                            w.rearrange("p (h o) -> p h o", o=1).broadcast_to([P, H0, HD0]), ALU.mult).then_inc(used.sem, 1)
                    if not peeled:
                        add(i * U + u - LAG, (u - LAG) % U, b[u])
                    elif u >= LAG:
                        add(u - LAG, u - LAG, b[u - LAG])
            round_(0, True)
            with v.Fori(1, ITEMS // U) as i:
                round_(i, False)
            b = blocks(ITEMS - LAG, LAG)
            for u in range(LAG):
                add(ITEMS - LAG + u, U - LAG + u, b[u])
            ch = Chain(v, dve)
            added.done(v, ITEMS - 1)
            ch.link(nc.vector.tensor_scalar(den[:, :, :], acc[:, :, D:D + H0], 1e-12, None, ALU.add))
            ch.link(nc.vector.reciprocal(den[:, :, :], den[:, :, :]))

            def finish(t, u):
                m = col(acc, t)[:, 0:D].rearrange("p (h d) -> p h d", h=H0)
                nc.vector.tensor_tensor(m, m, col(den, t).rearrange("p (h o) -> p h o", o=1).broadcast_to([P, H0, HD0]), ALU.mult).then_inc(mean_ok, 1)
            def tile_stats(t, u):
                v.wait_ge(x_ok, t + 1)
                nc.vector.bn_stats(col(k.stats, t), col(k.x, t))
            for u in range(4):
                finish(u, u)
            with v.Fori(0, NT // 4 - 1) as i:
                for u in range(4):
                    finish(i * 4 + 4 + u, u)
                    tile_stats(i * 4 + u, u)
            finish(NT - 1, 0)
            for t in range(NT - 5, NT):
                tile_stats(t, 0)

        @block.tensor
        def _(pe):
            summed.start(pe)
            with pe.Fori(0, ITEMS // U) as i:
                for u in range(U):
                    used.done(pe, i * U + u)
                    pe.wait_ge(hot_ok, i * U + u + 1)
                    nc.tensor.matmul(bank[u][:, 0:D + H0], hot[:, u, :], msg[:, u, :], start=True, stop=True).then_inc(summed.sem, 1)


def route_tiles(experts, top, step=P):
    return (N * top + experts * (step - 1)) // step


class Route:

    def __init__(self, nc, s, k, experts, top, spare=0, step=P):
        self.nc, self.k, self.K, self.top = nc, k, experts, top
        self.step, self.shift = step, step.bit_length() - 1
        self.tiles = route_tiles(experts, top, step) + spare
        self.place = [s.sb(f"place{j}", [P, NT]) for j in range(top)]
        self.expert = s.sb("expert", [1, self.tiles], I32)

    def work_in(self, s, bank):
        experts, top, self.bank = self.K, self.top, bank
        K, T = experts, self.tiles
        self.logits = s.sb("logits", [P, NT, K])
        self.pick = [s.sb(f"pick{j}", [P, NT, K]) for j in range(top)]
        self.best = [s.sb(f"best{j}", [P, NT]) for j in range(top)]
        self.at = s.sb("at", [P, NT])
        self.work = s.sb("work", [P, NT, K])
        self.mask = self.logits
        self.reset = self.work[:, :, :].rearrange("p t e -> p (t e)").rearrange("p (e t) -> p e t", e=K)
        self.number, self.total = s.sb("number", [P, K]), s.sb("total", [P, K, NT])
        self.running = s.sb("running", [P, K, NT])
        self.count, self.start_row, self.count_i = s.sb("count", [P, K]), s.sb("start_row", [P, K]), s.sb("count_i", [P, K], I32)
        self.valid = s.sb("valid", [P, 1])
        self.tile_row_i, self.tile_row = s.sb("tile_row_i", [1, T], I32), s.sb("tile_row", [1, T])
        self.tile_cmp, self.expert_f = s.sb("tile_cmp", [1, T, K]), s.sb("expert_f", [1, T])
        self.iotas, self.picked, self.counted = s.sem("route_iotas"), s.sem("picked"), s.sem("counted")
        self.per = NT * K // 4 if NT * K > 512 else NT * K
        self.chunks = NT * K // self.per
        assert self.per <= 512 and self.chunks * self.per == NT * K

    def pool(self):
        nc = self.nc
        nc.gpsimd.iota(self.tile_row_i[:, :], [[self.step, self.tiles]], base=0, channel_multiplier=0).then_inc(self.iotas, 1)

    def choose(self, v, ch):
        nc, K = self.nc, self.K
        b3 = lambda x: x.rearrange("p (t o) -> p t o", o=1).broadcast_to([P, NT, K])
        bk = lambda x: x.rearrange("p (o e) -> p o e", o=1).broadcast_to([P, NT, K])
        ch.link(nc.vector.tensor_copy(self.number[:, :], self.k.iota[:, 0:K]))
        for j in range(self.top):
            ch.link(nc.vector.reduce_max(self.best[j][:, :], self.logits[:, :, :], AX.X))
            ch.link(nc.vector.tensor_tensor(self.work[:, :, :], self.logits[:, :, :], b3(self.best[j][:, :]), ALU.is_equal))
            ch.link(nc.vector.scalar_tensor_tensor(self.work[:, :, :], self.work[:, :, :], -1000.0, bk(self.number[:, :]), ALU.mult, ALU.add))
            ch.link(nc.vector.tensor_reduce(self.at[:, :], self.work[:, :, :], AX.X, ALU.min))
            ch.link(nc.vector.scalar_tensor_tensor(self.pick[j][:, :, :], bk(self.number[:, :]), -1000.0, b3(self.at[:, :]), ALU.add, ALU.is_equal))
            if j + 1 < self.top:
                ch.link(nc.vector.scalar_tensor_tensor(self.logits[:, :, :], self.pick[j][:, :, :], -3e38, self.logits[:, :, :], ALU.mult, ALU.add))

    def vector(self, v, ch):
        nc, K = self.nc, self.K
        v.wait_ge(self.iotas, 1)
        self.choose(v, ch)
        ch.link(nc.vector.tensor_scalar(self.valid[:, :], self.k.col[:, :], float(TAIL), None, ALU.is_lt))
        ch.link(nc.vector.tensor_copy(self.mask[:, :, :], self.pick[0][:, :, :]))
        for j in range(1, self.top):
            ch.link(nc.vector.tensor_tensor(self.mask[:, :, :], self.mask[:, :, :], self.pick[j][:, :, :], ALU.add))
        ch.link(nc.vector.tensor_scalar(self.mask[:, NT - 1, :], self.mask[:, NT - 1, :], self.valid[:, 0:1], None, ALU.mult))
        v.sem_inc(self.picked, 1)
        ch.link(nc.vector.tensor_copy(self.tile_row[:, :], self.tile_row_i[:, :]))
        v.wait_ge(self.counted, 1)
        w = flat(self.work[:, :, :])
        for n in range(self.chunks):
            ch.link(nc.vector.tensor_copy(w[:, n * self.per:(n + 1) * self.per], self.bank[4 + n][:, 0:self.per]))
        ch.link(nc.vector.tensor_copy(self.total[:, :, :], self.work[:, :, :].rearrange("p t e -> p e t")))
        ch.link(nc.vector.memset(self.reset, 1.0))
        ch.link(nc.vector.memset(self.reset[:, :, 0:1], 0.0))
        ch.link(nc.vector.tensor_tensor_scan(flat(self.running[:, :, :]), flat(self.reset), flat(self.total[:, :, :]), 0.0, ALU.mult, ALU.add))
        ch.link(nc.vector.tensor_scalar(self.count[:, :], self.running[:, :, NT - 1], float(self.step - 1), None, ALU.add))
        ch.link(nc.vector.tensor_copy(self.count_i[:, :], self.count[:, :]))
        ch.link(nc.vector.tensor_scalar(self.count_i[:, :], self.count_i[:, :], self.shift, self.shift, ALU.arith_shift_right, ALU.logical_shift_left))
        ch.link(nc.vector.tensor_copy(self.count[:, :], self.count_i[:, :]))
        ch.link(nc.vector.tensor_tensor_scan(self.start_row[:, :], self.count[:, :], self.count[:, :], 0.0, ALU.add, ALU.bypass))
        ch.link(nc.vector.tensor_tensor(self.start_row[:, :], self.start_row[:, :], self.count[:, :], ALU.subtract))
        ch.link(nc.vector.tensor_tensor(self.running[:, :, :], self.running[:, :, :], self.total[:, :, :], ALU.subtract))
        sr = self.start_row[:, :].rearrange("p (e o) -> p e o", o=1).broadcast_to([P, K, NT])
        ch.link(nc.vector.tensor_tensor(self.running[:, :, :], self.running[:, :, :], sr, ALU.add))
        ch.link(nc.vector.tensor_copy(self.work[:, :, :], self.running[:, :, :].rearrange("p e t -> p t e")))
        for n in range(self.chunks):
            c = w[:, n * self.per:(n + 1) * self.per]
            ch.link(nc.vector.tensor_tensor(c, self.bank[n][:, 0:self.per], c, ALU.add))
        for j in range(self.top):
            ch.link(nc.vector.tensor_tensor(self.mask[:, :, :], self.pick[j][:, :, :], self.work[:, :, :], ALU.mult))
            ch.link(nc.vector.reduce_sum(self.place[j][:, :], self.mask[:, :, :], AX.X))
        T = self.tiles
        ch.link(nc.vector.tensor_tensor(self.tile_cmp[:, :, :], self.tile_row[:, :].rearrange("p (t o) -> p t o", o=1).broadcast_to([1, T, K]),
                                        self.start_row[0:1, :].rearrange("p (o e) -> p o e", o=1).broadcast_to([1, T, K]), ALU.is_ge))
        ch.link(nc.vector.reduce_sum(self.expert_f[:, :], self.tile_cmp[:, :, :], AX.X))
        ch.link(nc.vector.tensor_scalar(self.expert_f[:, :], self.expert_f[:, :], -1.0, None, ALU.add))
        ch.link(nc.vector.tensor_copy(self.expert[:, :], self.expert_f[:, :]))

    def tensor(self, pe):
        nc = self.nc
        pe.wait_ge(self.picked, 1)
        m = flat(self.mask[:, :, :])
        for n in range(self.chunks):
            c = m[:, n * self.per:(n + 1) * self.per]
            nc.tensor.matmul(self.bank[n][:, 0:self.per], self.k.before[:, :], c, start=True, stop=True)
            last = nc.tensor.matmul(self.bank[4 + n][:, 0:self.per], self.k.ones[:, :], c, start=True, stop=True)
        last.then_inc(self.counted, 1)


def moe0(nc, a, k):
    with Stage(nc, "moe0") as s:
        bank = s.banks()
        norm = Norm(nc, s, k, bank[0:2])
        route = Route(nc, s, k, E0, 1)
        route.work_in(s, bank)
        T = route.tiles
        rw_n, rw = s.sb("router_natural", [E0, D]), s.sb("router", [P, DC, E0])
        rb = s.sb("router_bias", [P, E0])
        w1, w2 = s.sb("w1", [P, DC, E0, F0]), s.sb("w2", [F0, E0, D])
        b1, b2 = s.sb("b1", [P, E0, F0]), s.sb("b2", [P, E0, D])
        ids = s.sb("rows", [P, 4], I32)
        xi, xT = s.sb("tile", [P, 4, D]), s.sb("tile_T", [P, 4, D])
        hid, hT = s.sb("hidden", [P, 4, P]), s.sb("hidden_T", [F0, 4, P])
        y = s.sb("y", [P, 4, D])
        router, loaded, rw_ps, rw_ok = s.sem("router_loaded"), s.sem("weights_loaded"), s.sem("router_in_psum"), s.sem("router_ready")
        lg_ps, lg_ok = Count(s, "logits_in_psum", 2), Count(s, "logits_ready", 2)
        route_ok, row_ok = s.sem("route_ready"), s.sem("row_ready")
        scattered, gathered = [s.sem(f"scattered{u}") for u in range(4)], [s.sem(f"gathered{u}") for u in range(4)]
        begun, all_out, node_ok = s.sem("dma_begun"), s.sem("all_results_written"), s.sem("x_ready")
        tile_in = [s.sem(f"tile_loaded{u}") for u in range(4)]
        out_ok = Landed(s, "y_written", 4)
        x_ps, x_ok, h_ps, h_ok, ht_ps, ht_ok, y_ps, y_add, y_ok = (Count(s, n, 4) for n in (
            "x_in_psum", "xT_ready", "hidden_in_psum", "hidden_ready", "hidden_T_in_psum", "hidden_T_ready", "y_in_psum", "y_biased", "y_ready"))
        block = s.block()

        @block.gpsimd
        def _(pool):
            route.pool()

            def scatter(i, u):
                t = i * 4 + u
                m = P if not isinstance(t, int) or t < NT - 1 else TAIL
                pool.wait_ge(row_ok, t + 1)
                pool.sem_inc(begun, 1)
                nc.gpsimd.indirect_dma_start(k.xs0, bass.IndirectOffsetOnAxis(ids[0:m, u:u + 1], 0), xi[0:m, u, :], None).then_inc(scattered[u], 16)
            rounds(pool, NT, 4, scatter)
            for u in range(4):
                pool.wait_ge(scattered[u], 16 * ((NT - u + 3) // 4))

            def load(i, u):
                x_ps.slot(pool, i * 4 + u)
                pool.dma_start(xi[:, u, :], rows(k.xs0, (i * 4 + u) * P, P)).then_inc(tile_in[u], 16)
            turns(pool, T + 4, 4, load)
            pool.wait_ge(all_out, 1)

            def gather(i, u):
                t = i * 4 + u
                m = P if not isinstance(t, int) or t < NT - 1 else TAIL
                pool.wait_ge(row_ok, NT + t + 1)
                pool.sem_inc(begun, 1)
                nc.gpsimd.indirect_dma_start(y[0:m, u, :], None, k.ys0, bass.IndirectOffsetOnAxis(ids[0:m, u:u + 1], 0)).then_inc(gathered[u], 16)
            rounds(pool, NT, 4, gather)

        @block.sync
        def _(sp):
            sp.dma_start(rw_n[:, :], a["L0_ffn_router_w"]).then_inc(router, 16)
            sp.dma_start(rb[:, :], a["L0_ffn_router_b"].rearrange("(o e) -> o e", o=1).broadcast_to([P, E0])).then_inc(router, 16)
            for c in range(DC):
                sp.dma_start(w1[:, c, :, :], a["L0_ffn_W1"][:, c * P:(c + 1) * P, :].rearrange("e p h -> p e h")).then_inc(loaded, 16)
            sp.dma_start(w2[:, :, :], a["L0_ffn_W2"].rearrange("e h d -> h e d")).then_inc(loaded, 16)
            for t, name in ((b1, "L0_ffn_b1"), (b2, "L0_ffn_b2")):
                v = a[name].rearrange("e h -> (e h)").rearrange("(o n) -> o n", o=1)
                sp.dma_start(flat(t[:, :, :]), v.broadcast_to([P, v.shape[1]])).then_inc(loaded, 16)
            out_ok.start(sp)

            def save(i, u):
                y_ok.done(sp, i * 4 + u)
                sp.dma_start(rows(k.ys0, (i * 4 + u) * P, P), y[:, u, :]).then_inc(out_ok.sems[u], 16)
            turns(sp, T, 4, save)
            out_ok.all(sp, T)
            sp.sem_inc(all_out, 1)

        @block.scalar
        def _(act):
            norm.root(act)
            tiles(act, NT, 2, lambda t, u: norm.keep(act, t, u, lg_ps))
            act.wait_ge(route_ok, 1)
            for n in (x_ok, ht_ok, y_ok):
                n.start(act)

            def columns(t, u):
                x_ps.done(act, t)
                nc.scalar.activation(xT[:, u, :], bank[2 * u + 1][:, D:2 * D], ACT.Copy).then_inc(x_ok.sem, 1)
            for u in range(4):
                columns(u, u)
            with act.Fori(0, T // 4) as i:
                for u in range(4):
                    columns(i * 4 + 4 + u, u)
                for u in range(4):
                    ht_ps.done(act, i * 4 + u)
                    nc.scalar.activation(hT[:, u, :], bank[2 * u][0:F0, 3 * P:4 * P], ACT.Relu).then_inc(ht_ok.sem, 1)
                for u in range(4):
                    y_add.done(act, i * 4 + u)
                    nc.scalar.activation(y[:, u, :], y[:, u, :], ACT.Relu).then_inc(y_ok.sem, 1)

        @block.vector
        def _(v):
            ch = Chain(v, norm.dve)
            ch.link(nc.vector.memset(hid[:, :, :], 0.0))
            norm.statistics(v, ch)
            v.wait_ge(router, 32)
            v.wait_ge(rw_ps, 1)
            nc.vector.tensor_copy(rw[:, :, :], bank[4][:, 0:DC * E0].rearrange("p (c e) -> p c e", c=DC)).then_inc(rw_ok, 1)
            lg_ok.start(v)

            def logits(i, u):
                lg_ps.done(v, i * 2 + u)
                nc.vector.tensor_tensor(col(route.logits, i * 2 + u), bank[2 + u][:, 0:E0], rb[:, :], ALU.add).then_inc(lg_ok.sem, 1)
            norm.lead(v, lambda t, u: norm.normalise(v, t, u), logits)
            lg_ok.done(v, NT - 1)
            route.vector(v, ch)
            v.sem_inc(route_ok, 1)

            def send(i, u):
                t = i * 4 + u
                if not isinstance(i, int) or i:
                    v.wait_ge(scattered[u], i * 16)
                nc.vector.tensor_scalar(xi[:, u, :], col(k.x, t), col(norm.mean, t), col(norm.rstd, t), ALU.subtract, ALU.mult)
                nc.vector.tensor_copy(ids[:, u:u + 1], col(route.place[0], t)).then_inc(row_ok, 1)
            rounds(v, NT, 4, send)
            for n in (h_ok, y_add):
                n.start(v)
            v.wait_ge(loaded, 5 * 16)
            with v.Fori(0, T // 4) as i:
                e = registers(nc, mybir.EngineType.DVE, route.expert[0:1, bass.ds(i * 4, 4)], E0 - 1)
                for u in range(4):
                    h_ps.done(v, i * 4 + u)
                    nc.vector.tensor_tensor(hid[:, u, 0:F0], bank[2 * u][:, 0:F0], col(b1, e[u]), ALU.add).then_inc(h_ok.sem, 1)
                for u in range(4):
                    y_ps.done(v, i * 4 + u)
                    out_ok.slot(v, i, u)
                    nc.vector.tensor_tensor(y[:, u, :], bank[2 * u + 1][:, 0:D], col(b2, e[u]), ALU.add).then_inc(y_add.sem, 1)
            for u in range(4):
                v.wait_ge(scattered[u], 16 * ((NT - u + 3) // 4))

            def address(i, u):
                nc.vector.tensor_copy(ids[:, u:u + 1], col(route.place[0], i * 4 + u)).then_inc(row_ok, 1)

            def add(i, u):
                v.wait_ge(gathered[u], i * 16 + 16)
                m = P if not isinstance(i, int) or i * 4 + u < NT - 1 else TAIL
                x = col(k.x, i * 4 + u)[0:m]
                nc.vector.tensor_tensor(x, x, y[0:m, u, :], ALU.add).then_inc(node_ok, 1)

            def tile_stats(i, u):
                v.wait_ge(node_ok, i * 4 + u + 1)
                nc.vector.bn_stats(col(k.stats, i * 4 + u), col(k.x, i * 4 + u))
            for u in range(4):
                address(0, u)
            with v.Fori(0, NT // 4 - 1) as i:
                for u in range(4):
                    add(i, u)
                    address(i + 1, u)
                for u in range(4):
                    tile_stats(i, u)
            for u in range(4):
                add(NT // 4 - 1, u)
            address(NT // 4, 0)
            for u in range(4):
                tile_stats(NT // 4 - 1, u)
            add(NT // 4, 0)
            tile_stats(NT // 4, 0)

        @block.tensor
        def _(pe):
            pe.wait_ge(router, 32)
            for c in range(DC):
                last = nc.tensor.transpose(bank[4][:, c * E0:(c + 1) * E0], rw_n[:, c * P:(c + 1) * P], k.ident[0:E0, 0:E0])
            last.then_inc(rw_ps, 1)
            pe.wait_ge(rw_ok, 1)
            norm.t_ps.start(pe)
            lg_ps.start(pe)

            def product(t, u):
                norm.t_ok.done(pe, t)
                lg_ok.slot(pe, t)
                for c in range(DC):
                    last = nc.tensor.matmul(bank[2 + u][:, 0:E0], norm.xT[:, u, c * P:(c + 1) * P], rw[:, c, :], start=(c == 0), stop=(c == DC - 1))
                last.then_inc(lg_ps.sem, 1)
            norm.feed(pe, product)
            route.tensor(pe)
            pe.wait_ge(route_ok, 1)
            pe.wait_ge(loaded, 5 * 16)
            for n in (x_ps, h_ps, ht_ps, y_ps):
                n.start(pe)

            def turn(i, u):
                pe.wait_ge(tile_in[u], (i + 1) * 16)
                for c in range(DC):
                    last = nc.tensor.transpose(bank[2 * u + 1][:, D + c * P:D + (c + 1) * P], xi[:, u, c * P:(c + 1) * P], k.ident[:, :])
                last.then_inc(x_ps.sem, 1)
            for u in range(4):
                turn(0, u)
            with pe.Fori(0, T // 4) as i:
                e = registers(nc, mybir.EngineType.PE, route.expert[0:1, bass.ds(i * 4, 4)], E0 - 1)
                for u in range(4):
                    x_ok.done(pe, i * 4 + u)
                    for c in range(DC):
                        last = nc.tensor.matmul(bank[2 * u][:, 0:F0], xT[:, u, c * P:(c + 1) * P], col(w1[:, c], e[u]),
                                                start=(c == 0), stop=(c == DC - 1))
                    last.then_inc(h_ps.sem, 1)
                for u in range(4):
                    y_add.slot(pe, i * 4 + u)
                    turn(i + 1, u)
                for u in range(4):
                    h_ok.done(pe, i * 4 + u)
                    nc.tensor.transpose(bank[2 * u][:, 3 * P:4 * P], hid[:, u, :], k.ident[:, :]).then_inc(ht_ps.sem, 1)
                for u in range(4):
                    ht_ok.done(pe, i * 4 + u)
                    x_ok.done(pe, i * 4 + 4 + u)
                    nc.tensor.matmul(bank[2 * u + 1][:, 0:D], hT[:, u, :], col(w2, e[u]), start=True, stop=True).then_inc(y_ps.sem, 1)


def attend1(nc, a, k):
    with Stage(nc, "gnn1") as s:
        bank = s.banks()
        norm = Norm(nc, s, k, bank[0:2])
        W = D + 2 * H1
        w, wT = s.sb("w", [P, DC, W]), s.sb("wT", [P, DC, D])
        ablk = s.sb("attn_blocks", [P, DC, 2 * H1])
        g = s.sb("rows_out", [P, 2, W])
        ids = s.sb("rows", [P, 2, 2, 4], I32)
        got, left = s.sb("gathered", [P, 2, 4, W]), s.sb("row_half", [P, 2, 4, H1])
        al, ex = s.sb("alpha", [P, 4, H1]), s.sb("exp", [P, 4, H1])
        mx, sm, prod, red = s.sb("max", [P, 4]), s.sb("sum", [P, 4]), s.sb("products", [P, 4, H1, HD1]), s.sb("reduced", [P, 4, HD1])
        loaded, cleared, wt_ps, wt_ok, v_ps, v_ok = (s.sem(n) for n in ("weights_loaded", "cleared", "wT_in_psum", "wT_ready", "v_in_psum", "v_ready"))
        xt_ps, g_ok, stored = Count(s, "products_in_psum", 2), Count(s, "rows_ready", 2), Landed(s, "rows_stored", 2, 2)
        tables, begun, ids_ok = s.sem("tables_written"), s.sem("gathers_begun"), s.sem("ids_ready")
        arrived = [s.sem(f"arrived{g}") for g in range(2)]
        used, al_ok, ex_ok, x_ok = s.sem("gathered_used"), s.sem("alpha_ready"), s.sem("exp_ready"), s.sem("x_ready")
        GROUPS = NT // 4
        assert NT % 4 == 1 and GROUPS % 2 == 0
        block = s.block()

        @block.gpsimd
        def _(pool):
            nc.gpsimd.memset(ablk[:, :, :], 0.0).then_inc(cleared, 1)
            pool.wait_ge(tables, 1)

            def gather(n, p, m):
                pool.wait_ge(ids_ok, n + 1)
                pool.sem_inc(begun, 1)
                for u in range(m):
                    nc.gpsimd.indirect_dma_start(got[:, p, u, :], None, k.g_tab, bass.IndirectOffsetOnAxis(ids[:, p, 0, u:u + 1], 0)).then_inc(arrived[p], 16)
                    nc.gpsimd.indirect_dma_start(left[:, p, u, :], None, k.l_tab, bass.IndirectOffsetOnAxis(ids[:, p, 1, u:u + 1], 0)).then_inc(arrived[p], 16)
            tiles(pool, GROUPS, 2, lambda n, p: gather(n, p, 4))
            gather(GROUPS, 0, 1)

        @block.sync
        def _(sp):
            sp.dma_start(w[:, :, 0:D], a["L1_gnn_weight"].rearrange("(c p) o -> p c o", p=P)).then_inc(loaded, 16)
            sp.wait_ge(cleared, 1)
            with nc.allow_non_contiguous_dma(reason="short vectors onto partitions"):
                for j, name in enumerate(("L1_gnn_attn_r", "L1_gnn_attn_l")):
                    for h in range(H1):
                        p0 = h * HD1 % P
                        sp.dma_start(ablk[p0:p0 + HD1, h * HD1 // P, j * H1 + h:j * H1 + h + 1],
                                     a[name][h:h + 1, :].rearrange("a b -> b a")).then_inc(loaded, 16)
            stored.start(sp)

            def save(t, u):
                g_ok.done(sp, t)
                sp.dma_start(rows(k.g_tab, t * P, P), g[:, u, :]).then_inc(stored.sems[u], 16)
                sp.dma_start(rows(k.l_tab, t * P, P), g[:, u, D + H1:W]).then_inc(stored.sems[u], 16)
            tiles(sp, NT, 2, save)
            stored.all(sp, NT)
            sp.sem_inc(tables, 1)

        @block.scalar
        def _(act):
            norm.root(act)
            g_ok.start(act)

            def emit(i, u):
                xt_ps.done(act, i * 2 + u)
                stored.slot(act, i, u)
                nc.scalar.activation(g[:, u, :], bank[2 + u][:, 0:W], ACT.Copy).then_inc(g_ok.sem, 1)
            norm.keep(act, 0, 0, xt_ps)
            with act.Fori(0, (NT - 1) // 2) as i:
                for u in range(2):
                    norm.keep(act, i * 2 + u + 1, 1 - u, xt_ps)
                    emit(i, u)
            emit((NT - 1) // 2, 0)

            def exps(n, m):
                act.wait_ge(al_ok, n + 1)
                nc.scalar.activation(ex[:, 0:m, :], al[:, 0:m, :], ACT.Exp).then_inc(ex_ok, 1)
            tiles(act, GROUPS, 2, lambda n, p: exps(n, 4))
            exps(GROUPS, 1)

        @block.vector
        def _(v):
            ch = Chain(v, norm.dve)
            norm.statistics(v, ch)
            v.wait_ge(wt_ps, 1)
            nc.vector.tensor_copy(wT[:, :, :], bank[4][:, :].rearrange("p (c f) -> p c f", c=DC)).then_inc(wt_ok, 1)
            v.wait_ge(v_ps, 1)
            nc.vector.tensor_copy(w[:, :, D:W], bank[5][:, 0:DC * 2 * H1].rearrange("p (c j) -> p c j", c=DC)).then_inc(v_ok, 1)
            tiles(v, NT, 2, lambda t, u: norm.normalise(v, t, u))
            c0 = ch.n

            def address(n, p, m):
                nc.vector.tensor_copy(ids[:, p, 0, 0:m], col(k.dst_i, n * 4, m) if m > 1 else col(k.dst_i, n * 4))
                nc.vector.tensor_copy(ids[:, p, 1, 0:m], col(k.src_i, n * 4, m) if m > 1 else col(k.src_i, n * 4)).then_inc(ids_ok, 1)

            def attend(i, p, m):
                n = i * 2 + p
                v.wait_ge(arrived[p], i * 128 + m * 32)
                a4, g4 = al[:, 0:m, :], got[:, p, 0:m, :]
                b = lambda t, w: t.rearrange("p (u o) -> p u o", o=1).broadcast_to([P, m, w])
                ch.link(nc.vector.tensor_tensor(a4, left[:, p, 0:m, :], g4[:, :, D:D + H1], ALU.add))
                ch.link(nc.vector.scalar_tensor_tensor(a4, a4, 0.01, a4, ALU.mult, ALU.max))
                ch.link(nc.vector.reduce_max(mx[:, 0:m], a4, AX.X))
                nc.vector.tensor_tensor(a4, a4, b(mx[:, 0:m], H1), ALU.subtract).then_inc(al_ok, 1)
                v.wait_ge(ex_ok, n + 1)
                nc.vector.tensor_tensor(prod[:, 0:m], g4[:, :, 0:D].rearrange("p u (h d) -> p u h d", h=H1),
                                        ex[:, 0:m, :].rearrange("p u (h o) -> p u h o", o=1).broadcast_to([P, m, H1, HD1]), ALU.mult).then_inc(used, 1)
                ch.link(nc.vector.reduce_sum(sm[:, 0:m], ex[:, 0:m, :], AX.X))
                ch.link(nc.vector.reciprocal(mx[:, 0:m], sm[:, 0:m]))
                v.wait_ge(used, n + 1)
                ch.link(nc.vector.reduce_sum(red[:, 0:m, :], prod[:, 0:m].rearrange("p u h d -> p u d h"), AX.X))
                ch.link(nc.vector.tensor_tensor(red[:, 0:m, :], red[:, 0:m, :], b(mx[:, 0:m], HD1), ALU.mult))
                x4 = (k.x[:, bass.ds(n * 4, m), :] if not isinstance(n, int) else k.x[:, n * 4:n * 4 + m, :]).rearrange("p u (h d) -> p u h d", h=H1)
                nc.vector.tensor_tensor(x4, x4, red[:, 0:m, :].rearrange("p u (o d) -> p u o d", o=1).broadcast_to([P, m, H1, HD1]), ALU.add).then_inc(x_ok, 1)
            def tile_stats(n, m):
                v.wait_ge(x_ok, n + 1)
                for u in range(m):
                    nc.vector.bn_stats(col(k.stats, n * 4 + u), col(k.x, n * 4 + u))
            LINKS = 7
            for p in range(2):
                address(p, p, 4)
            with v.Fori(0, GROUPS // 2 - 1) as i:
                for p in range(2):
                    ch.n = c0 + (i * 2 + p) * LINKS
                    attend(i, p, 4)
                    address(i * 2 + p + 2, p, 4)
                    tile_stats(i * 2 + p, 4)
            ch.n = c0 + (GROUPS - 2) * LINKS
            attend(GROUPS // 2 - 1, 0, 4)
            address(GROUPS, 0, 1)
            tile_stats(GROUPS - 2, 4)
            attend(GROUPS // 2 - 1, 1, 4)
            tile_stats(GROUPS - 1, 4)
            attend(GROUPS // 2, 0, 1)
            tile_stats(GROUPS, 1)

        @block.tensor
        def _(pe):
            pe.wait_ge(loaded, 16 * (1 + 2 * H1))
            for oc in range(DC):
                for fc in range(DC):
                    last = nc.tensor.transpose(bank[4][:, oc * D + fc * P:oc * D + (fc + 1) * P], w[:, fc, oc * P:(oc + 1) * P], k.ident[:, :])
            last.then_inc(wt_ps, 1)
            pe.wait_ge(wt_ok, 1)
            for fc in range(DC):
                for oc in range(DC):
                    last = nc.tensor.matmul(bank[5][:, fc * 2 * H1:(fc + 1) * 2 * H1], wT[:, oc, fc * P:(fc + 1) * P], ablk[:, oc, :],
                                            start=(oc == 0), stop=(oc == DC - 1))
            last.then_inc(v_ps, 1)
            pe.wait_ge(v_ok, 1)
            norm.t_ps.start(pe)
            xt_ps.start(pe)

            def product(t, u):
                norm.t_ok.done(pe, t)
                g_ok.slot(pe, t)
                for c in range(DC):
                    last = nc.tensor.matmul(bank[2 + u][:, 0:W], norm.xT[:, u, c * P:(c + 1) * P], w[:, c, :], start=(c == 0), stop=(c == DC - 1))
                last.then_inc(xt_ps.sem, 1)
            norm.feed(pe, product)


B1 = 2 * P
SPARE = 2 + route_tiles(E1, 2, B1) % 2
T1 = route_tiles(E1, 2, B1) + route_tiles(E1, 2, B1) % 2
MC = F1 // P
XS, WS, HS = 64.0, 256.0, 64.0


def route1(nc, a, k):
    with Stage(nc, "route1") as s:
        bank = s.banks()
        norm = Norm(nc, s, k, bank[0:2])
        route = k.route1
        route.work_in(s, bank)
        wr, br = s.sb("router", [P, DC, E1]), s.sb("router_bias", [P, E1])
        st2, mean2, rstd2, var2, sd2, tmp2 = s.sb("stats2", [P, NT, 6]), *(s.sb(n, [P, NT]) for n in ("mean2", "rstd2", "var2", "sd2", "tmp2"))
        ids, out = s.sb("rows", [P, 4, 2], I32), s.sb("out", [P, 4, D])
        mid = s.sb("mid", [P, 4, D])
        loaded, lg_ps, lg_ok = s.sem("loaded"), Count(s, "logits_in_psum", 2), Count(s, "logits_ready", 2)
        var2_ok, sd2_ok, diff_ok, share_ok, row_ok, begun = (s.sem(n) for n in ("var2_ready", "sd2_ready", "diff_ready", "share_ready", "row_ready", "scatters_begun"))
        scattered = [s.sem(f"scattered{u}") for u in range(4)]
        mid_ok = s.sem("mid_ready")
        saved = s.sem("x_saved")
        block = s.block()

        @block.gpsimd
        def _(pool):
            route.pool()

            def scatter(i, u):
                t = i * 4 + u
                m = P if not isinstance(t, int) or t < NT - 1 else TAIL
                pool.wait_ge(row_ok, t + 1)
                pool.sem_inc(begun, 1)
                for j in range(2):
                    nc.gpsimd.indirect_dma_start(k.xs1, bass.IndirectOffsetOnAxis(ids[0:m, u, j:j + 1], 0), out[0:m, u, :], None).then_inc(scattered[u], 16)
            rounds(pool, NT, 4, scatter)
            for u in range(4):
                pool.wait_ge(scattered[u], 32 * ((NT - u + 3) // 4))

        @block.sync
        def _(sp):
            sp.dma_start(wr[:, :, :], a["L1_ffn_Wr"].rearrange("(c p) e -> p c e", p=P)).then_inc(loaded, 16)
            sp.dma_start(br[:, :], a["L1_ffn_br"].rearrange("(o e) -> o e", o=1).broadcast_to([P, E1])).then_inc(loaded, 16)
            sp.dma_start(k.x3.rearrange("(t p) f -> p t f", p=P), k.x[:, :, :]).then_inc(saved, 16)
            sp.wait_ge(saved, 16)

        @block.scalar
        def _(act):
            norm.root(act)
            tiles(act, NT, 2, lambda t, u: norm.keep(act, t, u, lg_ps))
            act.wait_ge(var2_ok, 1)
            nc.scalar.activation(sd2[:, :], var2[:, :], ACT.Sqrt).then_inc(sd2_ok, 1)
            act.wait_ge(diff_ok, 1)
            nc.scalar.activation(k.share[1][:, :], k.share[1][:, :], ACT.Exp).then_inc(share_ok, 1)

        @block.vector
        def _(v):
            ch = Chain(v, norm.dve)
            norm.statistics(v, ch)
            v.wait_ge(loaded, 32)
            lg_ok.start(v)

            def logits(i, u):
                lg_ps.done(v, i * 2 + u)
                nc.vector.tensor_tensor(col(route.logits, i * 2 + u), bank[2 + u][:, 0:E1], br[:, :], ALU.add).then_inc(lg_ok.sem, 1)

            def normalise(t, u):
                norm.normalise(v, t, u)
                norm.xn_ok.done(v, t)
                nc.vector.bn_stats(col(st2, t), norm.xn[:, u, :]).then_inc(mid_ok, 1)
            norm.lead(v, normalise, logits)
            lg_ok.done(v, NT - 1)
            v.wait_ge(mid_ok, NT)
            me, ve, mo, vo = (st2[:, :, i] for i in (1, 2, 4, 5))
            tmp, var, mean = tmp2[:, :], var2[:, :], mean2[:, :]
            moments(nc, ch, me, ve, mo, vo, mean, var, tmp)
            v.sem_inc(var2_ok, 1)
            v.wait_ge(sd2_ok, 1)
            rsqrt_newton(nc, ch, rstd2[:, :], tmp, var, sd2[:, :])
            route.vector(v, ch)
            ch.link(nc.vector.tensor_tensor(k.share[1][:, :], route.best[1][:, :], route.best[0][:, :], ALU.subtract))
            v.sem_inc(diff_ok, 1)
            v.wait_ge(share_ok, 1)
            ch.link(nc.vector.tensor_scalar(k.share[0][:, :], k.share[1][:, :], 1.0, None, ALU.add))
            ch.link(nc.vector.reciprocal(k.share[0][:, :], k.share[0][:, :]))
            ch.link(nc.vector.tensor_tensor(k.share[1][:, :], k.share[1][:, :], k.share[0][:, :], ALU.mult))
            c0 = NT

            def send(i, u):
                t = i * 4 + u
                if not isinstance(i, int) or i:
                    v.wait_ge(scattered[u], i * 32)
                nc.vector.tensor_scalar(mid[:, u, :], col(k.x, t), col(norm.mean, t), col(norm.rstd, t), ALU.subtract, ALU.mult).then_inc(mid_ok, 1)
                for j in range(2):
                    nc.vector.tensor_copy(ids[:, u, j:j + 1], col(route.place[j], t))
                v.wait_ge(mid_ok, NT + 1 + t)
                nc.vector.tensor_scalar(out[:, u, :], mid[:, u, :], col(mean2, t), col(rstd2, t), ALU.subtract, ALU.mult).then_inc(row_ok, 1)
            rounds(v, NT, 4, send)

        @block.tensor
        def _(pe):
            pe.wait_ge(loaded, 32)
            norm.t_ps.start(pe)
            lg_ps.start(pe)

            def product(t, u):
                norm.t_ok.done(pe, t)
                lg_ok.slot(pe, t)
                for c in range(DC):
                    last = nc.tensor.matmul(bank[2 + u][:, 0:E1], norm.xT[:, u, c * P:(c + 1) * P], wr[:, c, :], start=(c == 0), stop=(c == DC - 1))
                last.then_inc(lg_ps.sem, 1)
            norm.feed(pe, product)
            route.tensor(pe)


def experts1(nc, a, k):
    with Stage(nc, "moe1") as s:
        bank = s.banks()
        Q = MC // 2
        route, DVE, PE, SC = k.route1, mybir.EngineType.DVE, mybir.EngineType.PE, mybir.EngineType.Activation
        w1 = [s.sb(f"w1_{n}", [P, DC, E1 * F1], F16) for n in ("high", "low")]
        w2 = [s.sb(f"w2_{n}", [P, MC, E1 * D], F16) for n in ("high", "low")]
        stage = s.sb("stage", [P, 3, 2048])
        lg, lb, b1 = s.sb("gain_T", [P, DC, E1]), s.sb("shift_T", [P, DC, E1]), s.sb("b1_T", [P, E1, MC])
        rows8, rowsb = s.sb("gain_rows", [E1, 2, D]), s.sb("b1_rows", [E1 * MC, P])
        b2 = s.sb("b2", [P, E1, D])
        xi, xe = s.sb("tile", [P, 2, 2, D]), s.sb("tile_T", [P, 2, DC, B1])
        xh = [s.sb(f"x_{n}", [P, 2, DC, B1], F16) for n in ("high", "low")]
        hg = s.sb("hidden", [P, Q, 2 * B1])
        hh = [s.sb(f"hidden_{n}", [P, 2, MC, B1], F16) for n in ("high", "low")]
        y = s.sb("y", [P, 2, 2, D])
        small, small_ps, small_ok = s.sem("small_loaded"), s.sem("small_in_psum"), s.sem("small_ready")
        staged = [s.sem(f"staged{u}") for u in range(3)]
        high_ok, low_ok = Count(s, "high_ready", 3), Count(s, "low_ready", 3)
        tile_in, out_ok = [s.sem(f"tile_loaded{u}") for u in range(2)], Landed(s, "y_written", 2)
        x_ps, xe_ok, xs_ok, y_ps, y_ok = (Count(s, n, 2) for n in (
            "x_in_psum", "xe_ready", "x_split", "y_in_psum", "y_ready"))
        h_ps, hg_ok, hs_ok = Count(s, "hidden_in_psum", Q), Count(s, "hidden_ready", Q), Count(s, "hidden_split", Q)
        xhi_ok, hhi_ok = Count(s, "x_high", 2), Count(s, "hidden_high", Q)
        PIECES = 2 * E1

        block = s.block()

        def part(n):
            e = n % E1
            if n < E1:
                return [t[:, :, e * F1:(e + 1) * F1] for t in w1], DC, a["L1_ffn_W1"][e].rearrange("(c p) h -> p c h", p=P)
            return [t[:, :, e * D:(e + 1) * D] for t in w2], MC, a["L1_ffn_W2"][e].rearrange("(c p) h -> p c h", p=P)

        @block.sync
        def _(sp):
            sp.dma_start(rows8[:, 0, :], a["L1_ffn_ln_g"]).then_inc(small, 16)
            sp.dma_start(rows8[:, 1, :], a["L1_ffn_ln_b"]).then_inc(small, 16)
            sp.dma_start(rowsb[:, :], a["L1_ffn_b1"].rearrange("e (m p) -> (e m) p", p=P)).then_inc(small, 16)
            v = a["L1_ffn_b2"].rearrange("e h -> (e h)").rearrange("(o n) -> o n", o=1)
            sp.dma_start(flat(b2[:, :, :]), v.broadcast_to([P, v.shape[1]])).then_inc(small, 16)
            for n in range(PIECES):
                low_ok.slot(sp, n)
                _, m, src = part(n)
                sp.dma_start(stage[:, n % 3, :].rearrange("p (c h) -> p c h", c=m), src).then_inc(staged[n % 3], 16)
            out_ok.start(sp)
            with sp.Fori(0, T1 // 2) as i:
                for u in range(2):
                    y_ok.done(sp, i * 2 + u)
                    sp.dma_start(rows(k.ys1, (i * 2 + u) * B1, B1).rearrange("(h p) f -> p h f", p=P), y[:, u]).then_inc(out_ok.sems[u], 16)
            out_ok.all(sp, T1)

        @block.gpsimd
        def _(pool):
            def load(i, u):
                x_ps.slot(pool, i * 2 + u)
                pool.dma_start(xi[:, u], rows(k.xs1, (i * 2 + u) * B1, B1).rearrange("(h p) f -> p h f", p=P)).then_inc(tile_in[u], 16)
            turns(pool, T1 + 2, 2, load)

        @block.scalar
        def _(act):
            high_ok.start(act)
            for n in range(PIECES):
                to, m, _ = part(n)
                act.wait_ge(staged[n % 3], 16 * (n // 3 + 1))
                nc.scalar.activation(to[0], stage[:, n % 3, :].rearrange("p (c h) -> p c h", c=m), ACT.Copy, scale=WS).then_inc(high_ok.sem, 1)
            act.wait_ge(small_ok, 1)
            xe_ok.start(act)
            hg_ok.start(act)

            def turn(t, u, e):
                x_ps.done(act, t)
                xs_ok.slot(act, t)
                for c in range(DC):
                    last = nc.scalar.activation(xe[:, u, c, :], bank[4 + u][:, c * B1:(c + 1) * B1], ACT.Identity,
                                                scale=col(lg[:, c, :], e), bias=col(lb[:, c, :], e))
                last.then_inc(xe_ok.sem, 1)

            def gelu(t, u, e):
                for q in range(Q):
                    h_ps.done(act, Q * t + q)
                    hs_ok.slot(act, Q * t + q)
                    for m in range(2):
                        last = nc.scalar.activation(hg[:, q, m * B1:(m + 1) * B1], bank[q][:, m * B1:(m + 1) * B1], ACT.Gelu,
                                                    scale=1.0 / (XS * WS), bias=col(b1[:, :, 2 * q + m], e))
                    last.then_inc(hg_ok.sem, 1)
            e = registers(nc, SC, route.expert[0:1, 0:2], E1 - 1)
            turn(0, 0, e[0])
            turn(1, 1, e[1])
            gelu(0, 0, e[0])
            with act.Fori(0, T1 // 2) as i:
                e = registers(nc, SC, route.expert[0:1, bass.ds(i * 2, 4)], E1 - 1)
                for u in range(2):
                    turn(i * 2 + 2 + u, u, e[2 + u])
                    gelu(i * 2 + 1 + u, 1 - u, e[1 + u])

        @block.vector
        def _(v):
            low_ok.start(v)
            v.wait_ge(small, 64)
            v.wait_ge(small_ps, 1)
            for j, t in ((0, lg), (1, lb)):
                nc.vector.tensor_scalar(t[:, :, :], bank[7][:, j * DC * E1:(j + 1) * DC * E1].rearrange("p (c e) -> p c e", c=DC), XS, None, ALU.mult)
            nc.vector.tensor_copy(b1[:, :, :], bank[7][:, 4 * E1:4 * E1 + E1 * MC].rearrange("p (e m) -> p e m", e=E1)).then_inc(small_ok, 1)
            for n in range(PIECES):
                to, m, _ = part(n)
                high_ok.done(v, n)
                nc.vector.scalar_tensor_tensor(to[1], stage[:, n % 3, :].rearrange("p (c h) -> p c h", c=m), WS, to[0], ALU.mult, ALU.subtract).then_inc(low_ok.sem, 1)
            for n in (xs_ok, xhi_ok, hs_ok, hhi_ok, y_ok):
                n.start(v)

            def split_x(t, u):
                xe_ok.done(v, t)
                if not isinstance(t, int) or t > 0:
                    v.wait_ge(h_ps.sem, Q * t)
                nc.vector.tensor_copy(xh[0][:, u], xe[:, u]).then_inc(xhi_ok.sem, 1)
                xhi_ok.done(v, t)
                nc.vector.tensor_tensor(xh[1][:, u], xe[:, u], xh[0][:, u], ALU.subtract).then_inc(xs_ok.sem, 1)

            def split_h(t, u):
                for q in range(Q):
                    hg_ok.done(v, Q * t + q)
                    if q == 0:
                        y_ps.slot(v, t)
                    f, high, low = hg[:, q, :], *(flat(part[:, u, 2 * q:2 * q + 2, :]) for part in hh)
                    nc.vector.tensor_scalar(high, f, HS, None, ALU.mult).then_inc(hhi_ok.sem, 1)
                    hhi_ok.done(v, Q * t + q)
                    nc.vector.scalar_tensor_tensor(low, f, HS, high, ALU.mult, ALU.subtract).then_inc(hs_ok.sem, 1)

            def result(i, u, e):
                y_ps.done(v, i * 2 + u)
                out_ok.slot(v, i, u)
                nc.vector.scalar_tensor_tensor(y[:, u], bank[6 + u][:, :].rearrange("p (h f) -> p h f", h=2), 1.0 / (HS * WS),
                                               col(b2, e).rearrange("p (o f) -> p o f", o=1).broadcast_to([P, 2, D]), ALU.mult, ALU.add).then_inc(y_ok.sem, 1)
            split_x(0, 0)
            split_x(1, 1)
            split_h(0, 0)
            with v.Fori(0, T1 // 2) as i:
                e = registers(nc, DVE, route.expert[0:1, bass.ds(i * 2, 2)], E1 - 1)
                for u in range(2):
                    split_x(i * 2 + 2 + u, u)
                    split_h(i * 2 + 1 + u, 1 - u)
                    result(i, u, e[u])

        @block.tensor
        def _(pe):
            pe.wait_ge(small, 64)
            for j in range(2):
                for c in range(DC):
                    o = (j * DC + c) * E1
                    nc.tensor.transpose(bank[7][:, o:o + E1], rows8[:, j, c * P:(c + 1) * P], k.ident[0:E1, 0:E1])
            nc.tensor.transpose(bank[7][:, 4 * E1:4 * E1 + E1 * MC], rowsb[:, :], k.ident[0:E1 * MC, 0:E1 * MC]).then_inc(small_ps, 1)
            pe.wait_ge(small_ok, 1)
            for n in (x_ps, h_ps, y_ps):
                n.start(pe)
            passes = ((0, 0), (0, 1), (1, 0))

            def turn(i, u):
                pe.wait_ge(tile_in[u], (i + 1) * 16)
                xe_ok.slot(pe, i * 2 + u)
                for c in range(DC):
                    for h in range(2):
                        o = c * B1 + h * P
                        last = nc.tensor.transpose(bank[4 + u][:, o:o + P], xi[:, u, h, c * P:(c + 1) * P], k.ident[:, :])
                last.then_inc(x_ps.sem, 1)

            def up(t, u, e):
                xs_ok.done(pe, t)
                for q in range(Q):
                    hg_ok.slot(pe, Q * t + q)
                    for m in range(2):
                        for n, (pw, px) in enumerate(passes):
                            for c in range(DC):
                                last = nc.tensor.matmul(bank[q][:, m * B1:(m + 1) * B1], w1[pw][:, c, bass.ds(e * F1 + (2 * q + m) * P, P)], xh[px][:, u, c, :],
                                                        start=(n == 0 and c == 0), stop=(n == 2 and c == DC - 1))
                    last.then_inc(h_ps.sem, 1)

            def down(t, u, e):
                y_ok.slot(pe, t)
                hs_ok.done(pe, Q * t + Q - 1)
                for h in range(2):
                    for m in range(MC):
                        for n, (pw, ph) in enumerate(passes):
                            last = nc.tensor.matmul(bank[6 + u][:, h * D:(h + 1) * D], hh[ph][:, u, m, h * P:(h + 1) * P], w2[pw][:, m, bass.ds(e * D, D)],
                                                    start=(m == 0 and n == 0), stop=(m == MC - 1 and n == 2))
                last.then_inc(y_ps.sem, 1)
            low_ok.done(pe, PIECES - 1)
            e = registers(nc, PE, route.expert[0:1, 0:2], E1 - 1)
            turn(0, 0)
            turn(0, 1)
            up(0, 0, e[0])
            with pe.Fori(0, T1 // 2) as i:
                e = registers(nc, PE, route.expert[0:1, bass.ds(i * 2, 3)], E1 - 1)
                for u in range(2):
                    turn(i + 1, u)
                    up(i * 2 + 1 + u, 1 - u, e[1 + u])
                    down(i * 2 + u, u, e[u])


def combine1(nc, a, k):
    with Stage(nc, "last") as s:
        ids = s.sb("rows", [P, 4, 2], I32)
        x, y = s.sb("x", [P, 4, D]), s.sb("y", [P, 4, 2, D])
        sent = [s.sem(f"x_loaded{u}") for u in range(4)]
        arrived = [s.sem(f"arrived{u}") for u in range(4)]
        ids_ok, begun, half, out_ok, free = s.sem("ids_ready"), s.sem("gathers_begun"), s.sem("half"), Count(s, "out_ready", 4), Landed(s, "out_stored", 4)
        block = s.block()

        def size(t):
            return P if not isinstance(t, int) or t < NT - 1 else TAIL

        @block.gpsimd
        def _(pool):
            def gather(t, u):
                pool.wait_ge(ids_ok, t + 1)
                pool.sem_inc(begun, 1)
                m = size(t)
                for j in range(2):
                    nc.gpsimd.indirect_dma_start(y[0:m, u, j, :], None, k.ys1, bass.IndirectOffsetOnAxis(ids[0:m, u, j:j + 1], 0)).then_inc(arrived[u], 16)
            tiles(pool, NT, 4, gather)

        @block.scalar
        def _(act):
            def load(i, u):
                free.slot(act, i, u)
                act.dma_start(x[:, u, :], rows(k.x3, (i * 4 + u) * P, P)).then_inc(sent[u], 16)
            turns(act, NT, 4, load)

        @block.sync
        def _(sp):
            free.start(sp)

            def save(t, u):
                out_ok.done(sp, t)
                m = size(t)
                sp.dma_start(rows(a["out"], t * P, m), x[0:m, u, :]).then_inc(free.sems[u], 16)
            tiles(sp, NT, 4, save)
            free.all(sp, NT)

        @block.vector
        def _(v):
            out_ok.start(v)

            def address(t, u):
                for j in range(2):
                    last = nc.vector.tensor_copy(ids[:, u, j:j + 1], col(k.route1.place[j], t))
                last.then_inc(ids_ok, 1)

            def add(i, u):
                t = i * 4 + u
                m = size(t)
                v.wait_ge(arrived[u], (i + 1) * 32)
                v.wait_ge(sent[u], (i + 1) * 16)
                nc.vector.scalar_tensor_tensor(x[0:m, u, :], y[0:m, u, 0, :], col(k.share[0], t)[0:m], x[0:m, u, :], ALU.mult, ALU.add).then_inc(half, 1)
                v.wait_ge(half, t + 1)
                nc.vector.scalar_tensor_tensor(x[0:m, u, :], y[0:m, u, 1, :], col(k.share[1], t)[0:m], x[0:m, u, :], ALU.mult, ALU.add).then_inc(out_ok.sem, 1)
            for u in range(4):
                address(u, u)
            with v.Fori(0, NT // 4 - 1) as i:
                for u in range(4):
                    add(i, u)
                    address(i * 4 + 4 + u, u)
            for u in range(4):
                add(NT // 4 - 1, u)
            address(NT - 1, 0)
            add(NT // 4, 0)


class Kept:
    pass


def build(nc, a):
    k = Kept()
    k.span_tab = nc.dram_tensor("span_tab", [2, C * NT], F32).ap()
    k.src_tab = nc.dram_tensor("src_tab", [NPAD * R, H0], F32).ap()
    k.item_tab = nc.dram_tensor("item_tab", [3, -(-ITEMS_MAX // P) * P], F32).ap()
    k.h_tab = nc.dram_tensor("h_tab", [NPAD * R, D], F32).ap()
    per0, per1 = -(-(route_tiles(E0, 1) + 4) // NT), -(-(T1 + 2) * B1 // (NT * P))
    k.xs0 = nc.dram_tensor("sorted0", [per0 * NT * P, D], F32).ap()
    k.ys0 = nc.dram_tensor("results0", [route_tiles(E0, 1) * P, D], F32).ap()
    k.xs1 = nc.dram_tensor("sorted1", [per1 * NT * P, D], F32).ap()
    k.ys1 = nc.dram_tensor("results1", [T1 * B1, D], F32).ap()
    k.x3 = nc.dram_tensor("x3", [NPAD, D], F32).ap()
    k.g_tab = nc.dram_tensor("g_tab", [NPAD, D + 2 * H1], F32).ap()
    k.l_tab = nc.dram_tensor("l_tab", [NPAD, H1], F32).ap()
    k.sorted = [(k.xs0, per0), (k.xs1, per1)]
    with Stage(nc, "all") as s:
        k.iota, k.ident, k.before, k.ones = (s.sb(n, [P, P]) for n in ("iota", "ident", "before", "ones"))
        k.col = s.sb("col", [P, 1])
        k.share = [s.sb(f"share{j}", [P, NT]) for j in range(2)]
        k.route1 = Route(nc, s, k, E1, 2, SPARE, B1)
        with Stage(nc, "nodes") as n:
            k.x, k.stats = n.sb("x", [P, NT, D]), n.sb("stats", [P, NT, 6])
            k.dst_i, k.src_i = n.sb("dst_i", [P, NT], I32), n.sb("src_i", [P, NT], I32)
            with Stage(nc, "gnn0") as g:
                k.edge_row = g.sb("edge_row", [P, NT * C], I32)
                k.dst_f = g.sb("dst_f", [P, NT * C])
                k.item_i = g.sb("item_i", [1, 2, ITEMS_MAX], I32)
                k.item_base = g.sb("item_base", [P, ITEMS_MAX])
                k.w = g.sb("edge_w", [P, NPAD])
                with Stage(nc, "scores") as sc:
                    k.score = sc.sb("score", [P, NPAD])
                    k.dst_rows = sc.sb("dst_rows", [P, CE], I32)
                    with Stage(nc, "att") as w:
                        k.wT = w.sb("wT", [P, DC, R * D])
                        k.dst_half, k.type_f = w.sb("dst_half", [P, NT, R * H0]), w.sb("type_f", [P, NT * C])
                        k.relation = w.sb("relation", [P, R * H0])
                        k.moments0 = w.sb("mean", [P, NT]), w.sb("rstd", [P, NT])
                        prepare(nc, a, k)
                        list_items(nc, a, k)
                        edge_scores(nc, a, k)
                    edge_weights(nc, a, k)
                aggregate(nc, a, k)
            moe0(nc, a, k)
            attend1(nc, a, k)
            route1(nc, a, k)
        experts1(nc, a, k)
        combine1(nc, a, k)


_INS = ["x", "src", "dst", "edge_type_8", "L0_gnn_W", "L0_gnn_attn_src", "L0_gnn_attn_dst", "L0_ffn_router_w",
        "L0_ffn_router_b", "L0_ffn_W1", "L0_ffn_b1", "L0_ffn_W2", "L0_ffn_b2", "L1_gnn_weight", "L1_gnn_attn_l",
        "L1_gnn_attn_r", "L1_ffn_Wr", "L1_ffn_br", "L1_ffn_ln_g", "L1_ffn_ln_b", "L1_ffn_W1", "L1_ffn_b1",
        "L1_ffn_W2", "L1_ffn_b2"]


def kernel(**inputs):
    import numpy as _np
    import concourse.bacc as _bacc
    from concourse import mybir as _mybir
    from concourse.bass_utils import run_bass_kernel_spmd as _run

    nc = _bacc.Bacc("TRN2", target_bir_lowering=False, num_devices=1)
    arrays, aps = {}, {}
    for name in _INS:
        array = _np.ascontiguousarray(inputs[name])
        arrays[f"in_{name}_dram"] = array
        aps[name] = nc.dram_tensor(f"in_{name}_dram", array.shape, _mybir.dt.from_np(array.dtype), kind="ExternalInput").ap()
    aps["out"] = nc.dram_tensor("out_0_dram", (N, D), F32, kind="ExternalOutput").ap()
    build(nc, aps)
    r = _run(nc, [arrays], core_ids=[0])
    return r.results[0]["out_0_dram"]
```
